# Optimizing a Trainium2 kernel written in Bass

```python
import numpy as np
import jax
import jax.numpy as jnp

def _softmax(x, axis=-1):
    return jax.nn.softmax(x, axis=axis)

def _gelu(x):
    return jax.nn.gelu(x, approximate=True)

def _silu(x):
    return jax.nn.silu(x)

def _sigmoid(x):
    return jax.nn.sigmoid(x)

def _layernorm(x, axis=-1, eps=1e-05):
    m = jnp.mean(x, axis=axis, keepdims=True)
    v = jnp.var(x, axis=axis, keepdims=True)
    return (x - m) / jnp.sqrt(v + eps)

def _scatter_add(tgt, idx, src, axis=0):
    return tgt.at[idx].add(src)

def _segment_sum(src, seg, n):
    return jax.ops.segment_sum(src, seg, n)
kernel_name = 'mk_flamingo_gated_d1_seqx_r4_d8b72b'

def setup_inputs(seed: int=0):
    np.random.seed(seed)
    _w = jnp.asarray

    def _rec_inputs():
        import jax
        import jax.numpy as jnp
        _rk = jax.random.key(seed)
        x = -0.0005207 + 1.001 * jax.random.normal(jax.random.fold_in(_rk, 1), (8, 512, 256), jnp.float32)
        _lenS = 512 - jax.random.randint(jax.random.fold_in(_rk, 7), (8,), 0, max(1, 512 // 4) + 1, jnp.int32)
        _lenS2 = 1024 - jax.random.randint(jax.random.fold_in(_rk, 8), (8,), 0, max(1, 1024 // 4) + 1, jnp.int32)
        _ctx_1024P = jax.random.normal(jax.random.fold_in(_rk, 11), (8, 16, 256), jnp.float32)
        _ctx_1024c = jax.random.dirichlet(jax.random.fold_in(_rk, 511), 0.3 * jnp.ones((16,), jnp.float32), (8, 1024))
        _ctx_1024t = jnp.einsum('bsk,bkd->bsd', _ctx_1024c, _ctx_1024P)
        _ctx_1024t = _ctx_1024t * jax.lax.rsqrt(jnp.mean(jnp.square(_ctx_1024t)) + 1e-12) * 0.953939
        ctx_1024 = -1.52775e-05 + 0.999936 * (_ctx_1024t + 0.3 * jax.random.normal(jax.random.fold_in(_rk, 611), (8, 1024, 256), jnp.float32))
        _g = jax.random.normal(jax.random.fold_in(_rk, 9001), (2, 1), jnp.float32)
        _g = jnp.sign(_g) * jnp.maximum(jnp.abs(_g), 1.0) + (_g == 0) * 1.0
        g_xattn = _g[0]
        g_ffn = _g[1]
        return (x, ctx_1024, g_xattn, g_ffn)
    x, ctx_1024, g_xattn, g_ffn = _rec_inputs()

    def _L0_xattn_setup():
        import jax, jax.numpy as jnp
        import numpy as np
        DIM = 256
        HEADS = 16
        DHEAD = 64
        INNER = HEADS * DHEAD
        EPS = 1e-05

        def layer_norm(x, g, b):
            mu = jnp.mean(x, axis=-1, keepdims=True)
            var = jnp.mean(jnp.square(x - mu), axis=-1, keepdims=True)
            return (x - mu) * jax.lax.rsqrt(var + EPS) * g + b

        def apply_rope(x, cos, sin):
            d2 = x.shape[-1] // 2
            x1, x2 = (x[..., :d2], x[..., d2:])
            return jnp.concatenate([x1 * cos - x2 * sin, x2 * cos + x1 * sin], axis=-1)
        key = jax.random.key(seed)
        ks = jax.random.split(key, 10)
        B, N, S = (8, 64, 1024)
        latents = jax.random.normal(ks[0], (B, N, DIM), dtype=jnp.float32)
        context = jax.random.normal(ks[1], (B, S, DIM), dtype=jnp.float32)
        cos = jax.random.uniform(ks[2], (S, DHEAD // 2), dtype=jnp.float32)
        sin = jax.random.uniform(ks[3], (S, DHEAD // 2), dtype=jnp.float32)
        init = lambda k, shp, fan_in: jax.random.normal(k, shp, dtype=jnp.float32) / np.sqrt(fan_in)
        return {'latents': latents, 'context': context, 'cos': cos, 'sin': sin, 'ln_lat_g': jnp.ones((DIM,), jnp.float32), 'ln_lat_b': jnp.zeros((DIM,), jnp.float32), 'ln_ctx_g': jnp.ones((DIM,), jnp.float32), 'ln_ctx_b': jnp.zeros((DIM,), jnp.float32), 'Wq': init(ks[4], (DIM, INNER), DIM), 'Wkv': init(ks[5], (DIM, 2 * INNER), DIM), 'Wo': init(ks[6], (INNER, DIM), INNER), 'bo': jnp.zeros((DIM,), jnp.float32)}
    _L0_xattn_all = _L0_xattn_setup()
    _L0_xattn_in = {k: v for k, v in _L0_xattn_all.items() if k in ('cos', 'sin', 'ln_lat_g', 'ln_lat_b', 'ln_ctx_g', 'ln_ctx_b', 'Wq', 'Wkv', 'Wo', 'bo')}
    del _L0_xattn_all

    def _L0_ffn_setup():
        import jax, jax.numpy as jnp
        import numpy as np
        H = 256
        E = 64
        K = 8
        G = 8
        TOPK_GROUP = 4
        I_MOE = 128
        I_SHARED = 512
        SCALE = 2.5

        def relu2(x):
            return jnp.square(jax.nn.relu(x))

        def _route(xf, router_w, correction_bias):
            T = xf.shape[0]
            logits = xf @ router_w.T
            scores = jax.nn.sigmoid(logits)
            sfc = scores + correction_bias[None, :]
            grp = sfc.reshape(T, G, E // G)
            top2, _ = jax.lax.top_k(grp, 2)
            group_scores = top2.sum(-1)
            _, gidx = jax.lax.top_k(group_scores, TOPK_GROUP)
            gmask = jnp.zeros((T, G), sfc.dtype).at[jnp.arange(T)[:, None], gidx].set(1.0)
            emask = jnp.repeat(gmask, E // G, axis=1)
            masked = jnp.where(emask > 0, sfc, 0.0)
            _, tidx = jax.lax.top_k(masked, K)
            tw = jnp.take_along_axis(scores, tidx, axis=1)
            tw = tw / (tw.sum(-1, keepdims=True) + 1e-20)
            return (tidx, tw * SCALE)
        key = jax.random.key(seed)
        ks = jax.random.split(key, 7)
        x = jax.random.normal(ks[0], (2, 256, H), dtype=jnp.float32)
        router_w = jax.random.normal(ks[1], (E, H), dtype=jnp.float32) * 0.02
        correction_bias = jax.random.normal(ks[2], (E,), dtype=jnp.float32) * 0.01
        up_w = jax.random.normal(ks[3], (E, H, I_MOE), dtype=jnp.float32) * 0.02
        down_w = jax.random.normal(ks[4], (E, I_MOE, H), dtype=jnp.float32) * 0.02
        shared_up_w = jax.random.normal(ks[5], (H, I_SHARED), dtype=jnp.float32) * 0.02
        shared_down_w = jax.random.normal(ks[6], (I_SHARED, H), dtype=jnp.float32) * 0.02
        return {'x': x, 'router_w': router_w, 'correction_bias': correction_bias, 'up_w': up_w, 'down_w': down_w, 'shared_up_w': shared_up_w, 'shared_down_w': shared_down_w}
    _L0_ffn_all = _L0_ffn_setup()
    _L0_ffn_in = {k: v for k, v in _L0_ffn_all.items() if k in ('router_w', 'correction_bias', 'up_w', 'down_w', 'shared_up_w', 'shared_down_w')}
    del _L0_ffn_all
    return {'x': x, 'ctx_1024': ctx_1024, 'g_xattn': g_xattn, 'g_ffn': g_ffn, 'L0_xattn_cos': _L0_xattn_in['cos'], 'L0_xattn_sin': _L0_xattn_in['sin'], 'L0_xattn_ln_lat_g': _L0_xattn_in['ln_lat_g'], 'L0_xattn_ln_lat_b': _L0_xattn_in['ln_lat_b'], 'L0_xattn_ln_ctx_g': _L0_xattn_in['ln_ctx_g'], 'L0_xattn_ln_ctx_b': _L0_xattn_in['ln_ctx_b'], 'L0_xattn_Wq': _L0_xattn_in['Wq'], 'L0_xattn_Wkv': _L0_xattn_in['Wkv'], 'L0_xattn_Wo': _L0_xattn_in['Wo'], 'L0_xattn_bo': _L0_xattn_in['bo'], 'L0_ffn_router_w': _L0_ffn_in['router_w'], 'L0_ffn_correction_bias': _L0_ffn_in['correction_bias'], 'L0_ffn_up_w': _L0_ffn_in['up_w'], 'L0_ffn_down_w': _L0_ffn_in['down_w'], 'L0_ffn_shared_up_w': _L0_ffn_in['shared_up_w'], 'L0_ffn_shared_down_w': _L0_ffn_in['shared_down_w']}

def reference(x, ctx_1024, g_xattn, g_ffn, L0_xattn_cos, L0_xattn_sin, L0_xattn_ln_lat_g, L0_xattn_ln_lat_b, L0_xattn_ln_ctx_g, L0_xattn_ln_ctx_b, L0_xattn_Wq, L0_xattn_Wkv, L0_xattn_Wo, L0_xattn_bo, L0_ffn_router_w, L0_ffn_correction_bias, L0_ffn_up_w, L0_ffn_down_w, L0_ffn_shared_up_w, L0_ffn_shared_down_w):
    import jax
    import jax.numpy as jnp

    def _L0_xattn_ref(latents, context, cos, sin, ln_lat_g, ln_lat_b, ln_ctx_g, ln_ctx_b, Wq, Wkv, Wo, bo):
        import jax, jax.numpy as jnp
        import numpy as np
        DIM = 256
        HEADS = 16
        DHEAD = 64
        INNER = HEADS * DHEAD
        EPS = 1e-05

        def layer_norm(x, g, b):
            mu = jnp.mean(x, axis=-1, keepdims=True)
            var = jnp.mean(jnp.square(x - mu), axis=-1, keepdims=True)
            return (x - mu) * jax.lax.rsqrt(var + EPS) * g + b

        def apply_rope(x, cos, sin):
            d2 = x.shape[-1] // 2
            x1, x2 = (x[..., :d2], x[..., d2:])
            return jnp.concatenate([x1 * cos - x2 * sin, x2 * cos + x1 * sin], axis=-1)
        b, n, _ = latents.shape
        s = context.shape[1]
        lat = layer_norm(latents, ln_lat_g, ln_lat_b)
        ctx = layer_norm(context, ln_ctx_g, ln_ctx_b)
        q = (lat @ Wq).reshape(b, n, HEADS, DHEAD).transpose(0, 2, 1, 3)
        kv = ctx @ Wkv
        k, v = jnp.split(kv, 2, axis=-1)
        k = k.reshape(b, s, HEADS, DHEAD).transpose(0, 2, 1, 3)
        v = v.reshape(b, s, HEADS, DHEAD).transpose(0, 2, 1, 3)
        k = apply_rope(k, cos[None, None], sin[None, None])
        scale = DHEAD ** (-0.5)
        attn = jnp.einsum('bhnd,bhsd->bhns', q, k) * scale
        attn = jnp.clip(attn, -11.0, 11.0)
        attn = jax.nn.softmax(attn, axis=-1)
        out = jnp.einsum('bhns,bhsd->bhnd', attn, v)
        out = out.transpose(0, 2, 1, 3).reshape(b, n, INNER)
        return out @ Wo + bo

    def _L0_ffn_ref(x, router_w, correction_bias, up_w, down_w, shared_up_w, shared_down_w):
        import jax, jax.numpy as jnp
        import numpy as np
        H = 256
        E = 64
        K = 8
        G = 8
        TOPK_GROUP = 4
        I_MOE = 128
        I_SHARED = 512
        SCALE = 2.5

        def relu2(x):
            return jnp.square(jax.nn.relu(x))

        def _route(xf, router_w, correction_bias):
            T = xf.shape[0]
            logits = xf @ router_w.T
            scores = jax.nn.sigmoid(logits)
            sfc = scores + correction_bias[None, :]
            grp = sfc.reshape(T, G, E // G)
            top2, _ = jax.lax.top_k(grp, 2)
            group_scores = top2.sum(-1)
            _, gidx = jax.lax.top_k(group_scores, TOPK_GROUP)
            gmask = jnp.zeros((T, G), sfc.dtype).at[jnp.arange(T)[:, None], gidx].set(1.0)
            emask = jnp.repeat(gmask, E // G, axis=1)
            masked = jnp.where(emask > 0, sfc, 0.0)
            _, tidx = jax.lax.top_k(masked, K)
            tw = jnp.take_along_axis(scores, tidx, axis=1)
            tw = tw / (tw.sum(-1, keepdims=True) + 1e-20)
            return (tidx, tw * SCALE)
        B, S, Hd = x.shape
        xf = x.reshape(-1, Hd)
        T = xf.shape[0]
        tidx, tw = _route(xf.astype(jnp.float32), router_w, correction_bias)
        combine = jnp.zeros((T, E), xf.dtype).at[jnp.arange(T)[:, None], tidx].add(tw.astype(xf.dtype))

        def body(acc, ew):
            wu, wd, c = ew
            return (acc + c[:, None] * (relu2(xf @ wu) @ wd), None)
        routed, _ = jax.lax.scan(body, jnp.zeros_like(xf), (up_w, down_w, combine.T))
        shared = relu2(xf @ shared_up_w) @ shared_down_w
        return (routed + shared).reshape(B, S, Hd)
    x = x + jnp.tanh(g_xattn[0]) * _L0_xattn_ref(_layernorm(x, axis=-1), ctx_1024, L0_xattn_cos, L0_xattn_sin, L0_xattn_ln_lat_g, L0_xattn_ln_lat_b, L0_xattn_ln_ctx_g, L0_xattn_ln_ctx_b, L0_xattn_Wq, L0_xattn_Wkv, L0_xattn_Wo, L0_xattn_bo)
    x = x + jnp.tanh(g_ffn[0]) * _L0_ffn_ref(_layernorm(x, axis=-1), L0_ffn_router_w, L0_ffn_correction_bias, L0_ffn_up_w, L0_ffn_down_w, L0_ffn_shared_up_w, L0_ffn_shared_down_w)
    return x

_drawn_inputs = setup_inputs


def setup_inputs(seed=0):
    import zlib

    import numpy as np

    out = dict(_drawn_inputs(seed))
    spreads = {'L0_xattn_ln_lat_g': (1.0, 0.6),
     'L0_xattn_ln_lat_b': (0.0, 0.778),
     'L0_xattn_ln_ctx_g': (1.0, 0.2),
     'L0_xattn_ln_ctx_b': (0.0, 0.1),
     'L0_xattn_bo': (0.0, 0.1)}
    factors = {'L0_xattn_cos': 6.932,
     'L0_xattn_sin': 6.89,
     'L0_ffn_router_w': 2.791,
     'L0_ffn_correction_bias': 7.12,
     'L0_ffn_up_w': 2.858}
    for name, (base, spread) in spreads.items():
        noise = np.random.default_rng([zlib.crc32(name.encode()), seed]).standard_normal(out[name].shape)
        drawn = base * np.exp(spread * noise) if base else spread * noise
        out[name] = jnp.asarray(drawn.astype(out[name].dtype))
    for name, factor in factors.items():
        out[name] = (out[name] * factor).astype(out[name].dtype)
    return out
```

```python
from contextlib import ExitStack

import concourse.bass as bass
from concourse import mybir

ALU = mybir.AluOpType
ACT = mybir.ActivationFunctionType
F32 = mybir.dt.float32
FR = mybir.dt.float32r

P = 128
B, N, S, D = 8, 512, 1024, 256
H, DH = 16, 64
PAIRS = H // 2
NT = N // P
ST = S // P
C2 = D // P
EPS = 1e-5
CH = 2 * N
EXP_LO = 1.670170079024566e-05
EXP_HI = 59874.14171519782
SCALE = DH ** -0.5


def f32(ap):
    return ap.bitcast(F32)


class Persistent:

    def __init__(self, nc, ctx):
        def sb(name, shape, dt=F32):
            return ctx.enter_context(nc.sbuf_tensor(name, shape, dt))

        self.ident = sb("ident", [P, P])
        self.x1 = sb("x1", [P, B * NT, D])
        self.cos = sb("cos", [P, ST, DH // 2])
        self.sin = sb("sin", [P, ST, DH // 2])
        self.gain = sb("gain", [P, 2, C2])
        self.shift = sb("shift", [P, 2, C2])
        self.gates = sb("gates", [P, 2])
        self.minus_half = sb("minus_half", [P, NT])
        self.ones = sb("ones", [P, 1])
        self.eps = sb("eps", [P, 1])


def setup(nc, pers, ins, w_dram, wo_dram):
    with ExitStack() as ctx:
        def sb(name, shape, dt=F32):
            return ctx.enter_context(nc.sbuf_tensor(name, shape, dt))

        def sem(name):
            return ctx.enter_context(nc.semaphore(name))

        raw = sb("w_raw", [P, C2, 3, PAIRS, P])
        split = sb("w_split", [P, 2, 2, C2, 4, P], FR)
        wo_raw = sb("wo_raw", [P, H, D])
        wo_split = sb("wo_split", [P, H, 2, D], FR)
        gates_in = sb("gates_in", [P, 2])
        wq_loaded, wo_loaded, consts_loaded = sem("wq_loaded"), sem("wo_loaded"), sem("consts_loaded")
        hi_done, lo_done, stored = sem("hi_done"), sem("lo_done"), (sem("stored_even"), sem("stored_odd"))
        wo_hi_done, wo_lo_done, wo_stored = sem("wo_hi_done"), sem("wo_lo_done"), sem("wo_stored")
        zeroed, selected = sem("zeroed"), sem("selected")
        block = ctx.enter_context(nc.Block())

        @block.sync
        def _(sp):
            for c in range(C2):
                sp.dma_start(raw[:, c, 0], ins["Wq"][c * P:(c + 1) * P, :].rearrange("p (g m) -> p g m", m=P)
                             ).then_inc(wq_loaded, 16)
                sp.dma_start(raw[:, c, 1:3], ins["Wkv"][c * P:(c + 1) * P, :].rearrange(
                    "p (t g m) -> p t g m", t=2, m=P)).then_inc(wq_loaded, 16)
            for half in range(2):
                sp.dma_start(wo_raw[half * DH:(half + 1) * DH], ins["Wo"].rearrange("(h d) n -> d h n", d=DH)
                             ).then_inc(wo_loaded, 16)
            for b in range(B):
                sp.dma_start(pers.x1[:, b * NT:(b + 1) * NT, :],
                             ins["x"][b].rearrange("(t p) c -> p t c", p=P)).then_inc(consts_loaded, 16)
            for g in range(PAIRS + 1):
                sp.wait_ge(lo_done, g + 1)
                sp.dma_start(w_dram[g], f32(split[:, g % 2]).rearrange("p a c t m -> p (a c t m)")
                             ).then_inc(stored[g % 2], 16)
            sp.wait_ge(wo_hi_done, 1)
            sp.wait_ge(wo_lo_done, 1)
            for j in range(PAIRS):
                for hh in range(2):
                    head = 2 * ((j + 7 - hh) % PAIRS) + hh
                    sp.dma_start(wo_dram[j, :, hh], f32(wo_split[:, head])).then_inc(wo_stored, 16)
            sp.wait_ge(stored[0], 16 * (PAIRS // 2 + 1))
            sp.wait_ge(stored[1], 16 * (PAIRS // 2))
            sp.wait_ge(wo_stored, 16 * H)
            sp.wait_ge(consts_loaded, 16 * B)

        @block.scalar
        def _(act):
            loads = sem("small_loads")
            act.dma_start(pers.cos[:], ins["cos"].rearrange("(t p) d -> p t d", p=P)).then_inc(loads, 16)
            act.dma_start(pers.sin[:], ins["sin"].rearrange("(t p) d -> p t d", p=P)).then_inc(loads, 16)
            for k, who in enumerate(("lat", "ctx")):
                for c in range(C2):
                    act.dma_start(pers.gain[:, k, c:c + 1], ins[f"ln_{who}_g"][c * P:(c + 1) * P].unsqueeze(1)
                                  ).then_inc(loads, 16)
                    act.dma_start(pers.shift[:, k, c:c + 1], ins[f"ln_{who}_b"][c * P:(c + 1) * P].unsqueeze(1)
                                  ).then_inc(loads, 16)
            act.dma_start(gates_in[:, 0:1], ins["g_xattn"].partition_broadcast(P)).then_inc(loads, 16)
            act.dma_start(gates_in[:, 1:2], ins["g_ffn"].partition_broadcast(P)).then_inc(loads, 16)
            act.wait_ge(loads, 16 * 12)
            act.activation(pers.gates[:], gates_in[:], ACT.Tanh).then_inc(hi_done, 1)
            act.wait_ge(wo_loaded, 32)
            act.activation(wo_split[:, :, 0], wo_raw[:], ACT.Copy).then_inc(wo_hi_done, 1)

        @block.gpsimd
        def _(pool):
            pool.memset(pers.ident[:], 0.0).then_inc(zeroed, 1)
            pool.memset(pers.minus_half[:], -0.5)
            pool.memset(pers.eps[:], EPS)
            pool.memset(pers.ones[:], 1.0).then_inc(zeroed, 1)
            pool.wait_ge(zeroed, 2)
            pool.affine_select(out=pers.ident[:], in_=pers.ident[:], compare_op=ALU.not_equal, fill=1.0,
                               base=0, pattern=[[-1, P]], channel_multiplier=1).then_inc(selected, 1)
            pool.wait_ge(selected, 1)

        @block.vector
        def _(dve):
            hi = sem("w_hi")
            dve.wait_ge(wq_loaded, 16 * 4)
            for g in range(PAIRS + 1):
                pair = g % PAIRS
                if g >= 2:
                    dve.wait_ge(stored[g % 2], 16 * (g // 2))
                def parts(part, c):
                    queries = raw[:, c, 0, pair].rearrange("p (h d) -> p h d", h=2).unsqueeze(2)
                    return ((split[:, g % 2, part, c, 0:2], raw[:, c, 1:3, pair]),
                            (split[:, g % 2, part, c, 2:4].rearrange("p h (r d) -> p h r d", r=2),
                             queries.broadcast_to([P, 2, 2, DH])))

                for c in range(C2):
                    for dst, src in parts(0, c):
                        dve.tensor_copy(dst, src).then_inc(hi, 1)
                dve.wait_ge(hi, 2 * C2 * (g + 1))
                for c in range(C2):
                    for (dst, src), (high, _) in zip(parts(1, c), parts(0, c)):
                        last = dve.tensor_tensor(dst, src, f32(high), ALU.subtract)
                last.then_inc(lo_done, 1)
            dve.wait_ge(wo_hi_done, 1)
            dve.tensor_tensor(wo_split[:, :, 1], wo_raw[:], f32(wo_split[:, :, 0]), ALU.subtract
                              ).then_inc(wo_lo_done, 1)


def attention(nc, pers, ins, w_dram, wo_dram):
    with ExitStack() as ctx:
        def sb(name, shape, dt=F32):
            return ctx.enter_context(nc.sbuf_tensor(name, shape, dt))

        def sem(name):
            return ctx.enter_context(nc.semaphore(name))

        x_nat = sb("x_nat", [P, NT, D])
        stats = sb("stats", [P, NT, 6])
        moments = sb("moments", [P, NT, 2])
        power = sb("power", [P, 3, NT])
        affine = sb("affine", [P, C2, N])
        ctx_t = sb("ctx_t", [P, 2, C2, S], FR)
        lat_t = sb("lat_t", [P, 2, C2, N], FR)
        w = sb("w", [P, 2, 2, C2, 4, P], FR)
        wo = sb("wo", [P, 2, 2, D], FR)
        k_t = sb("k_t", [P, 2, 2, S], FR)
        v = sb("v", [P, 2, ST, 2, P], FR)
        q_t = sb("q_t", [P, 2, 2, 2, N], FR)
        rope_c = sb("rope_c", [P, 2, 2, DH])
        rope_s = sb("rope_s", [P, 2, 2, DH])
        k_rot = sb("k_rot", [P, 2, 2, DH])
        k_nat = sb("k_nat", [P, 2, 2, P], FR)
        e = sb("e", [P, 4, CH])
        e_hi = sb("e_hi", [P, 4, CH], FR)
        e_lo = sb("e_lo", [P, 4, CH], FR)
        e_sum = sb("e_sum", [P, CH])
        e_fold = sb("e_fold", [P, 2, N])
        o_hi = sb("o_hi", [P, 2, N], FR)
        o_lo = sb("o_lo", [P, 2, N], FR)
        settle = sb("settle_a", [P, 1])
        r_den = sb("r_den", [P, 2, NT])
        scores = ctx.enter_context(nc.psum_tensor("scores", [P, 2, CH], F32))
        ps_o = ctx.enter_context(nc.psum_tensor("ps_o", [P, N], F32))
        ps_kv = ctx.enter_context(nc.psum_tensor("ps_kv", [P, N], F32))
        ps_kt = ctx.enter_context(nc.psum_tensor("ps_kt", [P, N], F32))
        ps_y = ctx.enter_context(nc.psum_tensor("ps_y", [P, 2, D], F32))
        DEN = 256

        init = sem("init")
        x_loaded = sem("x_loaded")
        stats_done, rstd_step, rstd_done = sem("stats_done"), sem("rstd_step"), sem("rstd_done")
        normed, turned = sem("normed"), sem("turned")
        t_aff, t_hi, t_lo = sem("t_aff"), sem("t_hi"), sem("t_lo")
        w_loaded, wo_loaded = (sem("w_loaded_even"), sem("w_loaded_odd")), sem("wo_loaded")
        s_scores, s_exp, s_clip, s_ehi, s_elo, s_sum = (sem("s_scores"), sem("s_exp"), sem("s_clip"),
                                                         sem("s_ehi"), sem("s_elo"), sem("s_sum"))
        s_pv, s_ohi, s_olo = sem("s_pv"), sem("s_ohi"), sem("s_olo")
        s_kv, s_m0, s_vhi, s_vlo = sem("s_kv"), sem("s_m0"), sem("s_vhi"), sem("s_vlo")
        s_rope, s_rot, s_khi, s_klo, s_kt, s_kte = (sem("s_rope"), sem("s_rot"), sem("s_khi"), sem("s_klo"),
                                                    sem("s_kt"), sem("s_kte"))
        s_q, s_qhi, s_den, s_y, s_m2 = sem("s_q"), sem("s_qhi"), sem("s_den"), sem("s_y"), sem("s_m2")
        bn_done, s_rden, s_gate = sem("bn_done"), sem("s_rden"), sem("s_gate")

        DEN_HEAD = {2: 1, 6: 0}
        QUERIES = {0: 0, 2: 1}
        OUT = {4: (1, 0), 5: (1, 1)}
        SUM_FREE = [1, 1, 2, 3]

        def loop(eng, tail):
            step, before, per_iteration = tail
            with eng.Fori(0, B) as b:
                if before:
                    before(b)
                with eng.Fori(0, PAIRS // 2) as i:
                    for jj in range(2):
                        g = b * PAIRS + i * 2 + jj
                        j = i * 2 + jj
                        if per_iteration:
                            per_iteration(g, j, jj)
                        for c in range(8):
                            step(g, jj, c, True, True)
            g = B * PAIRS
            if per_iteration:
                per_iteration(g, 0, 0)
            for c in range(8):
                step(g, 0, c, False, True)
            for c in range(6):
                step(g + 1, 1, c, False, False)

        block = ctx.enter_context(nc.Block())

        @block.sync
        def _(sp):
            sp.dma_start(f32(w[:, 0]).rearrange("p a c t m -> p (a c t m)"), w_dram[0]).then_inc(w_loaded[0], 16)

            def before(b):
                for half in range(2):
                    sp.wait_ge(turned, 1 + b * 6 + 2 + 2 * half)
                    sp.dma_start(x_nat[:], ins["ctx"][bass.ds(b, 1), half * N:(half + 1) * N, :].rearrange(
                        "a (t p) c -> p (a t) c", p=P)).then_inc(x_loaded, 16)

            def per_iteration(g, j, jj):
                if not (isinstance(g, int)):
                    sp.wait_ge(s_kv, 1 + g * 8)
                    sp.dma_start(f32(w[:, 1 - jj]).rearrange("p a c t m -> p (a c t m)"),
                                 w_dram[bass.ds(j + 1, 1)].rearrange("a p n -> (a p) n")).then_inc(w_loaded[1 - jj], 16)
                sp.wait_ge(s_m2, 1 + g * 6 + 4)
                sp.dma_start(f32(wo[:]), wo_dram[bass.ds(j, 1)].rearrange("a p h k n -> (a p) h k n")).then_inc(wo_loaded, 16)

            loop(sp, (lambda *a: None, before, per_iteration))
            g = B * PAIRS + 1
            sp.wait_ge(s_m2, 1 + 6 * B * PAIRS + 8)
            sp.dma_start(f32(wo[:]), wo_dram[1]).then_inc(wo_loaded, 16)
            sp.wait_ge(w_loaded[0], 16 * (B * PAIRS // 2 + 1))
            sp.wait_ge(w_loaded[1], 16 * (B * PAIRS // 2))
            sp.wait_ge(wo_loaded, 16 * (B * PAIRS + 2))

        @block.tensor
        def _(pe):
            pe.wait_ge(init, 1)
            pe.matmul(ps_kv[:], v[:, 1, 0, 0, :], q_t[:, 1, 0, 0, :], start=True, stop=True)
            pe.matmul(ps_o[:], v[:, 1, 0, 0, :], q_t[:, 1, 0, 0, :], start=True, stop=False)

            def before(b):
                for u in range(3):
                    pe.wait_ge(normed, b * 3 + u + 1)
                    if u:
                        pe.wait_ge(t_aff, b * 6 + 2 * u)
                    else:
                        pe.wait_ge(s_m2, 1 + b * (6 * PAIRS) + 4)
                        pe.wait_ge(s_kte, 1 + b * (8 * PAIRS))
                    for c in range(C2):
                        bank = (ps_kt[:], ps_y[:].rearrange("p a n -> p (a n)"))[c]
                        for t in range(NT):
                            mm = pe.transpose(bank[:, t * P:(t + 1) * P], x_nat[:, t, c * P:(c + 1) * P],
                                              pers.ident[:])
                        mm.then_inc(turned, 1)

            def step(g, jj, c, project, attend):
                att = 1 - jj
                q4 = c % 4
                if c == 0 and project:
                    pe.wait_ge(t_lo, 1 + g // PAIRS * 6 + 6)
                    pe.wait_ge(w_loaded[jj], (g - jj) // 2 * 16 + 16)
                if attend:
                    pe.wait_ge(s_exp, 1 + g * 8 + c)
                    if c == 0:
                        pe.wait_ge(s_m2, 1 + g * 6)
                        pe.wait_ge(s_kte, 1 + g * 8)
                    if c == 3:
                        pe.wait_ge(s_kte, 1 + g * 8 + 2)
                    for r in range(2):
                        s = 2 * q4 + r
                        for part in range(2):
                            mm = pe.matmul(scores[:, c % 2, r * N:(r + 1) * N],
                                           k_t[:, att, c // 4, s * P:(s + 1) * P],
                                           q_t[:, att, c // 4, part, :], start=(part == 0), stop=(part == 1))
                    mm.then_inc(s_scores, 1)
                if project:
                    pe.wait_ge(s_m0, 1 + g * 8 + c + 1)
                    k = 0
                    for cc in range(C2):
                        for a, bb in ((0, 0), (0, 1), (1, 0)):
                            mm = pe.matmul(ps_kv[:, 0:2 * P], ctx_t[:, a, cc, c * P:(c + 1) * P],
                                           w[:, jj, bb, cc, 0:2].rearrange("p t m -> p (t m)"),
                                           start=(k == 0), stop=(k == 5))
                            k += 1
                    mm.then_inc(s_kv, 1)
                turn = project or (attend and c < 2)
                if turn:
                    pe.wait_ge(s_kte, 1 + g * 8 + c)
                    if (c + 7) % 8 in DEN_HEAD:
                        pe.wait_ge(s_rden, g * 2 + (1 if c == 3 else 2))
                elif c in DEN_HEAD and (attend or c == 2):
                    pe.wait_ge(s_kte, 1 + B * PAIRS * 8 + 2)
                    pe.wait_ge(s_rden, g * 2 + (0 if c == 2 else 1))
                if c in DEN_HEAD and (attend or c == 2):
                    hh = DEN_HEAD[c]
                    pe.wait_ge(s_sum, g * 8 + (4 if c == 2 else 8))
                    for t in range(NT):
                        mm = pe.matmul(ps_kt[:, DEN + t:DEN + t + 1], e_fold[:, hh, t * P:(t + 1) * P],
                                       pers.ones[:], start=True, stop=True)
                    mm.then_inc(s_den, 1)
                if turn:
                    pe.wait_ge(s_klo, 1 + g * 8 + c)
                    for hh in range(2):
                        mm = pe.transpose(ps_kt[:, hh * P:(hh + 1) * P], f32(k_nat[:, c % 2, hh]), pers.ident[:])
                    mm.then_inc(s_kt, 1)
                if project and c in QUERIES:
                    head = QUERIES[c]
                    pe.wait_ge(s_m2, 1 + g * 6 + 4 + head)
                    k = 0
                    for cc in range(C2):
                        for a, bb in ((0, 0), (0, 1), (1, 0)):
                            mm = pe.matmul(ps_y[:].rearrange("p a n -> p (a n)"), w[:, jj, bb, cc, 2 + head],
                                           lat_t[:, a, cc, :], start=(k == 0), stop=(k == 5))
                            k += 1
                    mm.then_inc(s_q, 1)

                def project_out(hh, half, use):
                    pe.wait_ge(s_m2, 1 + use + 4)
                    pe.wait_ge(s_olo, g * 2 + (1 if hh else 2))
                    pe.wait_ge(wo_loaded, g * 16 + 16)
                    for i in range(2):
                        t = 2 * half + i
                        for k, (o_part, wpart) in enumerate(((o_hi, 0), (o_hi, 1), (o_lo, 0))):
                            mm = pe.matmul(ps_y[:, i, :], o_part[:, hh, t * P:(t + 1) * P], wo[:, hh, wpart, :],
                                           start=(k == 0), stop=(k == 2))
                    mm.then_inc(s_y, 1)

                base = g * 6 if project else B * PAIRS * 6 - 2 + (0 if attend else 4)
                if c in OUT:
                    project_out(*OUT[c], base + 2 + OUT[c][1])
                if c == 7:
                    project_out(0, 0, base + 4)
                if attend or c < 2:
                    x4 = (c + 2) % 4
                    hh = ((c + 6) % 8) // 4
                    buf = att if c >= 2 else 1 - att
                    pe.wait_ge(s_elo, 1 + g * 8 + c)
                    if c in (2, 6):
                        pe.wait_ge(s_olo, g * 2 + (1 if c == 2 else 2))
                    for r in range(2):
                        s = 2 * x4 + r
                        for part, e_part in enumerate((e_hi, e_lo)):
                            mm = pe.matmul(ps_o[:], v[:, buf, s, hh, :], e_part[:, x4, r * N:(r + 1) * N],
                                           start=(x4 == 0 and r == 0 and part == 0),
                                           stop=(x4 == 3 and r == 1 and part == 1))
                    mm.then_inc(s_pv, 1)
                if c == 7:
                    project_out(0, 1, base + 5)

            loop(pe, (step, before, None))

        @block.scalar
        def _(act):
            act.wait_ge(init, 1)

            def before(b):
                for u in range(3):
                    dst = (lat_t[:, 0], ctx_t[:, 0, :, 0:N], ctx_t[:, 0, :, N:S])[u]
                    for c in range(C2):
                        act.wait_ge(t_aff, b * 6 + 2 * u + c + 1)
                        act.activation(dst[:, c], affine[:, c], ACT.Copy).then_inc(t_hi, 1)

            def step(g, jj, c, project, attend):
                if attend or c == 0:
                    act.wait_ge(s_clip, 1 + g * 8 + c)
                    act.wait_ge(s_pv, 1 + g * 8 + c)
                    act.activation(e_hi[:, (c + 3) % 4], e[:, (c + 3) % 4], ACT.Copy).then_inc(s_ehi, 1)
                if c in DEN_HEAD and (attend or c == 2):
                    hh = DEN_HEAD[c]
                    act.wait_ge(s_pv, 1 + g * 8 + c + 2)
                    act.activation(o_hi[:, hh], ps_o[:], ACT.Copy).then_inc(s_ohi, 1)
                if project and c - 1 in QUERIES:
                    head = QUERIES[c - 1]
                    act.wait_ge(s_q, g * 2 + head + 1)
                    act.activation(q_t[:, jj, head, 0], ps_y[:].rearrange("p a n -> p (a n)"), ACT.Copy
                                   ).then_inc(s_qhi, 1)
                if attend:
                    act.wait_ge(s_scores, g * 8 + c + 1)
                    act.wait_ge(s_sum, g * 8 + 4 * (c // 4) + SUM_FREE[c % 4])
                    act.activation(e[:, c % 4], scores[:, c % 2], ACT.Exp, scale=SCALE).then_inc(s_exp, 1)
                if project:
                    act.wait_ge(s_kv, 1 + g * 8 + c + 1)
                    act.activation(v[:, jj, c, :, 0:DH], ps_kv[:, P:2 * P].rearrange("p (h d) -> p h d", h=2),
                                   ACT.Copy).then_inc(s_vhi, 1)
                if project or (attend and c < 2):
                    buf = jj if c >= 2 else 1 - jj
                    s = (c + 6) % 8
                    act.wait_ge(s_kt, g * 8 + c + 1)
                    act.activation(k_t[:, buf, :, s * P:(s + 1) * P],
                                   ps_kt[:, 0:2 * P].rearrange("p (h n) -> p h n", h=2), ACT.Copy).then_inc(s_kte, 1)
                if project or (attend and c == 0):
                    act.wait_ge(s_rot, g * 8 + c + 1)
                    act.activation(k_nat[:, (c + 1) % 2, :, 0:DH], k_rot[:, (c + 1) % 2], ACT.Copy
                                   ).then_inc(s_khi, 1)

            loop(act, (step, before, None))

        @block.gpsimd
        def _(pool):
            for k, t in enumerate((v[:, 0], v[:, 1], k_t[:, 1], q_t[:, 1], k_nat[:, 0], k_nat[:, 1], e_hi[:, 2:4], e_lo[:, 2:4])):
                n = len(t.shape) - 1
                names = "abcd"[:n]
                flat = f32(t).rearrange(f"p {' '.join(names)} -> p ({' '.join(names)})") if n > 1 else f32(t)
                pool.memset(flat, 0.0)
            pool.memset(e[:], 1.0)
            pool.memset(e_fold[:], 1.0)
            pool.memset(e_sum[:], 0.0).then_inc(init, 1)
            pool.wait_ge(init, 1)
            pool.sem_inc(s_pv, 2 + 1)
            pool.sem_inc(s_sum, 2)
            pool.sem_inc(s_exp, 1 + 1)
            pool.sem_inc(s_m2, 4 + 1)
            for counted in (s_clip, s_elo, t_lo, turned, s_klo, s_kte, s_m0, s_kv, s_vhi):
                pool.sem_inc(counted, 1)

            def before(b):
                k = 0

                def do(out, in0, in1, op):
                    nonlocal k
                    pool.tensor_tensor(out, in0, in1, op).then_inc(rstd_step, 1)
                    k += 1
                    pool.wait_ge(rstd_step, b * 8 + k)

                var = moments[:, :, 1]
                a, r, rr = power[:, 0], power[:, 1], power[:, 2]
                eps = pers.eps[:].broadcast_to([P, NT])
                for u in range(3):
                    pool.wait_ge(stats_done, b * 3 + u + 1)
                    do(a, var, eps, ALU.add)
                    if u:
                        pool.tensor_tensor(rr, a, pers.minus_half[:], ALU.pow).then_inc(rstd_done, 1)
                    else:
                        do(rr, a, pers.minus_half[:], ALU.pow)
                        do(r, rr, rr, ALU.mult)
                        do(r, r, var, ALU.mult)
                        do(r, r, eps, ALU.add)
                        do(r, r, pers.minus_half[:], ALU.pow)
                        pool.tensor_tensor(rr, r, rr, ALU.mult).then_inc(rstd_done, 1)

            def step(g, jj, c, project, attend):
                if project or (attend and c == 0):
                    buf = (c + 1) % 2
                    pool.wait_ge(s_rope, g * 8 + c + 1)
                    pool.tensor_tensor(k_rot[:, buf, :, 0:DH // 2], rope_c[:, buf, :, 0:DH // 2],
                                       rope_s[:, buf, :, DH // 2:DH], ALU.subtract)
                    pool.tensor_tensor(k_rot[:, buf, :, DH // 2:DH], rope_c[:, buf, :, DH // 2:DH],
                                       rope_s[:, buf, :, 0:DH // 2], ALU.add).then_inc(s_rot, 1)
                q = (c + 3) % 4
                if q and (attend or c == 0):
                    head = g * 8 + (0 if c == 0 else 4 if c < 5 else 8)
                    pool.wait_ge(s_clip, 1 + g * 8 + c)
                    pool.wait_ge(s_sum, head + q - 1)
                    pool.tensor_tensor(e_sum[:], e[:, 0] if q == 1 else e_sum[:], e[:, q], ALU.add).then_inc(s_sum, 1)
                    if q == 3:
                        pool.wait_ge(s_sum, head + 3)
                        pool.tensor_tensor(e_fold[:, 0 if c == 4 else 1], e_sum[:, 0:N], e_sum[:, N:2 * N], ALU.add
                                           ).then_inc(s_sum, 1)

            loop(pool, (step, before, None))

        @block.vector
        def _(dve):
            dve.wait_ge(init, 1)
            half_cols = DH // 2

            def before(b):
                for u in range(3):
                    if u == 0:
                        src = pers.x1[:, bass.ds(b * NT, NT), :]
                        dve.wait_ge(turned, 1 + b * 6)
                    else:
                        src = x_nat[:]
                        dve.wait_ge(x_loaded, b * 32 + 16 * u)
                    for t in range(NT):
                        dve.bn_stats(stats[:, t], src[:, t]).then_inc(bn_done, 1)
                    dve.wait_ge(bn_done, b * 12 + 4 * u + 4)
                    dve.memset(settle[:], 0.0)
                    for t in range(NT):
                        st = dve.bn_aggr(moments[:, t], stats[:, t])
                    st.then_inc(stats_done, 1)
                    dve.wait_ge(stats_done, b * 3 + u + 1)
                    dve.wait_ge(rstd_done, b * 3 + u + 1)
                    for t in range(NT):
                        st = dve.tensor_scalar(x_nat[:, t], src[:, t], moments[:, t, 0:1], power[:, 2, t:t + 1],
                                               ALU.subtract, ALU.mult)
                    st.then_inc(normed, 1)
                    dst = (lat_t, ctx_t[:, :, :, 0:N], ctx_t[:, :, :, N:S])[u]
                    k = 0 if u == 0 else 1
                    for c in range(C2):
                        bank = (ps_kt[:], ps_y[:].rearrange("p a n -> p (a n)"))[c]
                        dve.wait_ge(turned, 1 + b * 6 + 2 * u + c + 1)
                        dve.wait_ge(t_lo, 1 + b * 6 + 2 * u)
                        dve.tensor_scalar(affine[:, c], bank, pers.gain[:, k, c:c + 1], pers.shift[:, k, c:c + 1],
                                          ALU.mult, ALU.add).then_inc(t_aff, 1)
                    for c in range(C2):
                        dve.wait_ge(t_hi, b * 6 + 2 * u + c + 1)
                        dve.tensor_tensor(dst[:, 1, c], affine[:, c], f32(dst[:, 0, c]), ALU.subtract).then_inc(t_lo, 1)

            def step(g, jj, c, project, attend):
                if project or (attend and c == 0):
                    buf = (c + 1) % 2
                    tile = (c + 7) % 8
                    vbuf = jj if c else 1 - jj
                    dve.wait_ge(s_vhi, 1 + g * 8 + c)
                    keys = ps_kv[:, 0:P].rearrange("p (a d) -> p a d", d=half_cols)
                    for table, dst in ((pers.cos, rope_c), (pers.sin, rope_s)):
                        last = dve.tensor_tensor(dst[:, buf].rearrange("p h (k d) -> p (h k) d", k=2), keys,
                                                 table[:, tile].unsqueeze(1).broadcast_to([P, 4, half_cols]), ALU.mult)
                    last.then_inc(s_rope, 1)
                    dve.tensor_tensor(v[:, vbuf, tile, :, DH:P], ps_kv[:, P:2 * P].rearrange("p (h d) -> p h d", h=2),
                                      f32(v[:, vbuf, tile, :, 0:DH]), ALU.subtract).then_inc(s_m0, 1)
                if c in DEN_HEAD and (attend or c == 2):
                    hh = DEN_HEAD[c]
                    dve.wait_ge(s_ohi, g * 2 + (1 if c == 2 else 2))
                    dve.tensor_tensor(o_lo[:, hh], ps_o[:], f32(o_hi[:, hh]), ALU.subtract).then_inc(s_olo, 1)
                if project and c - 1 in QUERIES:
                    head = QUERIES[c - 1]
                    dve.wait_ge(s_qhi, g * 2 + head + 1)
                    dve.tensor_tensor(q_t[:, jj, head, 1], ps_y[:].rearrange("p a n -> p (a n)"),
                                      f32(q_t[:, jj, head, 0]), ALU.subtract).then_inc(s_m2, 1)
                if attend or c == 0:
                    x4 = (c + 3) % 4
                    dve.wait_ge(s_ehi, g * 8 + c + 1)
                    dve.tensor_tensor(e_lo[:, x4], e[:, x4], f32(e_hi[:, x4]), ALU.subtract).then_inc(s_elo, 1)
                if attend:
                    dve.wait_ge(s_exp, 1 + g * 8 + c + 2)
                    dve.tensor_scalar(e[:, c % 4], e[:, c % 4], EXP_HI, EXP_LO, ALU.min, ALU.max).then_inc(s_clip, 1)
                if project or (attend and c == 0):
                    buf = (c + 1) % 2
                    dve.wait_ge(s_khi, g * 8 + c + 1)
                    dve.tensor_tensor(k_nat[:, buf, :, DH:P], k_rot[:, buf], f32(k_nat[:, buf, :, 0:DH]),
                                      ALU.subtract).then_inc(s_klo, 1)
                if c in DEN_HEAD and (attend or c == 2):
                    hh = DEN_HEAD[c]
                    n = g * 2 + (1 if c == 2 else 2)
                    dve.wait_ge(s_den, n)
                    if project:
                        dve.wait_ge(s_kte, 1 + g * 8 + c + 1)
                    dve.reciprocal(r_den[:, hh], ps_kt[:, DEN:DEN + NT]).then_inc(s_rden, 1)
                    dve.wait_ge(s_rden, n)
                    dve.tensor_scalar(r_gate[:, hh], r_den[:, hh], pers.gates[:, 0:1], None, ALU.mult
                                      ).then_inc(s_gate, 1)

                def add_out(hh, half, n_y):
                    dve.wait_ge(s_y, n_y)
                    for i in range(2):
                        t = 2 * half + i
                        row = x1_row(g, hh, t)
                        last = dve.scalar_tensor_tensor(out=row, in0=ps_y[:, i, :], scalar=r_gate[:, hh, t:t + 1],
                                                        in1=row, op0=ALU.mult, op1=ALU.add)
                    last.then_inc(s_m2, 1)

                if c in OUT:
                    if c == 4:
                        dve.wait_ge(s_gate, g * 2 + 1)
                    add_out(*OUT[c], g * 4 + 1 + OUT[c][1])
                if c == 7:
                    dve.wait_ge(s_gate, g * 2 + 2)
                    add_out(0, 0, g * 4 + 3)
                    add_out(0, 1, g * 4 + 4)

            def x1_row(g, hh, t):
                batch = ((g + (7 if hh == 0 else 6)) // PAIRS + B - 1) % B
                if isinstance(batch, int):
                    return pers.x1[:, batch * NT + t, :]
                return pers.x1[:, bass.ds(batch * NT + t, 1), :].rearrange("p a n -> p (a n)")

            r_gate = sb("r_gate", [P, 2, NT])
            loop(dve, (step, before, None))


E_R, E_S = 64, 4
GROUPS_R, PER_G, TOP_G, TOP_K = 8, 8, 4, 8
TG = 2 * N
GT = TG // P
NE = E_R + E_S
ROUTE_SCALE = 2.5
TAKEN = -3.0e38


def ffn(nc, pers, ins, out):
    groups = B * N // TG
    with ExitStack() as ctx:
        def sb(name, shape, dt=F32):
            return ctx.enter_context(nc.sbuf_tensor(name, shape, dt))

        def sem(name):
            return ctx.enter_context(nc.semaphore(name))

        bo = sb("bo", [P, D])
        bias = sb("bias", [P, E_R])
        router = sb("router", [E_R, D])
        router_t = sb("router_t", [P, C2, E_R])
        earlier = sb("earlier", [P, GROUPS_R, GROUPS_R])
        pick = sb("pick", [P, E_R])
        stats = sb("f_stats", [P, GT, 6])
        moments = sb("f_moments", [P, GT, 2])
        rstd = sb("rstd", [P, 2, GT])
        x_nat = sb("f_x_nat", [P, GT, D])
        x_f = sb("x_f", [P, C2, TG])
        x_t = sb("x_t", [P, 2, C2, TG], FR)
        prob = sb("prob", [P, GT, E_R])
        biased = sb("biased", [P, GT, E_R])
        best = sb("best", [P, GT, GROUPS_R, 8])
        g_score = sb("g_score", [P, GT, GROUPS_R])
        cmp_a = sb("cmp_a", [P, GT, GROUPS_R, GROUPS_R])
        cmp_b = sb("cmp_b", [P, GT, GROUPS_R, GROUPS_R])
        g_rank = sb("g_rank", [P, GT, GROUPS_R])
        top8 = sb("top8", [P, GT, 8])
        total = sb("total", [P, GT])
        gate = sb("gate", [P, GT, E_R])
        gate_parts = sb("gate_parts", [P, GT, 2, E_R], FR)
        gate_t = sb("gate_t", [P, TG], FR)
        up_raw = sb("up_raw", [P, 2, C2, P])
        dn_raw = sb("dn_raw", [P, 2, D])
        up_w = sb("up_w", [P, 2, 2, C2, P], FR)
        dn_w = sb("dn_w", [P, 2, 2, D], FR)
        sel = sb("sel", [P, 2, P], FR)
        act_r = sb("act_r", [P, 2, N])
        act_g = sb("act_g", [P, 2, N])
        g_hi = sb("g_hi", [P, 2, N], FR)
        g_lo = sb("g_lo", [P, 2, N], FR)
        y_t = sb("y_t", [P, C2, TG])
        y_out = sb("y_out", [P, GT, D])
        settle = sb("settle", [P, 1])
        pool_settle = sb("pool_settle", [P, 1])
        minus_half = sb("f_minus_half", [P, GT])
        ps_h = ctx.enter_context(nc.psum_tensor("ps_h", [P, 2, N], F32))
        ps_c = ctx.enter_context(nc.psum_tensor("ps_c", [P, 2, N], F32))
        ps_acc = ctx.enter_context(nc.psum_tensor("ps_acc", [P, C2, 2, N], F32))

        loaded, made, turned_w = sem("f_loaded"), sem("f_made"), sem("turned_w")
        router_done, gbo_done, pick_done = sem("router_done"), sem("gbo_done"), sem("pick_done")
        link, var_done, rstd_step, rstd_done = sem("link"), sem("var_done"), sem("f_rstd_step"), sem("f_rstd_done")
        x_normed, x_turned, x_copied, x_high, x_low = (sem("x_normed"), sem("x_turned"), sem("x_copied"),
                                                       sem("x_high"), sem("x_low"))
        logits_done, tanh_done, gates_done, gates_turned, gates_t_done = (
            sem("logits_done"), sem("tanh_done"), sem("gates_done"), sem("gates_turned"), sem("gates_t_done"))
        up_loaded = [sem("up_loaded_even"), sem("up_loaded_odd")]
        dn_loaded = [sem("dn_loaded_even"), sem("dn_loaded_odd")]
        up_hi, up_lo, dn_hi, dn_lo, sel_done = sem("up_hi"), sem("up_lo"), sem("dn_hi"), sem("dn_lo"), sem("sel_done")
        s_up, s_dn, s_relu, s_u, s_g, s_ghi, s_glo = (sem("s_up"), sem("s_dn"), sem("s_relu"), sem("s_u"),
                                                      sem("s_g"), sem("s_ghi"), sem("s_glo"))
        y_copied, y_turned, y_added, out_stored = sem("y_copied"), sem("y_turned"), sem("y_added"), sem("out_stored")

        def experts(eng, visit):
            def run(g):
                for x in range(E_S):
                    visit(g, x, None, x)
                with eng.Fori(0, (E_R - 2) // 2) as i:
                    for par in range(2):
                        visit(g, i * 2 + par + E_S, i * 2 + par, -1 - par)
                for x in range(NE - 2, NE):
                    visit(g, x, x - E_S, x)
            return run

        def is_last(static, by=0):
            return static >= NE - 2 and static + by >= NE

        block = ctx.enter_context(nc.Block())

        @block.sync
        def _(sp):
            sp.dma_start(bo[:], ins["bo"].partition_broadcast(P)).then_inc(loaded, 16)
            sp.dma_start(bias[:], ins["correction_bias"].partition_broadcast(P)).then_inc(loaded, 16)
            sp.dma_start(router[:], ins["router_w"]).then_inc(loaded, 16)

            def load_up(x, e, par):
                if e is None:
                    src = ins["shared_up_w"][:, x * P:(x + 1) * P]
                else:
                    src = ins["up_w"][bass.ds(e, 1)].rearrange("a c n -> (a c) n")
                sp.dma_start(up_raw[:, par], src.rearrange("(c p) n -> p c n", p=P)).then_inc(up_loaded[par], 16)

            def load_dn(x, e, par):
                if e is None:
                    src = ins["shared_down_w"][x * P:(x + 1) * P, :]
                else:
                    src = ins["down_w"][bass.ds(e, 1)].rearrange("a k n -> (a k) n")
                sp.dma_start(dn_raw[:, par], src).then_inc(dn_loaded[par], 16)

            def visit(g, x, e, static):
                par = x % 2 if isinstance(x, int) else (-1 - static) % 2
                base = g * NE + x
                if not is_last(static, 2):
                    sp.wait_ge(up_lo, base + 1)
                    nxt = (x + 2, None) if static in (0, 1) else (None, (e if e is not None else x - E_S) + 2)
                    load_up(*nxt, par)
                if not is_last(static, 1):
                    if static != 0:
                        sp.wait_ge(dn_lo, 1 + base)
                    nxt = (x + 1, None) if static in (0, 1, 2) else (None, (e if e is not None else x - E_S) + 1)
                    load_dn(*nxt, 1 - par)

            with sp.Fori(0, groups) as g:
                sp.wait_ge(dn_lo, 1 + g * NE)
                load_up(0, None, 0)
                load_up(1, None, 1)
                load_dn(0, None, 0)
                experts(sp, visit)(g)
                sp.wait_ge(y_added, 1 + g * (GT // 2) + GT // 2)
                sp.dma_start(out[bass.ds(g * 2, 2)].rearrange("b (t p) c -> p (b t) c", p=P), y_out[:]
                             ).then_inc(out_stored, 16)
            sp.wait_ge(out_stored, 1 + 16 * groups)

        @block.gpsimd
        def _(pool):
            for counted in (out_stored, y_added, dn_lo):
                pool.sem_inc(counted, 1)
            pool.tensor_tensor(f32(pick[:]), pers.ident[:, 0:E_R], pers.ident[:, E_R:P], ALU.add).then_inc(made, 1)
            pool.memset(earlier[:], 1.0).then_inc(made, 1)
            pool.wait_ge(made, 2)
            pool.affine_select(out=earlier[:], in_=earlier[:], compare_op=ALU.is_gt, fill=0.0, base=0,
                               pattern=[[1, GROUPS_R], [-1, GROUPS_R]], channel_multiplier=0).then_inc(made, 1)
            pool.wait_ge(made, 3)

            def choose(e, par):
                pool.tensor_tensor(pool_settle[:], pers.ones[:], pers.ones[:], ALU.mult)
                src = pick[:, e:e + 1] if isinstance(e, int) else pick[:, bass.ds(e, 1)]
                pool.tensor_copy(sel[:, par], src.broadcast_to([P, P])).then_inc(sel_done, 1)

            def visit(g, x, e, static):
                par = x % 2 if isinstance(x, int) else (-1 - static) % 2
                base = g * NE + x
                if not is_last(static, 1):
                    pool.wait_ge(up_hi, base + 2)
                    pool.tensor_tensor(up_w[:, 1 - par, 1], up_raw[:, 1 - par], f32(up_w[:, 1 - par, 0]),
                                       ALU.subtract).then_inc(up_lo, 1)
                    if static not in (0, 1, 2):
                        nxt = (e if e is not None else x - E_S) + 1
                        pool.wait_ge(s_up, base * 2)
                        choose(nxt, 1 - par)
                pool.wait_ge(dn_hi, base + 1)
                pool.tensor_tensor(dn_w[:, par, 1], dn_raw[:, par], f32(dn_w[:, par, 0]), ALU.subtract
                                   ).then_inc(dn_lo, 1)

            with pool.Fori(0, groups) as g:
                pool.wait_ge(var_done, g + 1)
                pool.tensor_tensor(rstd[:, 0], moments[:, :, 1], pers.eps[:].broadcast_to([P, GT]), ALU.add
                                   ).then_inc(rstd_step, 1)
                pool.wait_ge(rstd_step, g + 1)
                pool.tensor_tensor(rstd[:, 1], rstd[:, 0], minus_half[:], ALU.pow).then_inc(rstd_done, 1)
                pool.wait_ge(up_hi, g * NE + 1)
                pool.tensor_tensor(up_w[:, 0, 1], up_raw[:, 0], f32(up_w[:, 0, 0]), ALU.subtract).then_inc(up_lo, 1)
                experts(pool, visit)(g)

        @block.tensor
        def _(pe):
            pe.wait_ge(loaded, 48)
            for c in range(C2):
                mm = pe.transpose(ps_c[:, 0, c * E_R:(c + 1) * E_R], router[:, c * P:(c + 1) * P],
                                  pers.ident[0:E_R, 0:E_R])
            mm.then_inc(turned_w, 1)

            def down(g, base, par, static, n, last):
                pe.wait_ge(s_glo, base * 2 + n + 1)
                if n == 0:
                    pe.wait_ge(dn_lo, 1 + base + 1)
                first = static == 0
                for m in range(C2):
                    for k, (wp, gp) in enumerate(((0, g_hi), (0, g_lo), (1, g_hi))):
                        mm = pe.matmul(ps_acc[:, m, n], dn_w[:, par, wp, m * P:(m + 1) * P], gp[:, n],
                                       start=(first and k == 0), stop=(last and k == 2))
                mm.then_inc(s_dn, 1)

            def visit(g, x, e, static):
                par = x % 2 if isinstance(x, int) else (-1 - static) % 2
                base = g * NE + x
                for n in range(2):
                    if n == 0:
                        pe.wait_ge(up_lo, base + 1)
                        if e is not None:
                            pe.wait_ge(sel_done, g * E_R + e + 1)
                    if static != 0:
                        pe.wait_ge(s_relu, base * 2 + n - 1)
                    k = 0
                    for c in range(C2):
                        for wp, xp in ((0, 0), (0, 1), (1, 0)):
                            mm = pe.matmul(ps_h[:, n], up_w[:, par, wp, c], x_t[:, xp, c, n * N:(n + 1) * N],
                                           start=(k == 0), stop=(k == 5))
                            k += 1
                    if e is not None:
                        if static != E_S and not (isinstance(e, int) and e == 0):
                            pe.wait_ge(s_u, g * (2 * E_R) + e * 2 + n + 1)
                        mm = pe.matmul(ps_c[:, n], sel[:, par], gate_t[:, n * N:(n + 1) * N], start=True, stop=True)
                    mm.then_inc(s_up, 1)
                    if static != 0:
                        down(g, base - 1, 1 - par, (static - 1 if static >= 0 else 99), n, False)

            with pe.Fori(0, groups) as g:
                for t in range(GT):
                    pass
                pe.wait_ge(x_normed, g + 1)
                pe.wait_ge(y_added, 1 + g * (GT // 2))
                pe.wait_ge(router_done, 1)
                for c in range(C2):
                    for n in range(2):
                        for t in range(GT // 2):
                            mm = pe.transpose(ps_acc[:, c, n, t * P:(t + 1) * P],
                                              x_nat[:, n * (GT // 2) + t, c * P:(c + 1) * P], pers.ident[:])
                        mm.then_inc(x_turned, 1)
                pe.wait_ge(x_copied, g * 4 + 4)
                for t in range(GT):
                    for c in range(C2):
                        mm = pe.matmul(ps_c[:, 0, t * E_R:(t + 1) * E_R], x_f[:, c, t * P:(t + 1) * P],
                                       router_t[:, c], start=(c == 0), stop=(c == C2 - 1))
                mm.then_inc(logits_done, 1)
                pe.wait_ge(gates_done, g + 1)
                for n in range(2):
                    for t in range(GT // 2):
                        mm = pe.transpose(ps_h[:, n, t * P:(t + 1) * P],
                                          f32(gate_parts[:, n * (GT // 2) + t]).rearrange("p k e -> p (k e)"),
                                          pers.ident[:])
                    mm.then_inc(gates_turned, 1)
                pe.wait_ge(gates_t_done, g * 2 + 2)
                pe.wait_ge(x_low, g * 4 + 4)
                experts(pe, visit)(g)
                for n in range(2):
                    down(g, g * NE + (NE - 1), (NE - 1) % 2, NE - 1, n, True)
                pe.wait_ge(y_copied, g * 4 + 4)
                for t in range(GT):
                    bank = ps_acc[:, t // 4, (t % 4) // 2]
                    for c in range(C2):
                        o = ((t % 2) * C2 + c) * P
                        mm = pe.transpose(bank[:, o:o + P], y_t[:, c, t * P:(t + 1) * P], pers.ident[:])
                    mm.then_inc(y_turned, 1)

        @block.scalar
        def _(act):
            act.wait_ge(turned_w, 1)
            act.activation(router_t[:], ps_c[:, 0, 0:C2 * E_R].rearrange("p (c e) -> p c e", c=C2), ACT.Copy
                           ).then_inc(router_done, 1)

            def high(g, base, n, first):
                act.wait_ge(s_g, base * 2 + n + 1)
                if not first:
                    act.wait_ge(s_dn, base * 2 + n - 1)
                act.activation(g_hi[:, n], act_g[:, n], ACT.Copy).then_inc(s_ghi, 1)

            def visit(g, x, e, static):
                par = x % 2 if isinstance(x, int) else (-1 - static) % 2
                base = g * NE + x
                half = (x // 2) if isinstance(x, int) else None
                for n in range(2):
                    act.wait_ge(s_up, base * 2 + n + 1)
                    if static != 0:
                        act.wait_ge(s_g, base * 2 + n - 1)
                    act.activation(act_r[:, n], ps_h[:, n], ACT.Relu).then_inc(s_relu, 1)
                    if n == 0:
                        if static != 0:
                            high(g, base - 1, 1, static == 1)
                        if not is_last(static, 1):
                            act.wait_ge(up_loaded[1 - par], (g * (NE // 2) + (x + 1 - (1 - par)) // 2) * 16 + 16)
                            if static != 0:
                                act.wait_ge(s_up, base * 2)
                            act.activation(up_w[:, 1 - par, 0], up_raw[:, 1 - par], ACT.Copy).then_inc(up_hi, 1)
                        act.wait_ge(dn_loaded[par], (g * (NE // 2) + (x - par) // 2) * 16 + 16)
                        if static not in (0, 1):
                            act.wait_ge(s_dn, base * 2 - 2)
                        act.activation(dn_w[:, par, 0], dn_raw[:, par], ACT.Copy).then_inc(dn_hi, 1)
                    else:
                        high(g, base, 0, static == 0)

            with act.Fori(0, groups) as g:
                for c in range(C2):
                    for n in range(2):
                        act.wait_ge(x_turned, g * 4 + 2 * c + n + 1)
                        act.activation(x_f[:, c, n * N:(n + 1) * N], ps_acc[:, c, n], ACT.Copy).then_inc(x_copied, 1)
                for c in range(C2):
                    for n in range(2):
                        act.wait_ge(x_copied, g * 4 + 2 * c + n + 1)
                        act.activation(x_t[:, 0, c, n * N:(n + 1) * N], x_f[:, c, n * N:(n + 1) * N], ACT.Copy
                                       ).then_inc(x_high, 1)
                act.wait_ge(logits_done, g + 1)
                act.activation(prob[:].rearrange("p t e -> p (t e)"), ps_c[:, 0], ACT.Tanh, scale=0.5
                               ).then_inc(tanh_done, 1)
                act.wait_ge(up_loaded[0], g * (16 * NE // 2) + 16)
                act.activation(up_w[:, 0, 0], up_raw[:, 0], ACT.Copy).then_inc(up_hi, 1)
                for n in range(2):
                    act.wait_ge(gates_turned, g * 2 + n + 1)
                    act.activation(gate_t[:, n * N:(n + 1) * N], ps_h[:, n], ACT.Copy).then_inc(gates_t_done, 1)
                experts(act, visit)(g)
                high(g, g * NE + (NE - 1), 1, False)
                act.wait_ge(s_dn, g * (2 * NE) + 2 * NE)
                for c in range(C2):
                    for n in range(2):
                        act.activation(y_t[:, c, n * N:(n + 1) * N], ps_acc[:, c, n], ACT.Copy,
                                       scale=pers.gates[:, 1:2]).then_inc(y_copied, 1)

        @block.vector
        def _(dve):
            dve.wait_ge(loaded, 48)
            dve.wait_ge(made, 3)
            dve.memset(minus_half[:], -0.5).then_inc(gbo_done, 1)
            dve.tensor_scalar(bo[:], bo[:], pers.gates[:, 0:1], None, ALU.mult).then_inc(gbo_done, 1)
            dve.wait_ge(gbo_done, 2)

            def low(base, n):
                dve.wait_ge(s_ghi, base * 2 + n + 1)
                dve.tensor_tensor(g_lo[:, n], act_g[:, n], f32(g_hi[:, n]), ALU.subtract).then_inc(s_glo, 1)

            def visit(g, x, e, static):
                base = g * NE + x
                for n in range(2):
                    dve.wait_ge(s_relu, base * 2 + n + 1)
                    if static != 0:
                        dve.wait_ge(s_glo, base * 2 + n - 1)
                    if e is None:
                        dve.tensor_tensor(act_g[:, n], act_r[:, n], act_r[:, n], ALU.mult).then_inc(s_g, 1)
                    else:
                        dve.tensor_tensor(act_g[:, n], act_r[:, n], ps_c[:, n], ALU.mult).then_inc(s_u, 1)
                        dve.wait_ge(s_u, g * (2 * E_R) + e * 2 + n + 3)
                        dve.tensor_tensor(act_g[:, n], act_g[:, n], act_r[:, n], ALU.mult).then_inc(s_g, 1)
                    if n == 0:
                        if static != 0:
                            low(base - 1, 1)
                    else:
                        low(base, 0)

            dve.sem_inc(s_u, 2)
            LINKS = 22
            with dve.Fori(0, groups) as g:
                k = 0

                def done(instruction):
                    nonlocal k
                    k += 1
                    instruction.then_inc(link, 1)
                    dve.wait_ge(link, g * LINKS + k)

                def settled():
                    dve.memset(settle[:], 0.0)

                x1g = pers.x1[:, bass.ds(g * GT, GT), :]
                done(dve.tensor_tensor(x1g, x1g, bo[:].unsqueeze(1).broadcast_to([P, GT, D]), ALU.add))
                settled()
                for t in range(GT):
                    st = dve.bn_stats(stats[:, t], x1g[:, t])
                done(st)
                settled()
                for t in range(GT):
                    st = dve.bn_aggr(moments[:, t], stats[:, t])
                st.then_inc(var_done, 1)
                dve.wait_ge(rstd_done, g + 1)
                for t in range(GT):
                    st = dve.tensor_scalar(x_nat[:, t], x1g[:, t], moments[:, t, 0:1], rstd[:, 1, t:t + 1],
                                           ALU.subtract, ALU.mult)
                st.then_inc(x_normed, 1)
                for c in range(C2):
                    for n in range(2):
                        dve.wait_ge(x_high, g * 4 + 2 * c + n + 1)
                        dve.tensor_tensor(x_t[:, 1, c, n * N:(n + 1) * N], x_f[:, c, n * N:(n + 1) * N],
                                          f32(x_t[:, 0, c, n * N:(n + 1) * N]), ALU.subtract).then_inc(x_low, 1)
                dve.wait_ge(tanh_done, g + 1)
                done(dve.tensor_scalar(prob[:], prob[:], 0.5, 0.5, ALU.mult, ALU.add))
                done(dve.tensor_tensor(biased[:], prob[:], bias[:].unsqueeze(1).broadcast_to([P, GT, E_R]), ALU.add))
                settled()
                for t in range(GT):
                    for gr in range(GROUPS_R):
                        st = dve.max(best[:, t, gr], biased[:, t, gr * PER_G:(gr + 1) * PER_G])
                done(st)
                done(dve.tensor_tensor(g_score[:], best[:, :, :, 0], best[:, :, :, 1], ALU.add))
                for t in range(GT):
                    other = g_score[:, t].unsqueeze(1).broadcast_to([P, GROUPS_R, GROUPS_R])
                    own = g_score[:, t].unsqueeze(2).broadcast_to([P, GROUPS_R, GROUPS_R])
                    dve.tensor_tensor(cmp_a[:, t], other, own, ALU.is_gt)
                    st = dve.tensor_tensor(cmp_b[:, t], other, own, ALU.is_equal)
                done(st)
                done(dve.tensor_tensor(cmp_b[:].rearrange("p t i j -> p t (i j)"), cmp_b[:].rearrange("p t i j -> p t (i j)"),
                                       earlier[:].rearrange("p i j -> p (i j)").unsqueeze(1).broadcast_to(
                                           [P, GT, GROUPS_R * GROUPS_R]), ALU.mult))
                done(dve.tensor_tensor(cmp_a[:], cmp_a[:], cmp_b[:], ALU.add))
                done(dve.tensor_reduce(g_rank[:], cmp_a[:], mybir.AxisListType.X, ALU.add))
                done(dve.tensor_scalar(g_rank[:], g_rank[:], float(TOP_G), None, ALU.is_lt))
                done(dve.tensor_tensor(biased[:].rearrange("p t (i j) -> p (t i) j", j=PER_G),
                                       biased[:].rearrange("p t (i j) -> p (t i) j", j=PER_G),
                                       g_rank[:].rearrange("p t i -> p (t i)").unsqueeze(2).broadcast_to(
                                           [P, GT * GROUPS_R, PER_G]), ALU.mult))
                settled()
                for t in range(GT):
                    st = dve.max(top8[:, t], biased[:, t])
                done(st)
                settled()
                for t in range(GT):
                    st = dve.match_replace(out=gate[:, t], in_to_replace=top8[:, t], in_values=biased[:, t],
                                           imm_value=TAKEN)
                done(st)
                done(dve.tensor_scalar(gate[:], gate[:], TAKEN, None, ALU.is_equal))
                done(dve.tensor_tensor(gate[:], gate[:], prob[:], ALU.mult))
                done(dve.tensor_reduce(total[:], gate[:], mybir.AxisListType.X, ALU.add))
                done(dve.tensor_scalar(total[:], total[:], 1e-20, None, ALU.add))
                done(dve.reciprocal(total[:], total[:]))
                done(dve.tensor_scalar(total[:], total[:], ROUTE_SCALE, None, ALU.mult))
                done(dve.tensor_tensor(gate[:], gate[:], total[:].unsqueeze(2).broadcast_to([P, GT, E_R]), ALU.mult))
                done(dve.tensor_copy(gate_parts[:, :, 0], gate[:]))
                dve.tensor_tensor(gate_parts[:, :, 1], gate[:], f32(gate_parts[:, :, 0]), ALU.subtract
                                  ).then_inc(gates_done, 1)
                assert k == LINKS, k
                experts(dve, visit)(g)
                low(g * NE + (NE - 1), 1)
                for t in range(0, GT, 2):
                    dve.wait_ge(y_turned, g * GT + t + 2)
                    if t == 0:
                        dve.wait_ge(out_stored, 1 + g * 16)
                    dve.tensor_tensor(y_out[:, t:t + 2], ps_acc[:, t // 4, (t % 4) // 2].rearrange(
                        "p (t n) -> p t n", t=2), x1g[:, t:t + 2], ALU.add).then_inc(y_added, 1)



INS = {"x": "x", "ctx_1024": "ctx", "g_xattn": "g_xattn", "g_ffn": "g_ffn", "L0_xattn_cos": "cos", "L0_xattn_sin": "sin",
       "L0_xattn_ln_lat_g": "ln_lat_g", "L0_xattn_ln_lat_b": "ln_lat_b", "L0_xattn_ln_ctx_g": "ln_ctx_g",
       "L0_xattn_ln_ctx_b": "ln_ctx_b", "L0_xattn_Wq": "Wq", "L0_xattn_Wkv": "Wkv", "L0_xattn_Wo": "Wo",
       "L0_xattn_bo": "bo", "L0_ffn_router_w": "router_w", "L0_ffn_correction_bias": "correction_bias",
       "L0_ffn_up_w": "up_w", "L0_ffn_down_w": "down_w", "L0_ffn_shared_up_w": "shared_up_w",
       "L0_ffn_shared_down_w": "shared_down_w"}


def program(nc, ins, out):
    w_dram = nc.dram_tensor("w_pairs", [PAIRS + 1, P, 2 * C2 * 4 * P], F32, kind="Internal").ap()
    wo_dram = nc.dram_tensor("wo_heads", [PAIRS, P, 2, 2, D], F32, kind="Internal").ap()
    with ExitStack() as ctx:
        pers = Persistent(nc, ctx)
        setup(nc, pers, ins, w_dram, wo_dram)
        attention(nc, pers, ins, w_dram, wo_dram)
        ffn(nc, pers, ins, out)


def kernel(**inputs):
    import numpy as _np
    import concourse.bacc as _bacc
    from concourse.bass_utils import run_bass_kernel_spmd as _run

    nc = _bacc.Bacc("TRN2", target_bir_lowering=False, num_devices=1)
    arrays, ins = {}, {}
    for name, short in INS.items():
        a = _np.ascontiguousarray(inputs[name])
        arrays[f"in_{name}"] = a
        ins[short] = nc.dram_tensor(f"in_{name}", a.shape, mybir.dt.from_np(a.dtype), kind="ExternalInput").ap()
    out = nc.dram_tensor("out_0", (B, N, D), F32, kind="ExternalOutput").ap()
    program(nc, ins, out)
    r = _run(nc, [arrays], core_ids=[0])
    return r.results[0]["out_0"]
```

```python
from contextlib import ExitStack

import concourse.bass as bass
from concourse import mybir

ALU = mybir.AluOpType
ACT = mybir.ActivationFunctionType
F32 = mybir.dt.float32
FR = mybir.dt.float32r

P = 128
B, N, S, D = 8, 512, 1024, 256
H, DH = 16, 64
PAIRS = H // 2
NT = N // P
ST = S // P
C2 = D // P
EPS = 1e-5
CH = 2 * N
EXP_LO = 1.670170079024566e-05
EXP_HI = 59874.14171519782
SCALE = DH ** -0.5


def f32(ap):
    return ap.bitcast(F32)


class Persistent:

    def __init__(self, nc, ctx):
        def sb(name, shape, dt=F32):
            return ctx.enter_context(nc.sbuf_tensor(name, shape, dt))

        self.ident = sb("ident", [P, P])
        self.x1 = sb("x1", [P, B * NT, D])
        self.cos = sb("cos", [P, ST, DH // 2])
        self.sin = sb("sin", [P, ST, DH // 2])
        self.gain = sb("gain", [P, 2, C2])
        self.shift = sb("shift", [P, 2, C2])
        self.gates = sb("gates", [P, 2])
        self.minus_half = sb("minus_half", [P, NT])
        self.ones = sb("ones", [P, 1])
        self.eps = sb("eps", [P, 1])


def setup(nc, pers, ins, w_dram, wo_dram):
    with ExitStack() as ctx:
        def sb(name, shape, dt=F32):
            return ctx.enter_context(nc.sbuf_tensor(name, shape, dt))

        def sem(name):
            return ctx.enter_context(nc.semaphore(name))

        raw = sb("w_raw", [P, C2, 3, PAIRS, P])
        split = sb("w_split", [P, PAIRS, 2, C2, 4, P], FR)
        wo_raw = sb("wo_raw", [DH, H, D])
        wo_split = sb("wo_split", [DH, H, 2, D], FR)
        gates_in = sb("gates_in", [P, 2])
        wq_loaded, wo_loaded, x_loaded = sem("wq_loaded"), sem("wo_loaded"), sem("x_loaded_first")
        gates_done, w_hi, lo_done, stored = sem("tanh_of_gates"), sem("w_hi"), sem("lo_done"), sem("stored")
        wo_hi_done, wo_lo_done, wo_stored = sem("wo_hi_done"), sem("wo_lo_done"), sem("wo_stored")
        zeroed, selected = sem("zeroed"), sem("selected")

        def parts(part, pair, c):
            queries = raw[:, c, 0, pair].rearrange("p (h d) -> p h d", h=2).unsqueeze(2)
            return ((split[:, pair, part, c, 0:2], raw[:, c, 1:3, pair]),
                    (split[:, pair, part, c, 2:4].rearrange("p h (r d) -> p h r d", r=2),
                     queries.broadcast_to([P, 2, 2, DH])))

        block = ctx.enter_context(nc.Block())

        @block.sync
        def _(sp):
            for c in range(C2):
                sp.dma_start(raw[:, c, 0], ins["Wq"][c * P:(c + 1) * P, :].rearrange("p (g m) -> p g m", m=P)
                             ).then_inc(wq_loaded, 16)
                sp.dma_start(raw[:, c, 1:3], ins["Wkv"][c * P:(c + 1) * P, :].rearrange(
                    "p (t g m) -> p t g m", t=2, m=P)).then_inc(wq_loaded, 16)
            sp.dma_start(wo_raw[:], ins["Wo"].rearrange("(h d) n -> d h n", d=DH)).then_inc(wo_loaded, 16)
            sp.dma_start(pers.x1[:, 0:NT, :], ins["x"][0].rearrange("(t p) c -> p t c", p=P)).then_inc(x_loaded, 16)
            for pair in range(PAIRS):
                sp.wait_ge(lo_done, pair + 1)
                sp.dma_start(w_dram[pair], f32(split[:, pair]).rearrange("p a c t m -> p (a c t m)")
                             ).then_inc(stored, 16)
            sp.wait_ge(wo_lo_done, 1)
            for hh in range(2):
                last = PAIRS - 1 - hh
                heads = f32(wo_split[:]).rearrange("d (j h) k n -> d j h k n", h=2)[:, :, hh]
                sp.dma_start(wo_dram[hh + 1:PAIRS, :, hh].rearrange("j d k n -> d j k n"), heads[:, 0:last]
                             ).then_inc(wo_stored, 16)
                sp.dma_start(wo_dram[0:hh + 1, :, hh].rearrange("j d k n -> d j k n"), heads[:, last:PAIRS]
                             ).then_inc(wo_stored, 16)
            sp.wait_ge(stored, 16 * PAIRS)
            sp.wait_ge(wo_stored, 16 * 4)
            sp.wait_ge(x_loaded, 16)

        @block.scalar
        def _(act):
            loads = sem("small_loads")
            act.dma_start(pers.cos[:], ins["cos"].rearrange("(t p) d -> p t d", p=P)).then_inc(loads, 16)
            act.dma_start(pers.sin[:], ins["sin"].rearrange("(t p) d -> p t d", p=P)).then_inc(loads, 16)
            for k, who in enumerate(("lat", "ctx")):
                for c in range(C2):
                    act.dma_start(pers.gain[:, k, c:c + 1], ins[f"ln_{who}_g"][c * P:(c + 1) * P].unsqueeze(1)
                                  ).then_inc(loads, 16)
                    act.dma_start(pers.shift[:, k, c:c + 1], ins[f"ln_{who}_b"][c * P:(c + 1) * P].unsqueeze(1)
                                  ).then_inc(loads, 16)
            act.dma_start(gates_in[:, 0:1], ins["g_xattn"].partition_broadcast(P)).then_inc(loads, 16)
            act.dma_start(gates_in[:, 1:2], ins["g_ffn"].partition_broadcast(P)).then_inc(loads, 16)
            act.wait_ge(wq_loaded, 16 * 4)
            for pair in range(PAIRS):
                for c in range(C2):
                    for dst, src in parts(0, pair, c):
                        act.activation(dst, src, ACT.Copy).then_inc(w_hi, 1)
            act.wait_ge(wo_loaded, 16)
            act.activation(wo_split[:, :, 0], wo_raw[:], ACT.Copy).then_inc(wo_hi_done, 1)
            act.wait_ge(loads, 16 * 12)
            act.activation(pers.gates[:], gates_in[:], ACT.Tanh).then_inc(gates_done, 1)

        @block.gpsimd
        def _(pool):
            pool.memset(pers.ident[:], 0.0).then_inc(zeroed, 1)
            pool.memset(pers.minus_half[:], -0.5)
            pool.memset(pers.eps[:], EPS)
            pool.memset(pers.ones[:], 1.0).then_inc(zeroed, 1)
            pool.wait_ge(zeroed, 2)
            pool.affine_select(out=pers.ident[:], in_=pers.ident[:], compare_op=ALU.not_equal, fill=1.0,
                               base=0, pattern=[[-1, P]], channel_multiplier=1).then_inc(selected, 1)
            pool.wait_ge(selected, 1)

        @block.vector
        def _(dve):
            for pair in range(PAIRS):
                dve.wait_ge(w_hi, 2 * C2 * (pair + 1))
                for c in range(C2):
                    for (dst, src), (high, _) in zip(parts(1, pair, c), parts(0, pair, c)):
                        last = dve.tensor_tensor(dst, src, f32(high), ALU.subtract)
                last.then_inc(lo_done, 1)
            dve.wait_ge(wo_hi_done, 1)
            dve.tensor_tensor(wo_split[:, :, 1], wo_raw[:], f32(wo_split[:, :, 0]), ALU.subtract
                              ).then_inc(wo_lo_done, 1)


def attention(nc, pers, ins, w_dram, wo_dram):
    with ExitStack() as ctx:
        def sb(name, shape, dt=F32):
            return ctx.enter_context(nc.sbuf_tensor(name, shape, dt))

        def sem(name):
            return ctx.enter_context(nc.semaphore(name))

        x_nat = sb("x_nat", [P, NT + ST, D])
        stats = sb("stats", [P, NT + ST, 6])
        moments = sb("moments", [P, NT + ST, 2])
        power = sb("power", [P, 3, NT + ST])
        affine = sb("affine", [P, 2, C2, N])
        ctx_t = sb("ctx_t", [P, 2, C2, S], FR)
        lat_t = sb("lat_t", [P, 2, C2, N], FR)
        w = sb("w", [P, 2, 2, C2, 4, P], FR)
        wo = sb("wo", [P, 2, 2, D], FR)
        k_t = sb("k_t", [P, 2, 2, S], FR)
        v = sb("v", [P, 2, ST, 2, P], FR)
        q_t = sb("q_t", [P, 2, 2, 2, N], FR)
        rope_c = sb("rope_c", [P, 2, 2, DH])
        rope_s = sb("rope_s", [P, 2, 2, DH])
        k_rot = sb("k_rot", [P, 2, 2, DH])
        k_nat = sb("k_nat", [P, 2, 2, P], FR)
        e = sb("e", [P, 4, CH])
        e_hi = sb("e_hi", [P, 4, CH], FR)
        e_lo = sb("e_lo", [P, 2, CH], FR)
        e_sum = sb("e_sum", [P, CH])
        e_fold = sb("e_fold", [P, 2, N])
        o_hi = sb("o_hi", [P, 2, N], FR)
        o_lo = sb("o_lo", [P, N], FR)
        settle = sb("settle_a", [P, 1])
        r_den = sb("r_den", [P, 2, NT])
        r_gate = sb("r_gate", [P, 2, NT])
        scores = ctx.enter_context(nc.psum_tensor("scores", [P, 2, CH], F32))
        ps_o = ctx.enter_context(nc.psum_tensor("ps_o", [P, N], F32))
        ps_kv = ctx.enter_context(nc.psum_tensor("ps_kv", [P, N], F32))
        ps_kt = ctx.enter_context(nc.psum_tensor("ps_kt", [P, N], F32))
        ps_y = ctx.enter_context(nc.psum_tensor("ps_y", [P, 2, D], F32))
        DEN = 256

        init = sem("init")
        x_first, x1_loaded, x_loaded = sem("x_first"), sem("x1_loaded"), (sem("x_loaded_even"), sem("x_loaded_odd"))
        stats_done, rstd_step, rstd_done = sem("stats_done"), sem("rstd_step"), sem("rstd_done")
        normed, turned = sem("normed"), sem("turned")
        aff_act, aff_dve, t_hi, t_lo = sem("aff_act"), sem("aff_dve"), sem("t_hi"), sem("t_lo")
        w_loaded, wo_loaded = (sem("w_loaded_even"), sem("w_loaded_odd")), sem("wo_loaded")
        s_scores, s_exp, s_clip, s_ehi, s_elo, s_sum = (sem("s_scores"), sem("s_exp"), sem("s_clip"),
                                                         sem("s_ehi"), sem("s_elo"), sem("s_sum"))
        s_pv, s_ohi, s_olo = sem("s_pv"), sem("s_ohi"), sem("s_olo")
        s_kv, s_m0, s_vhi, s_vlo = sem("s_kv"), sem("s_m0"), sem("s_vhi"), sem("s_vlo")
        s_rope, s_rot, s_khi, s_klo, s_kt, s_kte = (sem("s_rope"), sem("s_rot"), sem("s_khi"), sem("s_klo"),
                                                    sem("s_kt"), sem("s_kte"))
        s_q, s_qhi, s_den, s_y, s_m2 = sem("s_q"), sem("s_qhi"), sem("s_den"), sem("s_y"), sem("s_m2")
        bn_done, s_rden, s_gate = sem("bn_done"), sem("s_rden"), sem("s_gate")

        DEN_HEAD = {2: 1, 6: 0}
        QUERIES = {0: 0, 2: 1}
        OUT = {4: (1, 0), 5: (1, 1), 6: (0, 0), 7: (0, 1)}
        SUM_FREE = [1, 1, 2, 3]

        LAT_SLOT, CTX_SLOT = 0, 4
        UNITS = NT + ST

        def units_before(g, jj):
            return 2 + (g - jj) // 2 * 3 + 2 * jj

        def loop(eng, step, boundary=None, per_iteration=None, prepare=None):
            with eng.Fori(0, B) as b:
                if boundary:
                    boundary(b)
                with eng.Fori(0, PAIRS // 2) as i:
                    for jj in range(2):
                        g = b * PAIRS + i * 2 + jj
                        if per_iteration:
                            per_iteration(b, g, i * 2 + jj, jj)
                        for c in range(8):
                            step(g, jj, c, True, True)
                            if prepare:
                                prepare(b, i, jj, g, c)
            g = B * PAIRS
            if per_iteration:
                per_iteration(None, g, 0, 0)
            for c in range(8):
                step(g, 0, c, False, True)
            for c in range(7):
                step(g + 1, 1, c, False, False)

        block = ctx.enter_context(nc.Block())

        @block.sync
        def _(sp):
            sp.dma_start(x_nat[:, NT:NT + ST], ins["ctx"][0].rearrange("(t p) c -> p t c", p=P)).then_inc(x_first, 16)
            sp.dma_start(f32(w[:, 0]).rearrange("p a c t m -> p (a c t m)"), w_dram[0]).then_inc(w_loaded[0], 16)
            for b in range(1, B):
                sp.dma_start(pers.x1[:, b * NT:(b + 1) * NT, :],
                             ins["x"][b].rearrange("(t p) c -> p t c", p=P)).then_inc(x1_loaded, 16)

            def load_wo(j):
                src = wo_dram[j] if isinstance(j, int) else wo_dram[bass.ds(j, 1)].rearrange("a d h k n -> (a d) h k n")
                for half in range(2):
                    sp.dma_start(f32(wo[half * DH:(half + 1) * DH]), src).then_inc(wo_loaded, 16)

            def per_iteration(b, g, j, jj):
                if not (isinstance(g, int)):
                    sp.wait_ge(s_kv, 1 + g * 8)
                    sp.dma_start(f32(w[:, 1 - jj]).rearrange("p a c t m -> p (a c t m)"),
                                 w_dram[bass.ds((j + 1) % PAIRS, 1)].rearrange("a p n -> (a p) n")).then_inc(w_loaded[1 - jj], 16)
                sp.wait_ge(s_y, 1 + g * 4)
                load_wo(j)

                if b is not None:
                    sp.wait_ge(turned, 1 + b * 6 + 6)
                    sp.dma_start(x_nat[:, bass.ds(NT + j, 1), :].rearrange("p a c -> p (a c)"),
                                 ins["ctx"][bass.ds((b + 1) % B, 1), bass.ds(j * P, P), :].rearrange("a p c -> (a p) c")
                                 ).then_inc(x_loaded[jj], 16)

            loop(sp, lambda *a: None, per_iteration=per_iteration)
            g = B * PAIRS + 1
            sp.wait_ge(s_y, 1 + 4 * g)
            load_wo(1)
            sp.wait_ge(w_loaded[0], 16 * (B * PAIRS // 2 + 1))
            sp.wait_ge(w_loaded[1], 16 * (B * PAIRS // 2))
            sp.wait_ge(wo_loaded, 32 * (B * PAIRS + 2))
            sp.wait_ge(x_first, 16)
            sp.wait_ge(x_loaded[0], 16 * (B * PAIRS // 2))
            sp.wait_ge(x_loaded[1], 16 * (B * PAIRS // 2))

        @block.tensor
        def _(pe):
            pe.wait_ge(init, 1)
            pe.matmul(ps_kv[:], v[:, 1, 0, 0, :], q_t[:, 1, 0, 0, :], start=True, stop=True)
            pe.matmul(ps_o[:], v[:, 1, 0, 0, :], q_t[:, 1, 0, 0, :], start=True, stop=False)
            pe.matmul(ps_y[:].rearrange("p a n -> p (a n)"), v[:, 1, 0, 0, :], q_t[:, 1, 0, 0, :], start=True, stop=True
                      ).then_inc(s_y, 1)

            def boundary(b):
                pe.wait_ge(normed, 2 + b * UNITS)
                pe.wait_ge(s_exp, 2 + b * (8 * PAIRS))
                for u in range(3):
                    if u == 2:
                        pe.wait_ge(aff_act, b * 3 + 1)
                        pe.wait_ge(aff_dve, b * 3 + 1)
                    for c in range(C2):
                        for t in range(NT):
                            mm = pe.transpose(scores[:, u % 2, c * N + t * P:c * N + (t + 1) * P],
                                              x_nat[:, u * NT + t, c * P:(c + 1) * P], pers.ident[:])
                        mm.then_inc(turned, 1)

            def step(g, jj, c, project, attend):
                att = 1 - jj
                q4 = c % 4
                if c == 0 and project and jj == 0:
                    pe.wait_ge(aff_act, g // PAIRS * 3 + 3)
                    pe.wait_ge(aff_dve, g // PAIRS * 3 + 3)
                if attend:
                    pe.wait_ge(s_exp, 1 + g * 8 + c)
                    if c == 0:
                        pe.wait_ge(s_m2, g * 6 + 1)
                        pe.wait_ge(s_kte, 1 + g * 8)
                    if c == 3:
                        pe.wait_ge(s_kte, 1 + g * 8 + 2)
                    for r in range(2):
                        s = 2 * q4 + r
                        for part in range(2):
                            mm = pe.matmul(scores[:, c % 2, r * N:(r + 1) * N],
                                           k_t[:, att, c // 4, s * P:(s + 1) * P],
                                           q_t[:, att, c // 4, part, :], start=(part == 0), stop=(part == 1))
                    mm.then_inc(s_scores, 1)
                turn = project or (attend and c < 2)
                if c in DEN_HEAD and (attend or c == 2):
                    hh = DEN_HEAD[c]
                    pe.wait_ge(s_kte, 1 + (g * 8 + c if project else B * PAIRS * 8 + 2))
                    if not project:
                        pe.wait_ge(s_rden, g * 2 + (0 if c == 2 else 1))
                    pe.wait_ge(s_sum, g * 8 + (4 if c == 2 else 8))
                    for t in range(NT):
                        mm = pe.matmul(ps_kt[:, DEN + t:DEN + t + 1], e_fold[:, hh, t * P:(t + 1) * P],
                                       pers.ones[:], start=True, stop=True)
                    mm.then_inc(s_den, 1)
                if c == 0 and project:
                    pe.wait_ge(t_lo, 1 + g // PAIRS * 6 + 6)
                    pe.wait_ge(w_loaded[jj], (g - jj) // 2 * 16 + 16)
                if project:
                    pe.wait_ge(s_m0, 1 + g * 8 + c + 1)
                    k = 0
                    for cc in range(C2):
                        for a, bb in ((0, 0), (0, 1), (1, 0)):
                            mm = pe.matmul(ps_kv[:, 0:2 * P], ctx_t[:, a, cc, c * P:(c + 1) * P],
                                           w[:, jj, bb, cc, 0:2].rearrange("p t m -> p (t m)"),
                                           start=(k == 0), stop=(k == 5))
                            k += 1
                    mm.then_inc(s_kv, 1)
                if project and c in QUERIES:
                    head = QUERIES[c]
                    pe.wait_ge(s_m2, g * 6 + 5 + head)
                    k = 0
                    for cc in range(C2):
                        for a, bb in ((0, 0), (0, 1), (1, 0)):
                            mm = pe.matmul(ps_y[:].rearrange("p a n -> p (a n)"), w[:, jj, bb, cc, 2 + head],
                                           lat_t[:, a, cc, :], start=(k == 0), stop=(k == 5))
                            k += 1
                    mm.then_inc(s_q, 1)
                if turn:
                    pe.wait_ge(s_kte, 1 + g * 8 + c)
                    if c in DEN_HEAD:
                        pe.wait_ge(s_rden, g * 2 + (1 if c == 2 else 2))
                    pe.wait_ge(s_klo, g * 8 + c + 1)
                    for hh in range(2):
                        mm = pe.transpose(ps_kt[:, hh * P:(hh + 1) * P], f32(k_nat[:, c % 2, hh]), pers.ident[:])
                    mm.then_inc(s_kt, 1)

                def project_out(hh, half, use):
                    pe.wait_ge(s_m2, use)
                    pe.wait_ge(s_olo, g * 2 + (1 if hh else 2))
                    pe.wait_ge(wo_loaded, g * 32 + 32)
                    for i in range(2):
                        t = 2 * half + i
                        for k, (o_part, wpart) in enumerate(((o_hi[:, hh], 0), (o_hi[:, hh], 1), (o_lo[:], 0))):
                            mm = pe.matmul(ps_y[:, i, :], o_part[:, t * P:(t + 1) * P], wo[:, hh, wpart, :],
                                           start=(k == 0), stop=(k == 2))
                    mm.then_inc(s_y, 1)

                if attend or c < 2:
                    x4 = (c + 2) % 4
                    hh = ((c + 6) % 8) // 4
                    buf = att if c >= 2 else 1 - att
                    pe.wait_ge(s_elo, 1 + g * 8 + c)
                    if c in (2, 6):
                        pe.wait_ge(s_olo, g * 2 + (1 if c == 2 else 2))
                    for r in range(2):
                        s = 2 * x4 + r
                        for part, e_part in enumerate((e_hi, e_lo)):
                            mm = pe.matmul(ps_o[:], v[:, buf, s, hh, :], e_part[:, x4 % (4 if part == 0 else 2), r * N:(r + 1) * N],
                                           start=(x4 == 0 and r == 0 and part == 0),
                                           stop=(x4 == 3 and r == 1 and part == 1))
                    mm.then_inc(s_pv, 1)
                if c in OUT and (attend or OUT[c][0] == 1):
                    hh, half = OUT[c]
                    before_it = g * 6 + 3 if project else B * PAIRS * 6 + 1 + (0 if attend else 4)
                    project_out(hh, half, 4 + before_it + (c - 4))

            loop(pe, step, boundary)

        @block.scalar
        def _(act):
            act.wait_ge(init, 1)

            def boundary(b):
                for u in range(3):
                    dst = (lat_t[:, 0], ctx_t[:, 0, :, 0:N], ctx_t[:, 0, :, N:S])[u]
                    k = 0 if u == 0 else 1
                    act.wait_ge(turned, 1 + b * 6 + 2 * u + 1)
                    act.wait_ge(t_lo, 1 + b * 6 + (2 if u == 2 else 0))
                    act.activation(affine[:, u % 2, 0], scores[:, u % 2, 0:N], ACT.Identity,
                                   bias=pers.shift[:, k, 0:1], scale=pers.gain[:, k, 0:1]).then_inc(aff_act, 1)
                    for c, done in enumerate((aff_act, aff_dve)):
                        act.wait_ge(done, b * 3 + u + 1)
                        act.activation(dst[:, c], affine[:, u % 2, c], ACT.Copy).then_inc(t_hi, 1)

            def step(g, jj, c, project, attend):
                if c in DEN_HEAD and (attend or c == 2):
                    hh = DEN_HEAD[c]
                    act.wait_ge(s_pv, 1 + g * 8 + c + 2)
                    act.activation(o_hi[:, hh], ps_o[:], ACT.Copy).then_inc(s_ohi, 1)
                if attend or c == 0:
                    act.wait_ge(s_clip, 1 + g * 8 + c)
                    act.wait_ge(s_pv, 1 + g * 8 + c)
                    act.activation(e_hi[:, (c + 3) % 4], e[:, (c + 3) % 4], ACT.Copy).then_inc(s_ehi, 1)
                if attend:
                    act.wait_ge(s_scores, g * 8 + c + 1)
                    act.wait_ge(s_sum, g * 8 + 4 * (c // 4) + SUM_FREE[c % 4])
                    act.activation(e[:, c % 4], scores[:, c % 2], ACT.Exp, scale=SCALE).then_inc(s_exp, 1)
                if project and c - 1 in QUERIES:
                    head = QUERIES[c - 1]
                    act.wait_ge(s_q, g * 2 + head + 1)
                    act.activation(q_t[:, jj, head, 0], ps_y[:].rearrange("p a n -> p (a n)"), ACT.Copy
                                   ).then_inc(s_qhi, 1)
                if project or (attend and c == 0):
                    act.wait_ge(s_rot, g * 8 + c + 1)
                    act.activation(k_nat[:, (c + 1) % 2, :, 0:DH], k_rot[:, (c + 1) % 2], ACT.Copy
                                   ).then_inc(s_khi, 1)
                if project:
                    act.wait_ge(s_kv, 1 + g * 8 + c + 1)
                    act.activation(v[:, jj, c, :, 0:DH], ps_kv[:, P:2 * P].rearrange("p (h d) -> p h d", h=2),
                                   ACT.Copy).then_inc(s_vhi, 1)
                if project or (attend and c < 2):
                    buf = jj if c >= 2 else 1 - jj
                    s = (c + 6) % 8
                    act.wait_ge(s_kt, g * 8 + c + 1)
                    act.activation(k_t[:, buf, :, s * P:(s + 1) * P],
                                   ps_kt[:, 0:2 * P].rearrange("p (h n) -> p h n", h=2), ACT.Copy).then_inc(s_kte, 1)

            loop(act, step, boundary)

        @block.gpsimd
        def _(pool):
            pool.sem_inc(s_pv, 2 + 1)
            pool.sem_inc(s_sum, 2)
            pool.sem_inc(s_exp, 1 + 1)
            pool.sem_inc(s_m2, 4)
            for counted in (s_clip, s_elo, t_lo, turned, s_khi, s_kte, s_m0, s_kv, s_vhi):
                pool.sem_inc(counted, 1)

            LAT_STEPS = 6

            def reciprocals(tiles, latent, n_done, n_step):
                k = 0

                def do(out, in0, in1, op, last=False):
                    nonlocal k
                    pool.tensor_tensor(out, in0, in1, op).then_inc(rstd_done if last else rstd_step, 1)
                    if not last:
                        k += 1
                        pool.wait_ge(rstd_step, n_step + k)

                n = tiles.stop - tiles.start
                var = moments[:, tiles, 1]
                a, r, rr = (power[:, part, tiles] for part in range(3))
                eps = pers.eps[:].broadcast_to([P, n])
                minus_half = pers.minus_half[:, 0:1].broadcast_to([P, n])
                pool.wait_ge(stats_done, n_done + 1)
                do(a, var, eps, ALU.add)
                do(rr, a, minus_half, ALU.pow, not latent)
                if latent:
                    do(r, rr, rr, ALU.mult)
                    do(r, r, var, ALU.mult)
                    do(r, r, eps, ALU.add)
                    do(r, r, minus_half, ALU.pow)
                    do(rr, r, rr, ALU.mult, True)

            def fill(t, value):
                n = len(t.shape) - 1
                names = " ".join("abcd"[:n])
                return pool.memset(t if n == 1 else t.rearrange(f"p {names} -> p ({names})"), value)

            for t in (k_nat[:, 0], k_nat[:, 1], v[:, 1]):
                fill(f32(t), 0.0)
            fill(k_rot[:], 0.0)
            fill(r_gate[:], 1.0)
            reciprocals(slice(0, NT), True, 0, 0)
            fill(f32(q_t[:, 1]), 0.0)
            reciprocals(slice(NT, UNITS), False, 1, LAT_STEPS)
            fill(f32(k_t[:, 1]), 0.0)
            fill(f32(v[:, 0, ST // 2:ST]), 0.0)
            fill(f32(e_hi[:, 2]), 0.0)
            fill(f32(e_lo[:, 0]), 0.0)
            fill(e[:, 3], 1.0)
            fill(e_sum[:], 1.0).then_inc(init, 1)
            pool.wait_ge(init, 1)

            def prepare(b, i, jj, g, c):
                n_step = (LAT_STEPS + 1) + (g - jj) // 2 * (LAT_STEPS + 2) + jj * (LAT_STEPS + 1)
                if c == LAT_SLOT + 1 and jj == 0:
                    reciprocals(slice(0, 1), True, units_before(g, jj), n_step)
                if c == CTX_SLOT + 1:
                    reciprocals(slice(NT, NT + 1), False, units_before(g, jj) + (1 - jj), n_step + (1 - jj) * LAT_STEPS)

            def step(g, jj, c, project, attend):
                if project or (attend and c < 2):
                    pool.wait_ge(s_khi, 1 + g * 8 + c)
                    pool.tensor_tensor(k_nat[:, c % 2, :, DH:P], k_rot[:, c % 2], f32(k_nat[:, c % 2, :, 0:DH]),
                                       ALU.subtract).then_inc(s_klo, 1)
                if project or (attend and c == 0):
                    buf = (c + 1) % 2
                    pool.wait_ge(s_rope, g * 8 + c + 1)
                    pool.tensor_tensor(k_rot[:, buf, :, 0:DH // 2], rope_c[:, buf, :, 0:DH // 2],
                                       rope_s[:, buf, :, DH // 2:DH], ALU.subtract)
                    pool.tensor_tensor(k_rot[:, buf, :, DH // 2:DH], rope_c[:, buf, :, DH // 2:DH],
                                       rope_s[:, buf, :, 0:DH // 2], ALU.add).then_inc(s_rot, 1)
                q = (c + 3) % 4
                if q and (attend or c == 0):
                    head = g * 8 + (0 if c == 0 else 4 if c < 5 else 8)
                    pool.wait_ge(s_clip, 1 + g * 8 + c)
                    pool.wait_ge(s_sum, head + q - 1)
                    pool.tensor_tensor(e_sum[:], e[:, 0] if q == 1 else e_sum[:], e[:, q], ALU.add).then_inc(s_sum, 1)
                    if q == 3:
                        pool.wait_ge(s_sum, head + 3)
                        pool.tensor_tensor(e_fold[:, 0 if c == 4 else 1], e_sum[:, 0:N], e_sum[:, N:2 * N], ALU.add
                                           ).then_inc(s_sum, 1)


            loop(pool, step, prepare=prepare)

        @block.vector
        def _(dve):
            half_cols = DH // 2

            def moments_of(sources, first, n_done):
                for t, src in enumerate(sources):
                    st = dve.bn_stats(stats[:, first + t], src)
                st.then_inc(bn_done, 1)
                dve.wait_ge(bn_done, n_done + 1)
                dve.memset(settle[:], 0.0)
                for t in range(len(sources)):
                    st = dve.bn_aggr(moments[:, first + t], stats[:, first + t])
                st.then_inc(stats_done, 1)

            def normalise(sources, places, first, n_done):
                dve.wait_ge(rstd_done, n_done + 1)
                for t, (src, dst) in enumerate(zip(sources, places)):
                    st = dve.tensor_scalar(dst, src, moments[:, first + t, 0:1], power[:, 2, first + t:first + t + 1],
                                           ALU.subtract, ALU.mult)
                st.then_inc(normed, 1)

            latents = [pers.x1[:, t] for t in range(NT)]
            places = [x_nat[:, t] for t in range(UNITS)]
            moments_of(latents, 0, 0)
            dve.wait_ge(x_first, 16)
            moments_of(places[NT:], NT, 1)
            normalise(latents, places[:NT], 0, 0)
            normalise(places[NT:], places[NT:], NT, 1)
            dve.wait_ge(init, 1)
            dve.wait_ge(x1_loaded, 16 * (B - 1))

            def prepare(b, i, jj, g, c):
                if jj == 0:
                    latent = [pers.x1[:, bass.ds((b + 1) % B * NT + i, 1), :].rearrange("p a n -> p (a n)")]
                    if c == LAT_SLOT:
                        moments_of(latent, 0, units_before(g, jj))
                    if c == LAT_SLOT + 3:
                        normalise(latent, [x_nat[:, bass.ds(i, 1), :].rearrange("p a n -> p (a n)")], 0,
                                  units_before(g, jj))
                tile = [x_nat[:, bass.ds(NT + i * 2 + jj, 1), :].rearrange("p a n -> p (a n)")]
                if c == CTX_SLOT:
                    dve.wait_ge(x_loaded[jj], (g - jj) // 2 * 16 + 16)
                    moments_of(tile, NT, units_before(g, jj) + (1 - jj))
                if c == CTX_SLOT + 3:
                    normalise(tile, tile, NT, units_before(g, jj) + (1 - jj))

            def boundary(b):
                def shifted(u):
                    k = 0 if u == 0 else 1
                    dve.wait_ge(turned, 1 + b * 6 + 2 * u + 2)
                    dve.wait_ge(t_lo, 1 + b * 6 + (2 if u == 2 else 0))
                    dve.tensor_scalar(affine[:, u % 2, 1], scores[:, u % 2, N:2 * N], pers.gain[:, k, 1:2],
                                      pers.shift[:, k, 1:2], ALU.mult, ALU.add).then_inc(aff_dve, 1)

                def low(u):
                    dst = (lat_t, ctx_t[:, :, :, 0:N], ctx_t[:, :, :, N:S])[u]
                    for c in range(C2):
                        dve.wait_ge(t_hi, b * 6 + 2 * u + c + 1)
                        dve.tensor_tensor(dst[:, 1, c], affine[:, u % 2, c], f32(dst[:, 0, c]), ALU.subtract
                                          ).then_inc(t_lo, 1)

                shifted(0)
                shifted(1)
                low(0)
                shifted(2)
                low(1)
                low(2)

            def step(g, jj, c, project, attend):
                def add_out(hh, half, n_y):
                    dve.wait_ge(s_y, n_y)
                    for i in range(2):
                        t = 2 * half + i
                        row = x1_row(g - 1 if c == 0 else g, hh, t)
                        last = dve.scalar_tensor_tensor(out=row, in0=ps_y[:, i, :], scalar=r_gate[:, hh, t:t + 1],
                                                        in1=row, op0=ALU.mult, op1=ALU.add)
                    last.then_inc(s_m2, 1)

                if project or (attend and c == 0):
                    buf = (c + 1) % 2
                    tile = (c + 7) % 8
                    vbuf = jj if c else 1 - jj
                    dve.wait_ge(s_vhi, 1 + g * 8 + c)
                    keys = ps_kv[:, 0:P].rearrange("p (a d) -> p a d", d=half_cols)
                    for table, dst in ((pers.cos, rope_c), (pers.sin, rope_s)):
                        last = dve.tensor_tensor(dst[:, buf].rearrange("p h (k d) -> p (h k) d", k=2), keys,
                                                 table[:, tile].unsqueeze(1).broadcast_to([P, 4, half_cols]), ALU.mult)
                    last.then_inc(s_rope, 1)
                    dve.tensor_tensor(v[:, vbuf, tile, :, DH:P], ps_kv[:, P:2 * P].rearrange("p (h d) -> p h d", h=2),
                                      f32(v[:, vbuf, tile, :, 0:DH]), ALU.subtract).then_inc(s_m0, 1)
                if c == 0:
                    add_out(0, 1, g * 4 + 1)
                if c - 1 in OUT and (attend or OUT[c - 1][0] == 1):
                    hh, half = OUT[c - 1]
                    dve.wait_ge(s_gate, g * 2 + (1 if hh else 2))
                    add_out(hh, half, 1 + g * 4 + c - 4)
                if c in DEN_HEAD and (attend or c == 2):
                    hh = DEN_HEAD[c]
                    dve.wait_ge(s_ohi, g * 2 + (1 if c == 2 else 2))
                    dve.tensor_tensor(o_lo[:], ps_o[:], f32(o_hi[:, hh]), ALU.subtract).then_inc(s_olo, 1)
                if c in DEN_HEAD and (attend or c == 2):
                    hh = DEN_HEAD[c]
                    n = g * 2 + (1 if c == 2 else 2)
                    dve.wait_ge(s_den, n)
                    dve.reciprocal(r_den[:, hh], ps_kt[:, DEN:DEN + NT]).then_inc(s_rden, 1)
                    dve.wait_ge(s_rden, n)
                    dve.tensor_scalar(r_gate[:, hh], r_den[:, hh], pers.gates[:, 0:1], None, ALU.mult
                                      ).then_inc(s_gate, 1)
                if attend or c == 0:
                    x4 = (c + 3) % 4
                    dve.wait_ge(s_ehi, g * 8 + c + 1)
                    dve.wait_ge(s_pv, 3 + g * 8 + c)
                    dve.tensor_tensor(e_lo[:, x4 % 2], e[:, x4], f32(e_hi[:, x4]), ALU.subtract).then_inc(s_elo, 1)
                if attend:
                    dve.wait_ge(s_exp, 1 + g * 8 + c + 2)
                    dve.tensor_scalar(e[:, c % 4], e[:, c % 4], EXP_HI, EXP_LO, ALU.min, ALU.max).then_inc(s_clip, 1)
                if project and c - 1 in QUERIES:
                    head = QUERIES[c - 1]
                    dve.wait_ge(s_qhi, g * 2 + head + 1)
                    dve.tensor_tensor(q_t[:, jj, head, 1], ps_y[:].rearrange("p a n -> p (a n)"),
                                      f32(q_t[:, jj, head, 0]), ALU.subtract).then_inc(s_m2, 1)

            def x1_row(g, hh, t):
                batch = ((g + (7 if hh == 0 else 6)) // PAIRS + B - 1) % B
                if isinstance(batch, int):
                    return pers.x1[:, batch * NT + t, :]
                return pers.x1[:, bass.ds(batch * NT + t, 1), :].rearrange("p a n -> p (a n)")

            loop(dve, step, boundary, prepare=prepare)


E_R, E_S = 64, 4
GROUPS_R, PER_G, TOP_G, TOP_K = 8, 8, 4, 8
TG = 2 * N
GT = TG // P
NE = E_R + E_S
ROUTE_SCALE = 2.5
TAKEN = -3.0e38


def ffn(nc, pers, ins, out, gates_dram):
    groups = B * N // TG
    with ExitStack() as ctx:
        def sb(name, shape, dt=F32):
            return ctx.enter_context(nc.sbuf_tensor(name, shape, dt))

        def sem(name):
            return ctx.enter_context(nc.semaphore(name))

        bo = sb("bo", [P, D])
        bias = sb("bias", [P, E_R])
        router = sb("router", [E_R, D])
        router_t = sb("router_t", [P, C2, E_R])
        earlier = sb("earlier", [P, GROUPS_R, GROUPS_R])
        stats = sb("f_stats", [P, GT, 6])
        moments = sb("f_moments", [P, GT, 2])
        rstd = sb("rstd", [P, 2, GT])
        x_nat = sb("f_x_nat", [P, GT, D])
        x_f = sb("x_f", [P, C2, TG])
        x_t = sb("x_t", [P, 2, C2, TG], FR)
        prob = sb("prob", [P, GT, E_R])
        biased = sb("biased", [P, GT, E_R])
        best = sb("best", [P, GT, GROUPS_R, 8])
        g_score = sb("g_score", [P, GT, GROUPS_R])
        cmp_a = sb("cmp_a", [P, GT, GROUPS_R, GROUPS_R])
        cmp_b = sb("cmp_b", [P, GT, GROUPS_R, GROUPS_R])
        g_rank = sb("g_rank", [P, GT, GROUPS_R])
        top8 = sb("top8", [P, GT, 8])
        total = sb("total", [P, GT])
        gate = sb("gate", [P, GT, E_R])
        gate_t = sb("gate_t", [P, GT // 2, P])
        gate_b = sb("gate_b", [P, 2, TG])
        up_raw = sb("up_raw", [P, 2, C2, P])
        dn_raw = sb("dn_raw", [P, 2, D])
        up_w = sb("up_w", [P, 2, 2, C2, P], FR)
        dn_w = sb("dn_w", [P, 2, 2, D], FR)
        act_r = sb("act_r", [P, 2, N])
        act_g = sb("act_g", [P, 2, N])
        g_hi = sb("g_hi", [P, 2, N], FR)
        g_lo = sb("g_lo", [P, 2, N], FR)
        y_t = sb("y_t", [P, C2, TG])
        y_out = sb("y_out", [P, GT, D])
        settle = sb("settle", [P, 1])
        minus_half = sb("f_minus_half", [P, GT])
        ps_h = ctx.enter_context(nc.psum_tensor("ps_h", [P, 2, N], F32))
        ps_c = ctx.enter_context(nc.psum_tensor("ps_c", [P, 2, N], F32))
        ps_acc = ctx.enter_context(nc.psum_tensor("ps_acc", [P, C2, 2, N], F32))

        loaded, made, turned_w = sem("f_loaded"), sem("f_made"), sem("turned_w")
        router_done, gbo_done = sem("router_done"), sem("gbo_done")
        link, prep_link, var_done, rstd_step, rstd_done = sem("link"), sem("prep_link"), sem("var_done"), sem("f_rstd_step"), sem("f_rstd_done")
        x_normed, x_turned, x_copied, x_high, x_low = (sem("x_normed"), sem("x_turned"), sem("x_copied"),
                                                       sem("x_high"), sem("x_low"))
        logits_done, tanh_done, gates_done, gates_turned, gates_t_done = (
            sem("logits_done"), sem("tanh_done"), sem("gates_done"), sem("gates_turned"), sem("gates_t_done"))
        up_loaded = [sem("up_loaded_even"), sem("up_loaded_odd")]
        dn_loaded = [sem("dn_loaded_even"), sem("dn_loaded_odd")]
        gate_loaded = [sem("gate_loaded_even"), sem("gate_loaded_odd")]
        gates_stored = sem("gates_stored")
        up_hi, up_lo, dn_hi, dn_lo = sem("up_hi"), sem("up_lo"), sem("dn_hi"), sem("dn_lo")
        s_up, s_dn, s_relu, s_u, s_g, s_ghi, s_glo = (sem("s_up"), sem("s_dn"), sem("s_relu"), sem("s_u"),
                                                      sem("s_g"), sem("s_ghi"), sem("s_glo"))
        y_copied, y_turned, y_added, out_stored = sem("y_copied"), sem("y_turned"), sem("y_added"), sem("out_stored")

        TAIL = 6

        def experts(eng, visit):
            def run(g, routed=None):
                for x in range(E_S):
                    visit(g, x, None, x)
                if routed:
                    routed(g)
                with eng.Fori(0, (E_R - TAIL) // 2) as i:
                    for par in range(2):
                        visit(g, i * 2 + par + E_S, i * 2 + par, -1 - par)
                for x in range(NE - TAIL, NE):
                    visit(g, x, x - E_S, x)
            return run

        def is_last(static, by=0):
            return static + by >= NE

        block = ctx.enter_context(nc.Block())

        @block.sync
        def _(sp):
            sp.dma_start(bo[:], ins["bo"].partition_broadcast(P)).then_inc(loaded, 16)
            sp.dma_start(bias[:], ins["correction_bias"].partition_broadcast(P)).then_inc(loaded, 16)
            sp.dma_start(router[:], ins["router_w"]).then_inc(loaded, 16)

            def load_up(x, e, par):
                if e is None:
                    src = ins["shared_up_w"][:, x * P:(x + 1) * P]
                else:
                    src = ins["up_w"][bass.ds(e, 1)].rearrange("a c n -> (a c) n")
                sp.dma_start(up_raw[:, par], src.rearrange("(c p) n -> p c n", p=P)).then_inc(up_loaded[par], 16)

            def load_dn(x, e, par):
                if e is None:
                    src = ins["shared_down_w"][x * P:(x + 1) * P, :]
                else:
                    src = ins["down_w"][bass.ds(e, 1)].rearrange("a k n -> (a k) n")
                sp.dma_start(dn_raw[:, par], src).then_inc(dn_loaded[par], 16)

            def load_gates(e, par):
                sp.dma_start(gate_b[:, par], gates_dram[bass.ds(e, 1)].rearrange("a t -> (a t)").partition_broadcast(P)
                             ).then_inc(gate_loaded[par], 16)

            def routed(g):
                sp.wait_ge(gates_t_done, g + 1)
                for odd in range(2):
                    sp.dma_start(gates_dram.rearrange("e (t o n) -> o e t n", o=2, n=P)[odd],
                                 gate_t[odd * E_R:(odd + 1) * E_R]).then_inc(gates_stored, 16)
                sp.wait_ge(gates_stored, g * 32 + 32)
                load_gates(0, 0)

            def visit(g, x, e, static):
                par = x % 2 if isinstance(x, int) else (-1 - static) % 2
                base = g * NE + x
                if not is_last(static, 1) and e is not None:
                    sp.wait_ge(s_u, 1 + g * (2 * E_R) + e * 2)
                    load_gates(e + 1, 1 - par)
                if not is_last(static, 2):
                    sp.wait_ge(up_lo, base + 1)
                    nxt = (x + 2, None) if static in (0, 1) else (None, (e if e is not None else x - E_S) + 2)
                    load_up(*nxt, par)
                if not is_last(static, 1):
                    if static != 0:
                        sp.wait_ge(dn_lo, 1 + base)
                    nxt = (x + 1, None) if static in (0, 1, 2) else (None, (e if e is not None else x - E_S) + 1)
                    load_dn(*nxt, 1 - par)

            load_up(0, None, 0)
            load_up(1, None, 1)
            load_dn(0, None, 0)
            with sp.Fori(0, groups) as g:
                experts(sp, visit)(g, routed)
                sp.wait_ge(dn_lo, 1 + (g + 1) * NE)
                load_up(0, None, 0)
                load_up(1, None, 1)
                load_dn(0, None, 0)
                sp.wait_ge(y_added, 1 + g * (GT // 2) + GT // 2)
                sp.dma_start(out[bass.ds(g * 2, 2)].rearrange("b (t p) c -> p (b t) c", p=P), y_out[:]
                             ).then_inc(out_stored, 16)
            sp.wait_ge(out_stored, 1 + 16 * groups)
            for par in range(2):
                sp.wait_ge(up_loaded[par], 16 * (groups * (NE // 2) + 1))
            sp.wait_ge(dn_loaded[0], 16 * (groups * (NE // 2) + 1))

        @block.gpsimd
        def _(pool):
            for counted in (out_stored, y_added, dn_lo, s_u):
                pool.sem_inc(counted, 1)
            pool.memset(earlier[:], 1.0).then_inc(made, 1)
            pool.wait_ge(made, 1)
            pool.affine_select(out=earlier[:], in_=earlier[:], compare_op=ALU.is_gt, fill=0.0, base=0,
                               pattern=[[1, GROUPS_R], [-1, GROUPS_R]], channel_multiplier=0).then_inc(made, 1)

            def reciprocals(n):
                pool.wait_ge(var_done, n + 1)
                pool.tensor_tensor(rstd[:, 0], moments[:, :, 1], pers.eps[:].broadcast_to([P, GT]), ALU.add
                                   ).then_inc(rstd_step, 1)
                pool.wait_ge(rstd_step, n + 1)
                pool.tensor_tensor(rstd[:, 1], rstd[:, 0], minus_half[:], ALU.pow).then_inc(rstd_done, 1)

            def low(base, n):
                pool.wait_ge(s_ghi, base * 2 + n + 1)
                pool.tensor_tensor(g_lo[:, n], act_g[:, n], f32(g_hi[:, n]), ALU.subtract).then_inc(s_glo, 1)

            def visit(g, x, e, static):
                par = x % 2 if isinstance(x, int) else (-1 - static) % 2
                base = g * NE + x
                if static == NE - TAIL + 2:
                    reciprocals(g + 1)
                if static in range(1, E_S):
                    low(base - 1, 1)
                if not is_last(static, 1):
                    pool.wait_ge(up_hi, base + 2)
                    pool.tensor_tensor(up_w[:, 1 - par, 1], up_raw[:, 1 - par], f32(up_w[:, 1 - par, 0]),
                                       ALU.subtract).then_inc(up_lo, 1)
                pool.wait_ge(dn_hi, base + 1)
                pool.tensor_tensor(dn_w[:, par, 1], dn_raw[:, par], f32(dn_w[:, par, 0]), ALU.subtract
                                   ).then_inc(dn_lo, 1)
                if static in range(E_S):
                    low(base, 0)

            reciprocals(0)
            with pool.Fori(0, groups) as g:
                pool.wait_ge(up_hi, g * NE + 1)
                pool.tensor_tensor(up_w[:, 0, 1], up_raw[:, 0], f32(up_w[:, 0, 0]), ALU.subtract).then_inc(up_lo, 1)
                experts(pool, visit)(g)

        @block.tensor
        def _(pe):
            pe.wait_ge(loaded, 48)
            for c in range(C2):
                mm = pe.transpose(ps_c[:, 0, c * E_R:(c + 1) * E_R], router[:, c * P:(c + 1) * P],
                                  pers.ident[0:E_R, 0:E_R])
            mm.then_inc(turned_w, 1)

            def down(g, base, par, static, n, last):
                pe.wait_ge(s_glo, base * 2 + n + 1)
                if n == 0:
                    pe.wait_ge(dn_lo, 1 + base + 1)
                first = static == 0
                for m in range(C2):
                    for k, (wp, gp) in enumerate(((0, g_hi), (0, g_lo), (1, g_hi))):
                        mm = pe.matmul(ps_acc[:, m, n], dn_w[:, par, wp, m * P:(m + 1) * P], gp[:, n],
                                       start=(first and k == 0), stop=(last and k == 2))
                mm.then_inc(s_dn, 1)

            def visit(g, x, e, static):
                par = x % 2 if isinstance(x, int) else (-1 - static) % 2
                base = g * NE + x
                for n in range(2):
                    if n == 0:
                        pe.wait_ge(up_lo, base + 1)
                    if static != 0:
                        pe.wait_ge(s_relu, base * 2 + n - 1)
                    k = 0
                    for c in range(C2):
                        for wp, xp in ((0, 0), (0, 1), (1, 0)):
                            mm = pe.matmul(ps_h[:, n], up_w[:, par, wp, c], x_t[:, xp, c, n * N:(n + 1) * N],
                                           start=(k == 0), stop=(k == 5))
                            k += 1
                    mm.then_inc(s_up, 1)
                    if static != 0:
                        down(g, base - 1, 1 - par, (static - 1 if static >= 0 else 99), n, False)

            def turn(n):
                pe.wait_ge(x_normed, n + 1)
                for half in range(2):
                    for c in range(C2):
                        for t in range(GT // 2):
                            mm = pe.transpose((ps_h, ps_c)[half][:, c, t * P:(t + 1) * P],
                                              x_nat[:, half * (GT // 2) + t, c * P:(c + 1) * P], pers.ident[:])
                        mm.then_inc(x_turned, 1)

            def logits(n):
                pe.wait_ge(x_copied, n * 4 + 4)
                for t in range(GT):
                    for c in range(C2):
                        mm = pe.matmul(ps_c[:, 0, t * E_R:(t + 1) * E_R], x_f[:, c, t * P:(t + 1) * P],
                                       router_t[:, c], start=(c == 0), stop=(c == C2 - 1))
                mm.then_inc(logits_done, 1)

            def routed(g):
                pe.wait_ge(gates_done, g + 1)
                for t in range(GT // 2):
                    mm = pe.transpose(ps_c[:, 0, t * P:(t + 1) * P],
                                      gate[:, 2 * t:2 * t + 2].rearrange("p t e -> p (t e)"), pers.ident[:])
                mm.then_inc(gates_turned, 1)

            pe.wait_ge(router_done, 1)
            turn(0)
            logits(0)
            with pe.Fori(0, groups) as g:
                pe.wait_ge(x_low, g * 4 + 4)
                pe.wait_ge(y_added, 1 + g * (GT // 2))
                experts(pe, visit)(g, routed)
                for n in range(2):
                    down(g, g * NE + (NE - 1), (NE - 1) % 2, NE - 1, n, True)
                turn(g + 1)
                for t in range(GT):
                    if t % (GT // 2) == 0:
                        pe.wait_ge(y_copied, g * 4 + 2 + 2 * (t // (GT // 2)))
                    bank = ps_acc[:, (t % 4) // 2, t // 4]
                    for c in range(C2):
                        o = ((t % 2) * C2 + c) * P
                        mm = pe.transpose(bank[:, o:o + P], y_t[:, c, t * P:(t + 1) * P], pers.ident[:])
                    mm.then_inc(y_turned, 1)
                logits(g + 1)

        @block.scalar
        def _(act):
            act.wait_ge(turned_w, 1)
            act.activation(router_t[:], ps_c[:, 0, 0:C2 * E_R].rearrange("p (c e) -> p c e", c=C2), ACT.Copy
                           ).then_inc(router_done, 1)

            def high(g, base, n, first):
                act.wait_ge(s_g, base * 2 + n + 1)
                if not first:
                    act.wait_ge(s_dn, base * 2 + n - 1)
                act.activation(g_hi[:, n], act_g[:, n], ACT.Copy).then_inc(s_ghi, 1)

            def visit(g, x, e, static):
                par = x % 2 if isinstance(x, int) else (-1 - static) % 2
                base = g * NE + x
                for n in range(2):
                    act.wait_ge(s_up, base * 2 + n + 1)
                    if static != 0:
                        act.wait_ge(s_g, base * 2 + n - 1)
                    act.activation(act_r[:, n], ps_h[:, n], ACT.Relu).then_inc(s_relu, 1)
                    if n == 1:
                        high(g, base, 0, static == 0)
                    elif static != 0:
                        high(g, base - 1, 1, static == 1)
                    if static in range(E_S):
                        act.wait_ge(s_relu, base * 2 + n + 1)
                        if static != 0:
                            act.wait_ge(s_glo, base * 2 + n - 1)
                        act.activation(act_g[:, n], act_r[:, n], ACT.Square).then_inc(s_g, 1)
                    if n == 0:
                        if not is_last(static, 1):
                            act.wait_ge(up_loaded[1 - par], (g * (NE // 2) + (x + 1 - (1 - par)) // 2) * 16 + 16)
                            if static != 0:
                                act.wait_ge(s_up, base * 2)
                            act.activation(up_w[:, 1 - par, 0], up_raw[:, 1 - par], ACT.Copy).then_inc(up_hi, 1)
                        act.wait_ge(dn_loaded[par], (g * (NE // 2) + (x - par) // 2) * 16 + 16)
                        if static not in (0, 1):
                            act.wait_ge(s_dn, base * 2 - 2)
                        act.activation(dn_w[:, par, 0], dn_raw[:, par], ACT.Copy).then_inc(dn_hi, 1)

            def copies(n):
                for half in range(2):
                    for c in range(C2):
                        act.wait_ge(x_turned, n * 4 + 2 * half + c + 1)
                        act.activation(x_f[:, c, half * N:(half + 1) * N], (ps_h, ps_c)[half][:, c], ACT.Copy
                                       ).then_inc(x_copied, 1)

            def highs(n):
                for half in range(2):
                    for c in range(C2):
                        act.wait_ge(x_copied, n * 4 + 2 * half + c + 1)
                        act.activation(x_t[:, 0, c, half * N:(half + 1) * N], x_f[:, c, half * N:(half + 1) * N],
                                       ACT.Copy).then_inc(x_high, 1)

            def routed(g):
                act.wait_ge(gates_turned, g + 1)
                act.activation(gate_t[:].rearrange("p t n -> p (t n)"), ps_c[:, 0], ACT.Copy).then_inc(gates_t_done, 1)

            copies(0)
            highs(0)
            with act.Fori(0, groups) as g:
                act.wait_ge(up_loaded[0], g * (16 * NE // 2) + 16)
                act.activation(up_w[:, 0, 0], up_raw[:, 0], ACT.Copy).then_inc(up_hi, 1)
                act.wait_ge(logits_done, g + 1)
                act.activation(prob[:].rearrange("p t e -> p (t e)"), ps_c[:, 0], ACT.Tanh, scale=0.5
                               ).then_inc(tanh_done, 1)
                experts(act, visit)(g, routed)
                high(g, g * NE + (NE - 1), 1, False)
                for n in range(2):
                    act.wait_ge(s_dn, g * (2 * NE) + 2 * NE - 1 + n)
                    for c in range(C2):
                        act.activation(y_t[:, c, n * N:(n + 1) * N], ps_acc[:, c, n], ACT.Copy,
                                       scale=pers.gates[:, 1:2]).then_inc(y_copied, 1)
                copies(g + 1)
                highs(g + 1)

        @block.vector
        def _(dve):
            dve.wait_ge(loaded, 48)
            dve.wait_ge(made, 2)
            dve.memset(minus_half[:], -0.5).then_inc(gbo_done, 1)
            dve.tensor_scalar(bo[:], bo[:], pers.gates[:, 0:1], None, ALU.mult).then_inc(gbo_done, 1)
            dve.wait_ge(gbo_done, 2)

            def low(base, n):
                dve.wait_ge(s_ghi, base * 2 + n + 1)
                dve.tensor_tensor(g_lo[:, n], act_g[:, n], f32(g_hi[:, n]), ALU.subtract).then_inc(s_glo, 1)

            def visit(g, x, e, static):
                base = g * NE + x
                par = x % 2 if isinstance(x, int) else (-1 - static) % 2
                if e is None:
                    return
                if static >= NE - TAIL:
                    statistics(g + 1, static - (NE - TAIL))
                for n in range(2):
                    dve.wait_ge(s_relu, base * 2 + n + 1)
                    dve.wait_ge(s_glo, base * 2 + n - 1)
                    if n == 0:
                        dve.wait_ge(gate_loaded[par], (g * (E_R // 2) + (e - par) // 2) * 16 + 16)
                    dve.tensor_tensor(act_g[:, n], act_r[:, n], gate_b[:, par, n * N:(n + 1) * N], ALU.mult
                                      ).then_inc(s_u, 1)
                    low(*((base - 1, 1), (base, 0))[n])
                    dve.wait_ge(s_u, g * (2 * E_R) + e * 2 + n + 2)
                    dve.tensor_tensor(act_g[:, n], act_g[:, n], act_r[:, n], ALU.mult).then_inc(s_g, 1)

            LINKS = 18

            def settled():
                dve.memset(settle[:], 0.0)

            def statistics(n, part):
                x1g = pers.x1[:, bass.ds(n % groups * GT, GT), :]
                if part == 0:
                    dve.tensor_tensor(x1g, x1g, bo[:].unsqueeze(1).broadcast_to([P, GT, D]), ALU.add
                                      ).then_inc(prep_link, 1)
                elif part == 1:
                    dve.wait_ge(prep_link, n * 2 + 1)
                    settled()
                    for t in range(GT):
                        st = dve.bn_stats(stats[:, t], x1g[:, t])
                    st.then_inc(prep_link, 1)
                elif part == 2:
                    dve.wait_ge(prep_link, n * 2 + 2)
                    settled()
                    for t in range(GT):
                        st = dve.bn_aggr(moments[:, t], stats[:, t])
                    st.then_inc(var_done, 1)
                else:
                    if part == 3:
                        dve.wait_ge(rstd_done, n + 1)
                    for t in ((0, 1, 2), (3, 4, 5), (6, 7))[part - 3]:
                        st = dve.tensor_scalar(x_nat[:, t], x1g[:, t], moments[:, t, 0:1], rstd[:, 1, t:t + 1],
                                               ALU.subtract, ALU.mult)
                    if part == 5:
                        st.then_inc(x_normed, 1)

            def lows(n):
                for half in range(2):
                    for c in range(C2):
                        dve.wait_ge(x_high, n * 4 + 2 * half + c + 1)
                        dve.tensor_tensor(x_t[:, 1, c, half * N:(half + 1) * N], x_f[:, c, half * N:(half + 1) * N],
                                          f32(x_t[:, 0, c, half * N:(half + 1) * N]), ALU.subtract).then_inc(x_low, 1)

            for part in range(TAIL):
                statistics(0, part)
            with dve.Fori(0, groups) as g:
                k = 0

                def done(instruction):
                    nonlocal k
                    k += 1
                    instruction.then_inc(link, 1)
                    dve.wait_ge(link, g * LINKS + k)

                x1g = pers.x1[:, bass.ds(g * GT, GT), :]
                lows(g)
                dve.wait_ge(tanh_done, g + 1)
                done(dve.tensor_scalar(prob[:], prob[:], 0.5, 0.5, ALU.mult, ALU.add))
                done(dve.tensor_tensor(biased[:], prob[:], bias[:].unsqueeze(1).broadcast_to([P, GT, E_R]), ALU.add))
                settled()
                for t in range(GT):
                    for gr in range(GROUPS_R):
                        st = dve.max(best[:, t, gr], biased[:, t, gr * PER_G:(gr + 1) * PER_G])
                done(st)
                done(dve.tensor_tensor(g_score[:], best[:, :, :, 0], best[:, :, :, 1], ALU.add))
                for t in range(GT):
                    other = g_score[:, t].unsqueeze(1).broadcast_to([P, GROUPS_R, GROUPS_R])
                    own = g_score[:, t].unsqueeze(2).broadcast_to([P, GROUPS_R, GROUPS_R])
                    dve.tensor_tensor(cmp_a[:, t], other, own, ALU.is_gt)
                    st = dve.tensor_tensor(cmp_b[:, t], other, own, ALU.is_equal)
                done(st)
                done(dve.tensor_tensor(cmp_b[:].rearrange("p t i j -> p t (i j)"), cmp_b[:].rearrange("p t i j -> p t (i j)"),
                                       earlier[:].rearrange("p i j -> p (i j)").unsqueeze(1).broadcast_to(
                                           [P, GT, GROUPS_R * GROUPS_R]), ALU.mult))
                done(dve.tensor_tensor(cmp_a[:], cmp_a[:], cmp_b[:], ALU.add))
                done(dve.tensor_reduce(g_rank[:], cmp_a[:], mybir.AxisListType.X, ALU.add))
                done(dve.tensor_scalar(g_rank[:], g_rank[:], float(TOP_G), None, ALU.is_lt))
                done(dve.tensor_tensor(biased[:].rearrange("p t (i j) -> p (t i) j", j=PER_G),
                                       biased[:].rearrange("p t (i j) -> p (t i) j", j=PER_G),
                                       g_rank[:].rearrange("p t i -> p (t i)").unsqueeze(2).broadcast_to(
                                           [P, GT * GROUPS_R, PER_G]), ALU.mult))
                settled()
                for t in range(GT):
                    st = dve.max(top8[:, t], biased[:, t])
                done(st)
                settled()
                for t in range(GT):
                    st = dve.match_replace(out=gate[:, t], in_to_replace=top8[:, t], in_values=biased[:, t],
                                           imm_value=TAKEN)
                done(st)
                done(dve.tensor_scalar(gate[:], gate[:], TAKEN, None, ALU.is_equal))
                done(dve.tensor_tensor(gate[:], gate[:], prob[:], ALU.mult))
                done(dve.tensor_reduce(total[:], gate[:], mybir.AxisListType.X, ALU.add))
                done(dve.tensor_scalar(total[:], total[:], 1e-20, None, ALU.add))
                done(dve.reciprocal(total[:], total[:]))
                done(dve.tensor_scalar(total[:], total[:], ROUTE_SCALE, None, ALU.mult))
                dve.tensor_tensor(gate[:], gate[:], total[:].unsqueeze(2).broadcast_to([P, GT, E_R]), ALU.mult
                                  ).then_inc(gates_done, 1)
                assert k == LINKS, k
                experts(dve, visit)(g)
                low(g * NE + (NE - 1), 1)
                for t in range(0, GT, 2):
                    dve.wait_ge(y_turned, g * GT + t + 2)
                    if t == 0:
                        dve.wait_ge(out_stored, 1 + g * 16)
                    dve.tensor_tensor(y_out[:, t:t + 2], ps_acc[:, (t % 4) // 2, t // 4].rearrange(
                        "p (t n) -> p t n", t=2), x1g[:, t:t + 2], ALU.add).then_inc(y_added, 1)



INS = {"x": "x", "ctx_1024": "ctx", "g_xattn": "g_xattn", "g_ffn": "g_ffn", "L0_xattn_cos": "cos", "L0_xattn_sin": "sin",
       "L0_xattn_ln_lat_g": "ln_lat_g", "L0_xattn_ln_lat_b": "ln_lat_b", "L0_xattn_ln_ctx_g": "ln_ctx_g",
       "L0_xattn_ln_ctx_b": "ln_ctx_b", "L0_xattn_Wq": "Wq", "L0_xattn_Wkv": "Wkv", "L0_xattn_Wo": "Wo",
       "L0_xattn_bo": "bo", "L0_ffn_router_w": "router_w", "L0_ffn_correction_bias": "correction_bias",
       "L0_ffn_up_w": "up_w", "L0_ffn_down_w": "down_w", "L0_ffn_shared_up_w": "shared_up_w",
       "L0_ffn_shared_down_w": "shared_down_w"}


def program(nc, ins, out):
    w_dram = nc.dram_tensor("w_pairs", [PAIRS, P, 2 * C2 * 4 * P], F32, kind="Internal").ap()
    wo_dram = nc.dram_tensor("wo_heads", [PAIRS, DH, 2, 2, D], F32, kind="Internal").ap()
    gates_dram = nc.dram_tensor("gates_by_expert", [E_R, TG], F32, kind="Internal").ap()
    with ExitStack() as ctx:
        pers = Persistent(nc, ctx)
        setup(nc, pers, ins, w_dram, wo_dram)
        attention(nc, pers, ins, w_dram, wo_dram)
        ffn(nc, pers, ins, out, gates_dram)


def kernel(**inputs):
    import numpy as _np
    import concourse.bacc as _bacc
    from concourse.bass_utils import run_bass_kernel_spmd as _run

    nc = _bacc.Bacc("TRN2", target_bir_lowering=False, num_devices=1)
    arrays, ins = {}, {}
    for name, short in INS.items():
        a = _np.ascontiguousarray(inputs[name])
        arrays[f"in_{name}"] = a
        ins[short] = nc.dram_tensor(f"in_{name}", a.shape, mybir.dt.from_np(a.dtype), kind="ExternalInput").ap()
    out = nc.dram_tensor("out_0", (B, N, D), F32, kind="ExternalOutput").ap()
    program(nc, ins, out)
    r = _run(nc, [arrays], core_ids=[0])
    return r.results[0]["out_0"]
```

```python
from contextlib import ExitStack

import concourse.bass as bass
from concourse import mybir

ALU = mybir.AluOpType
ACT = mybir.ActivationFunctionType
F32 = mybir.dt.float32
FR = mybir.dt.float32r

P = 128
B, N, S, D = 8, 512, 1024, 256
H, DH = 16, 64
PAIRS = H // 2
NT = N // P
ST = S // P
C2 = D // P
EPS = 1e-5
CH = 2 * N
EXP_LO = 1.670170079024566e-05
EXP_HI = 59874.14171519782
SCALE = DH ** -0.5


def f32(ap):
    return ap.bitcast(F32)


class Persistent:

    def __init__(self, nc, ctx):
        def sb(name, shape, dt=F32):
            return ctx.enter_context(nc.sbuf_tensor(name, shape, dt))

        self.ident = sb("ident", [P, P])
        self.x1 = sb("x1", [P, B * NT, D])
        self.cos = sb("cos", [P, ST, DH // 2])
        self.sin = sb("sin", [P, ST, DH // 2])
        self.gain = sb("gain", [P, 2, C2])
        self.shift = sb("shift", [P, 2, C2])
        self.gates = sb("gates", [P, 2])
        self.minus_half = sb("minus_half", [P, NT])
        self.ones = sb("ones", [P, 1])
        self.eps = sb("eps", [P, 1])
        self.settle = sb("settle_d", [P, 1])
        self.x_nat = sb("x_nat", [P, NT + ST, D])
        self.stats = sb("stats", [P, NT + ST, 6])
        self.moments = sb("moments", [P, NT + ST, 2])
        self.power = sb("power", [P, 3, NT + ST])


class Norms:
    LAT_STEPS = 6

    def __init__(self, nc, pers, sem, name):
        self.nc, self.pers = nc, pers
        self.bn_done, self.stats_done = sem(name + "bn_done"), sem(name + "stats_done")
        self.rstd_step, self.rstd_done, self.normed = (sem(name + "rstd_step"), sem(name + "rstd_done"),
                                                       sem(name + "normed"))

    def moments_of(self, dve, sources, first, n_done):
        pers = self.pers
        for t, src in enumerate(sources):
            st = dve.bn_stats(pers.stats[:, first + t], src)
        st.then_inc(self.bn_done, 1)
        dve.wait_ge(self.bn_done, n_done + 1)
        dve.memset(pers.settle[:], 0.0)
        for t in range(len(sources)):
            st = dve.bn_aggr(pers.moments[:, first + t], pers.stats[:, first + t])
        st.then_inc(self.stats_done, 1)

    def normalise(self, dve, sources, places, first, n_done):
        pers = self.pers
        dve.wait_ge(self.rstd_done, n_done + 1)
        for t, (src, dst) in enumerate(zip(sources, places)):
            st = dve.tensor_scalar(dst, src, pers.moments[:, first + t, 0:1],
                                   pers.power[:, 2, first + t:first + t + 1], ALU.subtract, ALU.mult)
        st.then_inc(self.normed, 1)

    def reciprocals(self, pool, tiles, latent, n_done, n_step):
        pers = self.pers
        k = 0

        def do(out, in0, in1, op, last=False):
            nonlocal k
            pool.tensor_tensor(out, in0, in1, op).then_inc(self.rstd_done if last else self.rstd_step, 1)
            if not last:
                k += 1
                pool.wait_ge(self.rstd_step, n_step + k)

        n = tiles.stop - tiles.start
        var = pers.moments[:, tiles, 1]
        a, r, rr = (pers.power[:, part, tiles] for part in range(3))
        eps = pers.eps[:].broadcast_to([P, n])
        minus_half = pers.minus_half[:, 0:1].broadcast_to([P, n])
        pool.wait_ge(self.stats_done, n_done + 1)
        do(a, var, eps, ALU.add)
        do(rr, a, minus_half, ALU.pow, not latent)
        if latent:
            do(r, rr, rr, ALU.mult)
            do(r, r, var, ALU.mult)
            do(r, r, eps, ALU.add)
            do(r, r, minus_half, ALU.pow)
            do(rr, r, rr, ALU.mult, True)


def setup(nc, pers, ins, w_dram, wo_dram):
    with ExitStack() as ctx:
        def sb(name, shape, dt=F32):
            return ctx.enter_context(nc.sbuf_tensor(name, shape, dt))

        def sem(name):
            return ctx.enter_context(nc.semaphore(name))

        raw = sb("w_raw", [P, C2, 3, PAIRS, P])
        split = sb("w_split", [P, PAIRS, 2, C2, 3, P], FR)
        wo_raw = sb("wo_raw", [DH, H, D])
        wo_split = sb("wo_split", [DH, H, 2, D], FR)
        gates_in = sb("gates_in", [P, 2])
        wq_loaded, wo_loaded, x_loaded = sem("wq_loaded"), sem("wo_loaded"), sem("x_loaded_first")
        gates_done, w_hi, lo_done, stored = sem("tanh_of_gates"), sem("w_hi"), sem("lo_done"), sem("stored")
        wo_hi_done, wo_lo_done, wo_stored = sem("wo_hi_done"), sem("wo_lo_done"), sem("wo_stored")
        zeroed, selected = sem("zeroed"), sem("selected")
        norms, rows_loaded = Norms(nc, pers, sem, "first_"), sem("rows_loaded")

        def parts(part, pair, c):
            return split[:, pair, part, c], raw[:, c, :, pair]

        block = ctx.enter_context(nc.Block())

        @block.sync
        def _(sp):
            for c in range(C2):
                sp.dma_start(raw[:, c, 0], ins["Wq"][c * P:(c + 1) * P, :].rearrange("p (g m) -> p g m", m=P)
                             ).then_inc(wq_loaded, 16)
                sp.dma_start(raw[:, c, 1:3], ins["Wkv"][c * P:(c + 1) * P, :].rearrange(
                    "p (t g m) -> p t g m", t=2, m=P)).then_inc(wq_loaded, 16)
            sp.dma_start(wo_raw[:], ins["Wo"].rearrange("(h d) n -> d h n", d=DH)).then_inc(wo_loaded, 16)
            sp.dma_start(pers.x1[:, 0:NT, :], ins["x"][0].rearrange("(t p) c -> p t c", p=P)).then_inc(x_loaded, 16)
            sp.dma_start(pers.x_nat[:, NT:NT + ST], ins["ctx"][0].rearrange("(t p) c -> p t c", p=P)
                         ).then_inc(rows_loaded, 16)
            for pair in range(PAIRS):
                sp.wait_ge(lo_done, pair + 1)
                sp.dma_start(w_dram[pair], f32(split[:, pair]).rearrange("p a c t m -> p (a c t m)")
                             ).then_inc(stored, 16)
            sp.wait_ge(wo_lo_done, 1)
            for hh in range(2):
                last = PAIRS - 1 - hh
                heads = f32(wo_split[:]).rearrange("d (j h) k n -> d j h k n", h=2)[:, :, hh]
                sp.dma_start(wo_dram[hh + 1:PAIRS, :, hh].rearrange("j d k n -> d j k n"), heads[:, 0:last]
                             ).then_inc(wo_stored, 16)
                sp.dma_start(wo_dram[0:hh + 1, :, hh].rearrange("j d k n -> d j k n"), heads[:, last:PAIRS]
                             ).then_inc(wo_stored, 16)
            sp.wait_ge(stored, 16 * PAIRS)
            sp.wait_ge(wo_stored, 16 * 4)
            sp.wait_ge(x_loaded, 16)

        @block.scalar
        def _(act):
            loads = sem("small_loads")
            act.dma_start(pers.cos[:], ins["cos"].rearrange("(t p) d -> p t d", p=P)).then_inc(loads, 16)
            act.dma_start(pers.sin[:], ins["sin"].rearrange("(t p) d -> p t d", p=P)).then_inc(loads, 16)
            for k, who in enumerate(("lat", "ctx")):
                for c in range(C2):
                    act.dma_start(pers.gain[:, k, c:c + 1], ins[f"ln_{who}_g"][c * P:(c + 1) * P].unsqueeze(1)
                                  ).then_inc(loads, 16)
                    act.dma_start(pers.shift[:, k, c:c + 1], ins[f"ln_{who}_b"][c * P:(c + 1) * P].unsqueeze(1)
                                  ).then_inc(loads, 16)
            act.dma_start(gates_in[:, 0:1], ins["g_xattn"].partition_broadcast(P)).then_inc(loads, 16)
            act.dma_start(gates_in[:, 1:2], ins["g_ffn"].partition_broadcast(P)).then_inc(loads, 16)
            act.wait_ge(wq_loaded, 16 * 4)
            for pair in range(PAIRS):
                for c in range(C2):
                    act.activation(*parts(0, pair, c), ACT.Copy).then_inc(w_hi, 1)
            act.wait_ge(wo_loaded, 16)
            act.activation(wo_split[:, :, 0], wo_raw[:], ACT.Copy).then_inc(wo_hi_done, 1)
            act.wait_ge(loads, 16 * 12)
            act.activation(pers.gates[:], gates_in[:], ACT.Tanh).then_inc(gates_done, 1)

        @block.gpsimd
        def _(pool):
            pool.memset(pers.ident[:], 0.0).then_inc(zeroed, 1)
            pool.memset(pers.minus_half[:], -0.5)
            pool.memset(pers.eps[:], EPS)
            pool.memset(pers.ones[:], 1.0).then_inc(zeroed, 1)
            pool.wait_ge(zeroed, 2)
            pool.affine_select(out=pers.ident[:], in_=pers.ident[:], compare_op=ALU.not_equal, fill=1.0,
                               base=0, pattern=[[-1, P]], channel_multiplier=1).then_inc(selected, 1)
            pool.wait_ge(selected, 1)
            norms.reciprocals(pool, slice(0, NT), True, 0, 0)
            norms.reciprocals(pool, slice(NT, NT + ST), False, 1, norms.LAT_STEPS)

        @block.vector
        def _(dve):
            for pair in range(PAIRS):
                dve.wait_ge(w_hi, C2 * (pair + 1))
                for c in range(C2):
                    last = dve.tensor_tensor(*parts(1, pair, c), f32(parts(0, pair, c)[0]), ALU.subtract)
                last.then_inc(lo_done, 1)
            dve.wait_ge(wo_hi_done, 1)
            dve.tensor_tensor(wo_split[:, :, 1], wo_raw[:], f32(wo_split[:, :, 0]), ALU.subtract
                              ).then_inc(wo_lo_done, 1)
            latents = [pers.x1[:, t] for t in range(NT)]
            places = [pers.x_nat[:, t] for t in range(NT + ST)]
            dve.wait_ge(x_loaded, 16)
            norms.moments_of(dve, latents, 0, 0)
            dve.wait_ge(rows_loaded, 16)
            norms.moments_of(dve, places[NT:], NT, 1)
            norms.normalise(dve, latents, places[:NT], 0, 0)
            norms.normalise(dve, places[NT:], places[NT:], NT, 1)


def attention(nc, pers, ins, w_dram, wo_dram):
    with ExitStack() as ctx:
        def sb(name, shape, dt=F32):
            return ctx.enter_context(nc.sbuf_tensor(name, shape, dt))

        def sem(name):
            return ctx.enter_context(nc.semaphore(name))

        affine = sb("affine", [P, 2, C2, N])
        ctx_t = sb("ctx_t", [P, 2, C2, S], FR)
        lat_t = sb("lat_t", [P, 2, C2, N], FR)
        w = sb("w", [P, 2, 2, C2, 3, P], FR)
        q_s = sb("q_s", [P, 2, N], FR)
        wo = sb("wo", [P, 2, 2, D], FR)
        k_t = sb("k_t", [P, 2, 2, S], FR)
        v = sb("v", [P, 2, ST, 2, P], FR)
        q_t = sb("q_t", [P, 2, 2, 2, N], FR)
        rope_c = sb("rope_c", [P, 2, 2, DH])
        rope_s = sb("rope_s", [P, 2, 2, DH])
        k_rot = sb("k_rot", [P, 2, 2, DH])
        k_nat = sb("k_nat", [P, 2, 2, P], FR)
        e = sb("e", [P, 4, CH])
        e_hi = sb("e_hi", [P, 4, CH], FR)
        e_lo = sb("e_lo", [P, 2, CH], FR)
        e_sum = sb("e_sum", [P, CH])
        e_fold = sb("e_fold", [P, 2, N])
        o_hi = sb("o_hi", [P, 2, N], FR)
        o_lo = sb("o_lo", [P, N], FR)
        x_nat = pers.x_nat
        r_den = sb("r_den", [P, 2, NT])
        r_gate = sb("r_gate", [P, 2, NT])
        scores = ctx.enter_context(nc.psum_tensor("scores", [P, 2, CH], F32))
        ps_o = ctx.enter_context(nc.psum_tensor("ps_o", [P, N], F32))
        ps_kv = ctx.enter_context(nc.psum_tensor("ps_kv", [P, N], F32))
        ps_kt = ctx.enter_context(nc.psum_tensor("ps_kt", [P, N], F32))
        ps_y = ctx.enter_context(nc.psum_tensor("ps_y", [P, 2, D], F32))
        DEN = 256

        init = sem("init")
        norms = Norms(nc, pers, sem, "next_")
        x1_loaded, x_loaded = sem("x1_loaded"), (sem("x_loaded_even"), sem("x_loaded_odd"))
        turned = sem("turned")
        aff_act, aff_dve, t_hi, t_lo = sem("aff_act"), sem("aff_dve"), sem("t_hi"), sem("t_lo")
        w_loaded, wo_loaded = (sem("w_loaded_even"), sem("w_loaded_odd")), sem("wo_loaded")
        s_scores, s_exp, s_clip, s_ehi, s_elo, s_sum = (sem("s_scores"), sem("s_exp"), sem("s_clip"),
                                                         sem("s_ehi"), sem("s_elo"), sem("s_sum"))
        s_pv, s_ohi, s_olo = sem("s_pv"), sem("s_ohi"), sem("s_olo")
        s_kv, s_m0, s_vhi = sem("s_kv"), sem("s_m0"), sem("s_vhi")
        s_rope, s_rot, s_khi, s_klo, s_kt, s_kte = (sem("s_rope"), sem("s_rot"), sem("s_khi"), sem("s_klo"),
                                                    sem("s_kt"), sem("s_kte"))
        q_loaded = sem("q_loaded")
        s_q, s_qhi, s_den, s_y, s_m2 = sem("s_q"), sem("s_qhi"), sem("s_den"), sem("s_y"), sem("s_m2")
        s_rden, s_gate = sem("s_rden"), sem("s_gate")

        DEN_HEAD = {2: 1, 6: 0}
        QUERIES = 0
        OUT = {2: (1, 0), 4: (1, 1), 6: (0, 0), 7: (0, 1)}
        USES = sorted(OUT)
        SUM_FREE = [1, 1, 2, 3]

        LAT_SLOT, CTX_SLOT = 0, 4
        UNITS = NT + ST

        def units_before(g, jj):
            return (g - jj) // 2 * 3 + 2 * jj

        def loop(eng, step, boundary=None, per_iteration=None, prepare=None):
            with eng.Fori(0, B) as b:
                if boundary:
                    boundary(b)
                with eng.Fori(0, PAIRS // 2) as i:
                    for jj in range(2):
                        g = b * PAIRS + i * 2 + jj
                        if per_iteration:
                            per_iteration(b, g, i * 2 + jj, jj)
                        for c in range(8):
                            step(g, jj, c, True, True)
                            if prepare:
                                prepare(b, i, jj, g, c)
            g = B * PAIRS
            if per_iteration:
                per_iteration(None, g, 0, 0)
            for c in range(8):
                step(g, 0, c, False, True)
            for c in range(7):
                step(g + 1, 1, c, False, False)

        block = ctx.enter_context(nc.Block())

        @block.sync
        def _(sp):
            sp.dma_start(f32(w[:, 0]).rearrange("p a c t m -> p (a c t m)"), w_dram[0]).then_inc(w_loaded[0], 16)
            for b in range(1, B):
                sp.dma_start(pers.x1[:, b * NT:(b + 1) * NT, :],
                             ins["x"][b].rearrange("(t p) c -> p t c", p=P)).then_inc(x1_loaded, 16)

            def load_wo(j):
                src = wo_dram[j] if isinstance(j, int) else wo_dram[bass.ds(j, 1)].rearrange("a d h k n -> (a d) h k n")
                for half in range(2):
                    sp.dma_start(f32(wo[half * DH:(half + 1) * DH]), src).then_inc(wo_loaded, 16)

            def per_iteration(b, g, j, jj):
                if not (isinstance(g, int)):
                    sp.wait_ge(s_kv, 1 + g * 8)
                    sp.dma_start(f32(w[:, 1 - jj]).rearrange("p a c t m -> p (a c t m)"),
                                 w_dram[bass.ds((j + 1) % PAIRS, 1)].rearrange("a p n -> (a p) n")
                                 ).then_inc(w_loaded[1 - jj], 16)
                sp.wait_ge(s_y, 1 + g * 4)
                load_wo(j)

                if b is not None:
                    sp.wait_ge(turned, 1 + b * 6 + 6)
                    sp.dma_start(x_nat[:, bass.ds(NT + j, 1), :].rearrange("p a c -> p (a c)"),
                                 ins["ctx"][bass.ds((b + 1) % B, 1), bass.ds(j * P, P), :].rearrange("a p c -> (a p) c")
                                 ).then_inc(x_loaded[jj], 16)
                    sp.wait_ge(s_m2, g * 5 + 3)
                    for head in range(2):
                        for half in range(2):
                            sp.dma_start(f32(q_t[half * DH:(half + 1) * DH, jj, head]),
                                         f32(q_s[head * DH:(head + 1) * DH])).then_inc(q_loaded, 16)

            loop(sp, lambda *a: None, per_iteration=per_iteration)
            g = B * PAIRS + 1
            sp.wait_ge(s_y, 1 + 4 * g)
            load_wo(1)
            sp.wait_ge(w_loaded[0], 16 * (B * PAIRS // 2 + 1))
            sp.wait_ge(w_loaded[1], 16 * (B * PAIRS // 2))
            sp.wait_ge(wo_loaded, 32 * (B * PAIRS + 2))
            sp.wait_ge(q_loaded, 1 + 64 * B * PAIRS)
            sp.wait_ge(x_loaded[0], 16 * (B * PAIRS // 2))
            sp.wait_ge(x_loaded[1], 16 * (B * PAIRS // 2))

        @block.tensor
        def _(pe):
            pe.wait_ge(init, 2)
            pe.matmul(ps_kv[:], v[:, 1, 0, 0, :], q_t[:, 1, 0, 0, :], start=True, stop=True)
            pe.matmul(ps_o[:], v[:, 1, 0, 0, :], q_t[:, 1, 0, 0, :], start=True, stop=False)
            pe.matmul(ps_y[:].rearrange("p a n -> p (a n)"), v[:, 1, 0, 0, :], q_t[:, 1, 0, 0, :], start=True, stop=True
                      ).then_inc(s_y, 1)

            def boundary(b):
                pe.wait_ge(norms.normed, 1 + b * UNITS)
                pe.wait_ge(s_exp, 2 + b * (8 * PAIRS))
                for u in range(3):
                    if u == 2:
                        pe.wait_ge(aff_act, b * 3 + 1)
                        pe.wait_ge(aff_dve, b * 3 + 1)
                    for c in range(C2):
                        for t in range(NT):
                            mm = pe.transpose(scores[:, u % 2, c * N + t * P:c * N + (t + 1) * P],
                                              x_nat[:, u * NT + t, c * P:(c + 1) * P], pers.ident[:])
                        mm.then_inc(turned, 1)

            def step(g, jj, c, project, attend):
                att = 1 - jj
                q4 = c % 4
                if c == 0 and project and jj == 0:
                    pe.wait_ge(aff_act, g // PAIRS * 3 + 3)
                    pe.wait_ge(aff_dve, g // PAIRS * 3 + 3)
                if attend:
                    pe.wait_ge(s_exp, 1 + g * 8 + c)
                    if c == 0:
                        pe.wait_ge(q_loaded, 1 + g * 64)
                        pe.wait_ge(s_kte, 1 + g * 8)
                    if c == 3:
                        pe.wait_ge(s_kte, 1 + g * 8 + 2)
                    for r in range(2):
                        s = 2 * q4 + r
                        for part in range(2):
                            mm = pe.matmul(scores[:, c % 2, r * N:(r + 1) * N],
                                           k_t[:, att, c // 4, s * P:(s + 1) * P],
                                           q_t[:, att, c // 4, part, :], start=(part == 0), stop=(part == 1))
                    mm.then_inc(s_scores, 1)
                turn = project or (attend and c < 2)
                if c in DEN_HEAD and (attend or c == 2):
                    hh = DEN_HEAD[c]
                    pe.wait_ge(s_kte, 1 + (g * 8 + c if project else B * PAIRS * 8 + 2))
                    if not project:
                        pe.wait_ge(s_rden, g * 2 + (0 if c == 2 else 1))
                    pe.wait_ge(s_sum, g * 8 + (4 if c == 2 else 8))
                    for t in range(NT):
                        mm = pe.matmul(ps_kt[:, DEN + t:DEN + t + 1], e_fold[:, hh, t * P:(t + 1) * P],
                                       pers.ones[:], start=True, stop=True)
                    mm.then_inc(s_den, 1)
                if c == 0 and project:
                    pe.wait_ge(t_lo, 1 + g // PAIRS * 6 + 6)
                    pe.wait_ge(w_loaded[jj], (g - jj) // 2 * 16 + 16)
                if project:
                    pe.wait_ge(s_m0, 1 + g * 8 + c + 1)
                    k = 0
                    for cc in range(C2):
                        for a, bb in ((0, 0), (0, 1), (1, 0)):
                            mm = pe.matmul(ps_kv[:, 0:2 * P], ctx_t[:, a, cc, c * P:(c + 1) * P],
                                           w[:, jj, bb, cc, 1:3].rearrange("p t m -> p (t m)"),
                                           start=(k == 0), stop=(k == 5))
                            k += 1
                    mm.then_inc(s_kv, 1)
                if project and c == QUERIES:
                    pe.wait_ge(s_m2, g * 5 + 2)
                    k = 0
                    for cc in range(C2):
                        for a, bb in ((0, 0), (0, 1), (1, 0)):
                            mm = pe.matmul(ps_y[:].rearrange("p a n -> p (a n)"), w[:, jj, bb, cc, 0],
                                           lat_t[:, a, cc, :], start=(k == 0), stop=(k == 5))
                            k += 1
                    mm.then_inc(s_q, 1)
                if turn:
                    pe.wait_ge(s_kte, 1 + g * 8 + c)
                    if c in DEN_HEAD:
                        pe.wait_ge(s_rden, g * 2 + (1 if c == 2 else 2))
                    pe.wait_ge(s_klo, g * 8 + c + 1)
                    for hh in range(2):
                        mm = pe.transpose(ps_kt[:, hh * P:(hh + 1) * P], f32(k_nat[:, c % 2, hh]), pers.ident[:])
                    mm.then_inc(s_kt, 1)

                def project_out(hh, half, use):
                    pe.wait_ge(s_m2, use)
                    pe.wait_ge(s_olo, g * 2 + (1 if hh else 2))
                    pe.wait_ge(wo_loaded, g * 32 + 32)
                    for i in range(2):
                        t = 2 * half + i
                        for k, (o_part, wpart) in enumerate(((o_hi[:, hh], 0), (o_hi[:, hh], 1), (o_lo[:], 0))):
                            mm = pe.matmul(ps_y[:, i, :], o_part[:, t * P:(t + 1) * P], wo[:, hh, wpart, :],
                                           start=(k == 0), stop=(k == 2))
                    mm.then_inc(s_y, 1)

                if attend or c < 2:
                    x4 = (c + 2) % 4
                    hh = ((c + 6) % 8) // 4
                    buf = att if c >= 2 else 1 - att
                    pe.wait_ge(s_elo, 1 + g * 8 + c)
                    if c in (2, 6):
                        pe.wait_ge(s_olo, g * 2 + (1 if c == 2 else 2))
                    for r in range(2):
                        s = 2 * x4 + r
                        for part, e_part in enumerate((e_hi, e_lo)):
                            place = x4 % (4 if part == 0 else 2)
                            mm = pe.matmul(ps_o[:], v[:, buf, s, hh, :], e_part[:, place, r * N:(r + 1) * N],
                                           start=(x4 == 0 and r == 0 and part == 0),
                                           stop=(x4 == 3 and r == 1 and part == 1))
                    mm.then_inc(s_pv, 1)
                if c in OUT and (attend or OUT[c][0] == 1):
                    hh, half = OUT[c]
                    before_it = g * 5 + 2 if project else B * PAIRS * 5 + 1 + (0 if attend else 4)
                    project_out(hh, half, 1 + before_it + USES.index(c))

            loop(pe, step, boundary)

        @block.scalar
        def _(act):
            act.wait_ge(init, 2)

            def boundary(b):
                for u in range(3):
                    dst = (lat_t[:, 0], ctx_t[:, 0, :, 0:N], ctx_t[:, 0, :, N:S])[u]
                    k = 0 if u == 0 else 1
                    act.wait_ge(turned, 1 + b * 6 + 2 * u + 1)
                    act.wait_ge(t_lo, 1 + b * 6 + (2 if u == 2 else 0))
                    act.activation(affine[:, u % 2, 0], scores[:, u % 2, 0:N], ACT.Identity,
                                   bias=pers.shift[:, k, 0:1], scale=pers.gain[:, k, 0:1]).then_inc(aff_act, 1)
                    for c, done in enumerate((aff_act, aff_dve)):
                        act.wait_ge(done, b * 3 + u + 1)
                        act.activation(dst[:, c], affine[:, u % 2, c], ACT.Copy).then_inc(t_hi, 1)

            def step(g, jj, c, project, attend):
                if c in DEN_HEAD and (attend or c == 2):
                    hh = DEN_HEAD[c]
                    act.wait_ge(s_pv, 1 + g * 8 + c + 2)
                    act.activation(o_hi[:, hh], ps_o[:], ACT.Copy).then_inc(s_ohi, 1)
                if attend or c == 0:
                    act.wait_ge(s_clip, 1 + g * 8 + c)
                    act.wait_ge(s_pv, 1 + g * 8 + c)
                    act.activation(e_hi[:, (c + 3) % 4], e[:, (c + 3) % 4], ACT.Copy).then_inc(s_ehi, 1)
                if attend:
                    act.wait_ge(s_scores, g * 8 + c + 1)
                    act.wait_ge(s_sum, g * 8 + 4 * (c // 4) + SUM_FREE[c % 4])
                    act.activation(e[:, c % 4], scores[:, c % 2], ACT.Exp, scale=SCALE).then_inc(s_exp, 1)
                if project and c == QUERIES + 1:
                    act.wait_ge(s_q, g + 1)
                    act.activation(q_s[:, 0], ps_y[:].rearrange("p a n -> p (a n)"), ACT.Copy
                                   ).then_inc(s_qhi, 1)
                if project or (attend and c == 0):
                    act.wait_ge(s_rot, g * 8 + c + 1)
                    act.activation(k_nat[:, (c + 1) % 2, :, 0:DH], k_rot[:, (c + 1) % 2], ACT.Copy
                                   ).then_inc(s_khi, 1)
                if project:
                    act.wait_ge(s_kv, 1 + g * 8 + c + 1)
                    act.activation(v[:, jj, c, :, 0:DH], ps_kv[:, P:2 * P].rearrange("p (h d) -> p h d", h=2),
                                   ACT.Copy).then_inc(s_vhi, 1)
                if project or (attend and c < 2):
                    buf = jj if c >= 2 else 1 - jj
                    s = (c + 6) % 8
                    act.wait_ge(s_kt, g * 8 + c + 1)
                    act.activation(k_t[:, buf, :, s * P:(s + 1) * P],
                                   ps_kt[:, 0:2 * P].rearrange("p (h n) -> p h n", h=2), ACT.Copy).then_inc(s_kte, 1)

            loop(act, step, boundary)

        @block.gpsimd
        def _(pool):
            pool.sem_inc(s_pv, 2 + 1)
            pool.sem_inc(s_sum, 2)
            pool.sem_inc(s_exp, 1 + 1)
            pool.sem_inc(s_m2, 1)
            pool.sem_inc(q_loaded, 1)
            for counted in (s_clip, s_elo, t_lo, turned, norms.normed, s_khi, s_kte, s_m0, s_kv, s_vhi):
                pool.sem_inc(counted, 1)

            def fill(t, value):
                n = len(t.shape) - 1
                names = " ".join("abcd"[:n])
                return pool.memset(t if n == 1 else t.rearrange(f"p {names} -> p ({names})"), value)

            for t in (k_nat[:, 0], k_nat[:, 1], v[:, 1]):
                fill(f32(t), 0.0)
            fill(k_rot[:], 0.0)
            fill(r_gate[:], 1.0)
            fill(f32(q_t[:, 1]), 0.0)
            fill(f32(e_hi[:, 2]), 0.0)
            fill(f32(e_lo[:, 0]), 0.0)
            fill(e_sum[:], 1.0).then_inc(init, 1)
            pool.wait_ge(init, 2)

            def prepare(b, i, jj, g, c):
                n_step = (g - jj) // 2 * (norms.LAT_STEPS + 2) + jj * (norms.LAT_STEPS + 1)
                if c == LAT_SLOT + 1 and jj == 0:
                    norms.reciprocals(pool, slice(0, 1), True, units_before(g, jj), n_step)
                if c == CTX_SLOT + 1:
                    norms.reciprocals(pool, slice(NT, NT + 1), False, units_before(g, jj) + (1 - jj),
                                      n_step + (1 - jj) * norms.LAT_STEPS)

            def step(g, jj, c, project, attend):
                if project or (attend and c < 2):
                    pool.wait_ge(s_khi, 1 + g * 8 + c)
                    pool.tensor_tensor(k_nat[:, c % 2, :, DH:P], k_rot[:, c % 2], f32(k_nat[:, c % 2, :, 0:DH]),
                                       ALU.subtract).then_inc(s_klo, 1)
                if project or (attend and c == 0):
                    buf = (c + 1) % 2
                    pool.wait_ge(s_rope, g * 8 + c + 1)
                    pool.tensor_tensor(k_rot[:, buf, :, 0:DH // 2], rope_c[:, buf, :, 0:DH // 2],
                                       rope_s[:, buf, :, DH // 2:DH], ALU.subtract)
                    pool.tensor_tensor(k_rot[:, buf, :, DH // 2:DH], rope_c[:, buf, :, DH // 2:DH],
                                       rope_s[:, buf, :, 0:DH // 2], ALU.add).then_inc(s_rot, 1)
                q = (c + 3) % 4
                if q and (attend or c == 0):
                    head = g * 8 + (0 if c == 0 else 4 if c < 5 else 8)
                    pool.wait_ge(s_clip, 1 + g * 8 + c)
                    pool.wait_ge(s_sum, head + q - 1)
                    pool.tensor_tensor(e_sum[:], e[:, 0] if q == 1 else e_sum[:], e[:, q], ALU.add).then_inc(s_sum, 1)
                    if q == 3:
                        pool.wait_ge(s_sum, head + 3)
                        pool.tensor_tensor(e_fold[:, 0 if c == 4 else 1], e_sum[:, 0:N], e_sum[:, N:2 * N], ALU.add
                                           ).then_inc(s_sum, 1)


            loop(pool, step, prepare=prepare)

        @block.vector
        def _(dve):
            half_cols = DH // 2

            dve.memset(f32(k_t[:, 1]).rearrange("p h n -> p (h n)"), 0.0)
            dve.memset(f32(v[:, 0, ST // 2:ST]).rearrange("p t h n -> p (t h n)"), 0.0)
            dve.memset(e[:, 3], 1.0).then_inc(init, 1)
            dve.wait_ge(init, 2)
            dve.wait_ge(x1_loaded, 16 * (B - 1))

            def prepare(b, i, jj, g, c):
                if jj == 0:
                    latent = [pers.x1[:, bass.ds((b + 1) % B * NT + i, 1), :].rearrange("p a n -> p (a n)")]
                    if c == LAT_SLOT:
                        norms.moments_of(dve, latent, 0, units_before(g, jj))
                    if c == LAT_SLOT + 3:
                        norms.normalise(dve, latent, [x_nat[:, bass.ds(i, 1), :].rearrange("p a n -> p (a n)")], 0,
                                  units_before(g, jj))
                tile = [x_nat[:, bass.ds(NT + i * 2 + jj, 1), :].rearrange("p a n -> p (a n)")]
                if c == CTX_SLOT:
                    dve.wait_ge(x_loaded[jj], (g - jj) // 2 * 16 + 16)
                    norms.moments_of(dve, tile, NT, units_before(g, jj) + (1 - jj))
                if c == CTX_SLOT + 3:
                    norms.normalise(dve, tile, tile, NT, units_before(g, jj) + (1 - jj))

            def boundary(b):
                def shifted(u):
                    k = 0 if u == 0 else 1
                    dve.wait_ge(turned, 1 + b * 6 + 2 * u + 2)
                    dve.wait_ge(t_lo, 1 + b * 6 + (2 if u == 2 else 0))
                    dve.tensor_scalar(affine[:, u % 2, 1], scores[:, u % 2, N:2 * N], pers.gain[:, k, 1:2],
                                      pers.shift[:, k, 1:2], ALU.mult, ALU.add).then_inc(aff_dve, 1)

                def low(u):
                    dst = (lat_t, ctx_t[:, :, :, 0:N], ctx_t[:, :, :, N:S])[u]
                    for c in range(C2):
                        dve.wait_ge(t_hi, b * 6 + 2 * u + c + 1)
                        dve.tensor_tensor(dst[:, 1, c], affine[:, u % 2, c], f32(dst[:, 0, c]), ALU.subtract
                                          ).then_inc(t_lo, 1)

                shifted(0)
                shifted(1)
                low(0)
                shifted(2)
                low(1)
                low(2)

            def step(g, jj, c, project, attend):
                def add_out(hh, half, n_y):
                    dve.wait_ge(s_y, n_y)
                    for i in range(2):
                        t = 2 * half + i
                        row = x1_row(g - 1 if c == 0 else g, hh, t)
                        last = dve.scalar_tensor_tensor(out=row, in0=ps_y[:, i, :], scalar=r_gate[:, hh, t:t + 1],
                                                        in1=row, op0=ALU.mult, op1=ALU.add)
                    last.then_inc(s_m2, 1)

                if project or (attend and c == 0):
                    buf = (c + 1) % 2
                    tile = (c + 7) % 8
                    vbuf = jj if c else 1 - jj
                    dve.wait_ge(s_vhi, 1 + g * 8 + c)
                    keys = ps_kv[:, 0:P].rearrange("p (a d) -> p a d", d=half_cols)
                    for table, dst in ((pers.cos, rope_c), (pers.sin, rope_s)):
                        last = dve.tensor_tensor(dst[:, buf].rearrange("p h (k d) -> p (h k) d", k=2), keys,
                                                 table[:, tile].unsqueeze(1).broadcast_to([P, 4, half_cols]), ALU.mult)
                    last.then_inc(s_rope, 1)
                    dve.tensor_tensor(v[:, vbuf, tile, :, DH:P], ps_kv[:, P:2 * P].rearrange("p (h d) -> p h d", h=2),
                                      f32(v[:, vbuf, tile, :, 0:DH]), ALU.subtract).then_inc(s_m0, 1)
                if c == 0:
                    add_out(0, 1, g * 4 + 1)
                if c - 1 in OUT and (attend or OUT[c - 1][0] == 1):
                    hh, half = OUT[c - 1]
                    dve.wait_ge(s_gate, g * 2 + (1 if hh else 2))
                    add_out(hh, half, 1 + g * 4 + USES.index(c - 1) + 1)
                if c in DEN_HEAD and (attend or c == 2):
                    hh = DEN_HEAD[c]
                    dve.wait_ge(s_ohi, g * 2 + (1 if c == 2 else 2))
                    dve.tensor_tensor(o_lo[:], ps_o[:], f32(o_hi[:, hh]), ALU.subtract).then_inc(s_olo, 1)
                if c in DEN_HEAD and (attend or c == 2):
                    hh = DEN_HEAD[c]
                    n = g * 2 + (1 if c == 2 else 2)
                    dve.wait_ge(s_den, n)
                    dve.reciprocal(r_den[:, hh], ps_kt[:, DEN:DEN + NT]).then_inc(s_rden, 1)
                    dve.wait_ge(s_rden, n)
                    dve.tensor_scalar(r_gate[:, hh], r_den[:, hh], pers.gates[:, 0:1], None, ALU.mult
                                      ).then_inc(s_gate, 1)
                if attend or c == 0:
                    x4 = (c + 3) % 4
                    dve.wait_ge(s_ehi, g * 8 + c + 1)
                    dve.wait_ge(s_pv, 3 + g * 8 + c)
                    dve.tensor_tensor(e_lo[:, x4 % 2], e[:, x4], f32(e_hi[:, x4]), ALU.subtract).then_inc(s_elo, 1)
                if attend:
                    dve.wait_ge(s_exp, 1 + g * 8 + c + 2)
                    dve.tensor_scalar(e[:, c % 4], e[:, c % 4], EXP_HI, EXP_LO, ALU.min, ALU.max).then_inc(s_clip, 1)
                if project and c == QUERIES + 1:
                    dve.wait_ge(s_qhi, g + 1)
                    dve.tensor_tensor(q_s[:, 1], ps_y[:].rearrange("p a n -> p (a n)"), f32(q_s[:, 0]), ALU.subtract
                                      ).then_inc(s_m2, 1)

            def x1_row(g, hh, t):
                batch = ((g + (7 if hh == 0 else 6)) // PAIRS + B - 1) % B
                if isinstance(batch, int):
                    return pers.x1[:, batch * NT + t, :]
                return pers.x1[:, bass.ds(batch * NT + t, 1), :].rearrange("p a n -> p (a n)")

            loop(dve, step, boundary, prepare=prepare)


E_R, E_S = 64, 4
GROUPS_R, PER_G, TOP_G, TOP_K = 8, 8, 4, 8
TG = 2 * N
GT = TG // P
NE = E_R + E_S
ROUTE_SCALE = 2.5
TAKEN = -3.0e38


def ffn(nc, pers, ins, out, gates_dram):
    groups = B * N // TG
    with ExitStack() as ctx:
        def sb(name, shape, dt=F32):
            return ctx.enter_context(nc.sbuf_tensor(name, shape, dt))

        def sem(name):
            return ctx.enter_context(nc.semaphore(name))

        bo = sb("bo", [P, D])
        bias = sb("bias", [P, E_R])
        router = sb("router", [E_R, D])
        router_t = sb("router_t", [P, C2, E_R])
        earlier = sb("earlier", [P, GROUPS_R, GROUPS_R])
        stats = sb("f_stats", [P, GT, 6])
        moments = sb("f_moments", [P, GT, 2])
        rstd = sb("rstd", [P, 2, GT])
        x_nat = sb("f_x_nat", [P, GT, D])
        x_f = sb("x_f", [P, C2, TG])
        x_t = sb("x_t", [P, 2, C2, TG], FR)
        prob = sb("prob", [P, GT, E_R])
        biased = sb("biased", [P, GT, E_R])
        best = sb("best", [P, GT, GROUPS_R, 8])
        g_score = sb("g_score", [P, GT, GROUPS_R])
        cmp_a = sb("cmp_a", [P, GT, GROUPS_R, GROUPS_R])
        cmp_b = sb("cmp_b", [P, GT, GROUPS_R, GROUPS_R])
        g_rank = sb("g_rank", [P, GT, GROUPS_R])
        top8 = sb("top8", [P, GT, 8])
        total = sb("total", [P, GT])
        gate = sb("gate", [P, GT, E_R])
        gate_t = sb("gate_t", [P, GT // 2, P])
        gate_b = sb("gate_b", [P, 2, TG])
        up_raw = sb("up_raw", [P, 2, C2, P])
        dn_raw = sb("dn_raw", [P, 2, D])
        up_w = sb("up_w", [P, 2, 2, C2, P], FR)
        dn_w = sb("dn_w", [P, 2, 2, D], FR)
        act_r = sb("act_r", [P, 2, N])
        act_g = sb("act_g", [P, 2, N])
        g_hi = sb("g_hi", [P, 2, N], FR)
        g_lo = sb("g_lo", [P, 2, N], FR)
        y_t = sb("y_t", [P, C2, TG])
        y_out = sb("y_out", [P, GT, D])
        settle = sb("settle", [P, 1])
        minus_half = sb("f_minus_half", [P, GT])
        ps_h = ctx.enter_context(nc.psum_tensor("ps_h", [P, 2, N], F32))
        ps_c = ctx.enter_context(nc.psum_tensor("ps_c", [P, 2, N], F32))
        ps_acc = ctx.enter_context(nc.psum_tensor("ps_acc", [P, C2, 2, N], F32))

        loaded, made, turned_w = sem("f_loaded"), sem("f_made"), sem("turned_w")
        router_done, gbo_done = sem("router_done"), sem("gbo_done")
        link, prep_link, var_done = sem("link"), sem("prep_link"), sem("var_done")
        rstd_step, rstd_done = sem("f_rstd_step"), sem("f_rstd_done")
        x_normed, x_turned, x_copied, x_high, x_low = (sem("x_normed"), sem("x_turned"), sem("x_copied"),
                                                       sem("x_high"), sem("x_low"))
        logits_done, tanh_done, gates_done, gates_turned, gates_t_done = (
            sem("logits_done"), sem("tanh_done"), sem("gates_done"), sem("gates_turned"), sem("gates_t_done"))
        up_loaded = [sem("up_loaded_even"), sem("up_loaded_odd")]
        dn_loaded = [sem("dn_loaded_even"), sem("dn_loaded_odd")]
        gate_loaded = [sem("gate_loaded_even"), sem("gate_loaded_odd")]
        gates_stored = sem("gates_stored")
        up_hi, up_lo, dn_hi, dn_lo = sem("up_hi"), sem("up_lo"), sem("dn_hi"), sem("dn_lo")
        s_up, s_dn, s_relu, s_u, s_g, s_ghi, s_glo = (sem("s_up"), sem("s_dn"), sem("s_relu"), sem("s_u"),
                                                      sem("s_g"), sem("s_ghi"), sem("s_glo"))
        y_copied, y_turned, y_added, out_stored = sem("y_copied"), sem("y_turned"), sem("y_added"), sem("out_stored")

        TAIL = 8

        def experts(eng, visit):
            def run(g, routed=None):
                for x in range(E_S):
                    if routed and x == E_S - 1:
                        routed(g)
                    visit(g, x, None, x)
                with eng.Fori(0, (E_R - TAIL) // 2) as i:
                    for par in range(2):
                        visit(g, i * 2 + par + E_S, i * 2 + par, -1 - par)
                for x in range(NE - TAIL, NE):
                    visit(g, x, x - E_S, x)
            return run

        def is_last(static, by=0):
            return static + by >= NE

        block = ctx.enter_context(nc.Block())

        @block.sync
        def _(sp):
            sp.dma_start(bo[:], ins["bo"].partition_broadcast(P)).then_inc(loaded, 16)
            sp.dma_start(bias[:], ins["correction_bias"].partition_broadcast(P)).then_inc(loaded, 16)
            sp.dma_start(router[:], ins["router_w"]).then_inc(loaded, 16)

            def load_up(x, e, par):
                if e is None:
                    src = ins["shared_up_w"][:, x * P:(x + 1) * P]
                else:
                    src = ins["up_w"][bass.ds(e, 1)].rearrange("a c n -> (a c) n")
                sp.dma_start(up_raw[:, par], src.rearrange("(c p) n -> p c n", p=P)).then_inc(up_loaded[par], 16)

            def load_dn(x, e, par):
                if e is None:
                    src = ins["shared_down_w"][x * P:(x + 1) * P, :]
                else:
                    src = ins["down_w"][bass.ds(e, 1)].rearrange("a k n -> (a k) n")
                sp.dma_start(dn_raw[:, par], src).then_inc(dn_loaded[par], 16)

            def load_gates(e, par):
                sp.dma_start(gate_b[:, par], gates_dram[bass.ds(e, 1)].rearrange("a t -> (a t)").partition_broadcast(P)
                             ).then_inc(gate_loaded[par], 16)

            def routed(g):
                sp.wait_ge(gates_t_done, g + 1)
                for odd in range(2):
                    sp.dma_start(gates_dram.rearrange("e (t o n) -> o e t n", o=2, n=P)[odd],
                                 gate_t[odd * E_R:(odd + 1) * E_R]).then_inc(gates_stored, 16)
                sp.wait_ge(gates_stored, g * 32 + 32)
                load_gates(0, 0)

            def visit(g, x, e, static):
                par = x % 2 if isinstance(x, int) else (-1 - static) % 2
                base = g * NE + x
                if not is_last(static, 1) and e is not None:
                    sp.wait_ge(s_u, 1 + g * (2 * E_R) + e * 2)
                    load_gates(e + 1, 1 - par)
                if not is_last(static, 2):
                    sp.wait_ge(up_lo, base + 1)
                    nxt = (x + 2, None) if static in (0, 1) else (None, (e if e is not None else x - E_S) + 2)
                    load_up(*nxt, par)
                if not is_last(static, 1):
                    if static != 0:
                        sp.wait_ge(dn_lo, 1 + base)
                    nxt = (x + 1, None) if static in (0, 1, 2) else (None, (e if e is not None else x - E_S) + 1)
                    load_dn(*nxt, 1 - par)

            load_up(0, None, 0)
            load_up(1, None, 1)
            load_dn(0, None, 0)
            with sp.Fori(0, groups) as g:
                experts(sp, visit)(g, routed)
                sp.wait_ge(dn_lo, 1 + (g + 1) * NE)
                load_up(0, None, 0)
                load_up(1, None, 1)
                load_dn(0, None, 0)
                sp.wait_ge(y_added, 1 + g * (GT // 2) + GT // 2)
                sp.dma_start(out[bass.ds(g * 2, 2)].rearrange("b (t p) c -> p (b t) c", p=P), y_out[:]
                             ).then_inc(out_stored, 16)
            sp.wait_ge(out_stored, 1 + 16 * groups)
            for par in range(2):
                sp.wait_ge(up_loaded[par], 16 * (groups * (NE // 2) + 1))
            sp.wait_ge(dn_loaded[0], 16 * (groups * (NE // 2) + 1))

        @block.gpsimd
        def _(pool):
            for counted in (out_stored, y_added, dn_lo, s_u):
                pool.sem_inc(counted, 1)
            pool.memset(earlier[:], 1.0).then_inc(made, 1)
            pool.wait_ge(made, 1)
            pool.affine_select(out=earlier[:], in_=earlier[:], compare_op=ALU.is_gt, fill=0.0, base=0,
                               pattern=[[1, GROUPS_R], [-1, GROUPS_R]], channel_multiplier=0).then_inc(made, 1)

            def reciprocals(n):
                pool.wait_ge(var_done, n + 1)
                pool.tensor_tensor(rstd[:, 0], moments[:, :, 1], pers.eps[:].broadcast_to([P, GT]), ALU.add
                                   ).then_inc(rstd_step, 1)
                pool.wait_ge(rstd_step, n + 1)
                pool.tensor_tensor(rstd[:, 1], rstd[:, 0], minus_half[:], ALU.pow).then_inc(rstd_done, 1)

            def low(base, n):
                pool.wait_ge(s_ghi, base * 2 + n + 1)
                pool.tensor_tensor(g_lo[:, n], act_g[:, n], f32(g_hi[:, n]), ALU.subtract).then_inc(s_glo, 1)

            def visit(g, x, e, static):
                par = x % 2 if isinstance(x, int) else (-1 - static) % 2
                base = g * NE + x
                if static == NE - TAIL + 4:
                    reciprocals(g + 1)
                if static in range(1, E_S):
                    low(base - 1, 1)
                if not is_last(static, 1):
                    pool.wait_ge(up_hi, base + 2)
                    pool.tensor_tensor(up_w[:, 1 - par, 1], up_raw[:, 1 - par], f32(up_w[:, 1 - par, 0]),
                                       ALU.subtract).then_inc(up_lo, 1)
                pool.wait_ge(dn_hi, base + 1)
                pool.tensor_tensor(dn_w[:, par, 1], dn_raw[:, par], f32(dn_w[:, par, 0]), ALU.subtract
                                   ).then_inc(dn_lo, 1)
                if static in range(E_S):
                    low(base, 0)

            reciprocals(0)
            with pool.Fori(0, groups) as g:
                pool.wait_ge(up_hi, g * NE + 1)
                pool.tensor_tensor(up_w[:, 0, 1], up_raw[:, 0], f32(up_w[:, 0, 0]), ALU.subtract).then_inc(up_lo, 1)
                experts(pool, visit)(g)

        @block.tensor
        def _(pe):
            pe.wait_ge(loaded, 48)
            for c in range(C2):
                mm = pe.transpose(ps_c[:, 0, c * E_R:(c + 1) * E_R], router[:, c * P:(c + 1) * P],
                                  pers.ident[0:E_R, 0:E_R])
            mm.then_inc(turned_w, 1)

            def down(g, base, par, static, n, last):
                pe.wait_ge(s_glo, base * 2 + n + 1)
                if n == 0:
                    pe.wait_ge(dn_lo, 1 + base + 1)
                first = static == 0
                for m in range(C2):
                    for k, (wp, gp) in enumerate(((0, g_hi), (0, g_lo), (1, g_hi))):
                        mm = pe.matmul(ps_acc[:, m, n], dn_w[:, par, wp, m * P:(m + 1) * P], gp[:, n],
                                       start=(first and k == 0), stop=(last and k == 2))
                mm.then_inc(s_dn, 1)

            def visit(g, x, e, static):
                par = x % 2 if isinstance(x, int) else (-1 - static) % 2
                base = g * NE + x
                for n in range(2):
                    if n == 0:
                        pe.wait_ge(up_lo, base + 1)
                    if static != 0:
                        pe.wait_ge(s_relu, base * 2 + n - 1)
                    k = 0
                    for c in range(C2):
                        for wp, xp in ((0, 0), (0, 1), (1, 0)):
                            mm = pe.matmul(ps_h[:, n], up_w[:, par, wp, c], x_t[:, xp, c, n * N:(n + 1) * N],
                                           start=(k == 0), stop=(k == 5))
                            k += 1
                    mm.then_inc(s_up, 1)
                    if static != 0:
                        down(g, base - 1, 1 - par, (static - 1 if static >= 0 else 99), n, False)

            def turn(n):
                pe.wait_ge(x_normed, n + 1)
                for half in range(2):
                    for c in range(C2):
                        for t in range(GT // 2):
                            mm = pe.transpose((ps_h, ps_c)[half][:, c, t * P:(t + 1) * P],
                                              x_nat[:, half * (GT // 2) + t, c * P:(c + 1) * P], pers.ident[:])
                        mm.then_inc(x_turned, 1)

            def logits(n):
                pe.wait_ge(x_copied, n * 4 + 4)
                for t in range(GT):
                    for c in range(C2):
                        mm = pe.matmul(ps_c[:, 0, t * E_R:(t + 1) * E_R], x_f[:, c, t * P:(t + 1) * P],
                                       router_t[:, c], start=(c == 0), stop=(c == C2 - 1))
                mm.then_inc(logits_done, 1)

            def routed(g):
                pe.wait_ge(gates_done, g + 1)
                for t in range(GT // 2):
                    mm = pe.transpose(ps_c[:, 0, t * P:(t + 1) * P],
                                      gate[:, 2 * t:2 * t + 2].rearrange("p t e -> p (t e)"), pers.ident[:])
                mm.then_inc(gates_turned, 1)

            pe.wait_ge(router_done, 1)
            turn(0)
            logits(0)
            with pe.Fori(0, groups) as g:
                pe.wait_ge(x_low, g * 4 + 4)
                pe.wait_ge(y_added, 1 + g * (GT // 2))
                experts(pe, visit)(g, routed)
                for n in range(2):
                    down(g, g * NE + (NE - 1), (NE - 1) % 2, NE - 1, n, True)
                turn(g + 1)
                for t in range(GT):
                    if t % (GT // 2) == 0:
                        pe.wait_ge(y_copied, g * 4 + 2 + 2 * (t // (GT // 2)))
                    bank = ps_acc[:, (t % 4) // 2, t // 4]
                    for c in range(C2):
                        o = ((t % 2) * C2 + c) * P
                        mm = pe.transpose(bank[:, o:o + P], y_t[:, c, t * P:(t + 1) * P], pers.ident[:])
                    mm.then_inc(y_turned, 1)
                logits(g + 1)

        @block.scalar
        def _(act):
            act.wait_ge(turned_w, 1)
            act.activation(router_t[:], ps_c[:, 0, 0:C2 * E_R].rearrange("p (c e) -> p c e", c=C2), ACT.Copy
                           ).then_inc(router_done, 1)

            def high(g, base, n, first):
                act.wait_ge(s_g, base * 2 + n + 1)
                if not first:
                    act.wait_ge(s_dn, base * 2 + n - 1)
                act.activation(g_hi[:, n], act_g[:, n], ACT.Copy).then_inc(s_ghi, 1)

            def visit(g, x, e, static):
                par = x % 2 if isinstance(x, int) else (-1 - static) % 2
                base = g * NE + x
                for n in range(2):
                    act.wait_ge(s_up, base * 2 + n + 1)
                    if static != 0:
                        act.wait_ge(s_g, base * 2 + n - 1)
                    act.activation(act_r[:, n], ps_h[:, n], ACT.Relu).then_inc(s_relu, 1)
                    if n == 1:
                        high(g, base, 0, static == 0)
                    elif static != 0:
                        high(g, base - 1, 1, static == 1)
                    if static in range(E_S):
                        act.wait_ge(s_relu, base * 2 + n + 1)
                        if static != 0:
                            act.wait_ge(s_glo, base * 2 + n - 1)
                        act.activation(act_g[:, n], act_r[:, n], ACT.Square).then_inc(s_g, 1)
                    if n == 0:
                        if not is_last(static, 1):
                            act.wait_ge(up_loaded[1 - par], (g * (NE // 2) + (x + 1 - (1 - par)) // 2) * 16 + 16)
                            if static != 0:
                                act.wait_ge(s_up, base * 2)
                            act.activation(up_w[:, 1 - par, 0], up_raw[:, 1 - par], ACT.Copy).then_inc(up_hi, 1)
                        act.wait_ge(dn_loaded[par], (g * (NE // 2) + (x - par) // 2) * 16 + 16)
                        if static not in (0, 1):
                            act.wait_ge(s_dn, base * 2 - 2)
                        act.activation(dn_w[:, par, 0], dn_raw[:, par], ACT.Copy).then_inc(dn_hi, 1)

            def copies(n):
                for half in range(2):
                    for c in range(C2):
                        act.wait_ge(x_turned, n * 4 + 2 * half + c + 1)
                        act.activation(x_f[:, c, half * N:(half + 1) * N], (ps_h, ps_c)[half][:, c], ACT.Copy
                                       ).then_inc(x_copied, 1)

            def highs(n):
                for half in range(2):
                    for c in range(C2):
                        act.wait_ge(x_copied, n * 4 + 2 * half + c + 1)
                        act.activation(x_t[:, 0, c, half * N:(half + 1) * N], x_f[:, c, half * N:(half + 1) * N],
                                       ACT.Copy).then_inc(x_high, 1)

            def routed(g):
                act.wait_ge(gates_turned, g + 1)
                act.activation(gate_t[:].rearrange("p t n -> p (t n)"), ps_c[:, 0], ACT.Copy).then_inc(gates_t_done, 1)

            copies(0)
            highs(0)
            with act.Fori(0, groups) as g:
                act.wait_ge(up_loaded[0], g * (16 * NE // 2) + 16)
                act.activation(up_w[:, 0, 0], up_raw[:, 0], ACT.Copy).then_inc(up_hi, 1)
                act.wait_ge(logits_done, g + 1)
                act.activation(prob[:].rearrange("p t e -> p (t e)"), ps_c[:, 0], ACT.Tanh, scale=0.5
                               ).then_inc(tanh_done, 1)
                experts(act, visit)(g, routed)
                high(g, g * NE + (NE - 1), 1, False)
                for n in range(2):
                    act.wait_ge(s_dn, g * (2 * NE) + 2 * NE - 1 + n)
                    for c in range(C2):
                        act.activation(y_t[:, c, n * N:(n + 1) * N], ps_acc[:, c, n], ACT.Copy,
                                       scale=pers.gates[:, 1:2]).then_inc(y_copied, 1)
                copies(g + 1)
                highs(g + 1)

        @block.vector
        def _(dve):
            dve.wait_ge(loaded, 48)
            dve.wait_ge(made, 2)
            dve.memset(minus_half[:], -0.5).then_inc(gbo_done, 1)
            dve.tensor_scalar(bo[:], bo[:], pers.gates[:, 0:1], None, ALU.mult).then_inc(gbo_done, 1)
            dve.wait_ge(gbo_done, 2)

            def low(base, n):
                dve.wait_ge(s_ghi, base * 2 + n + 1)
                dve.tensor_tensor(g_lo[:, n], act_g[:, n], f32(g_hi[:, n]), ALU.subtract).then_inc(s_glo, 1)

            def visit(g, x, e, static):
                base = g * NE + x
                par = x % 2 if isinstance(x, int) else (-1 - static) % 2
                if e is None:
                    return
                if static >= NE - TAIL:
                    statistics(g + 1, static - (NE - TAIL))
                for n in range(2):
                    dve.wait_ge(s_relu, base * 2 + n + 1)
                    dve.wait_ge(s_glo, base * 2 + n - 1)
                    if n == 0:
                        dve.wait_ge(gate_loaded[par], (g * (E_R // 2) + (e - par) // 2) * 16 + 16)
                    dve.tensor_tensor(act_g[:, n], act_r[:, n], gate_b[:, par, n * N:(n + 1) * N], ALU.mult
                                      ).then_inc(s_u, 1)
                    low(*((base - 1, 1), (base, 0))[n])
                    dve.wait_ge(s_u, g * (2 * E_R) + e * 2 + n + 2)
                    dve.tensor_tensor(act_g[:, n], act_g[:, n], act_r[:, n], ALU.mult).then_inc(s_g, 1)

            LINKS = 18

            def settled():
                dve.memset(settle[:], 0.0)

            def statistics(n, part):
                x1g = pers.x1[:, bass.ds(n % groups * GT, GT), :]
                half = slice(part % 2 * (GT // 2), (part % 2 + 1) * (GT // 2))
                if part < 2:
                    dve.tensor_tensor(x1g[:, half], x1g[:, half], bo[:].unsqueeze(1).broadcast_to([P, GT // 2, D]),
                                      ALU.add).then_inc(prep_link, 1)
                elif part < 4:
                    dve.wait_ge(prep_link, n * 4 + part)
                    settled()
                    for t in range(half.start, half.stop):
                        st = dve.bn_stats(stats[:, t], x1g[:, t])
                    st.then_inc(prep_link, 1)
                elif part == 4:
                    dve.wait_ge(prep_link, n * 4 + 4)
                    settled()
                    for t in range(GT):
                        st = dve.bn_aggr(moments[:, t], stats[:, t])
                    st.then_inc(var_done, 1)
                else:
                    if part == 5:
                        dve.wait_ge(rstd_done, n + 1)
                    for t in ((0, 1, 2), (3, 4, 5), (6, 7))[part - 5]:
                        st = dve.tensor_scalar(x_nat[:, t], x1g[:, t], moments[:, t, 0:1], rstd[:, 1, t:t + 1],
                                               ALU.subtract, ALU.mult)
                    if part == 7:
                        st.then_inc(x_normed, 1)

            def lows(n):
                for half in range(2):
                    for c in range(C2):
                        dve.wait_ge(x_high, n * 4 + 2 * half + c + 1)
                        dve.tensor_tensor(x_t[:, 1, c, half * N:(half + 1) * N], x_f[:, c, half * N:(half + 1) * N],
                                          f32(x_t[:, 0, c, half * N:(half + 1) * N]), ALU.subtract).then_inc(x_low, 1)

            for part in range(TAIL):
                statistics(0, part)
            with dve.Fori(0, groups) as g:
                k = 0

                def done(instruction):
                    nonlocal k
                    k += 1
                    instruction.then_inc(link, 1)
                    dve.wait_ge(link, g * LINKS + k)

                x1g = pers.x1[:, bass.ds(g * GT, GT), :]
                lows(g)
                dve.wait_ge(tanh_done, g + 1)
                done(dve.tensor_scalar(prob[:], prob[:], 0.5, 0.5, ALU.mult, ALU.add))
                done(dve.tensor_tensor(biased[:], prob[:], bias[:].unsqueeze(1).broadcast_to([P, GT, E_R]), ALU.add))
                settled()
                for t in range(GT):
                    for gr in range(GROUPS_R):
                        st = dve.max(best[:, t, gr], biased[:, t, gr * PER_G:(gr + 1) * PER_G])
                done(st)
                done(dve.tensor_tensor(g_score[:], best[:, :, :, 0], best[:, :, :, 1], ALU.add))
                for t in range(GT):
                    other = g_score[:, t].unsqueeze(1).broadcast_to([P, GROUPS_R, GROUPS_R])
                    own = g_score[:, t].unsqueeze(2).broadcast_to([P, GROUPS_R, GROUPS_R])
                    dve.tensor_tensor(cmp_a[:, t], other, own, ALU.is_gt)
                    st = dve.tensor_tensor(cmp_b[:, t], other, own, ALU.is_equal)
                done(st)
                done(dve.tensor_tensor(cmp_b[:].rearrange("p t i j -> p t (i j)"), cmp_b[:].rearrange("p t i j -> p t (i j)"),
                                       earlier[:].rearrange("p i j -> p (i j)").unsqueeze(1).broadcast_to(
                                           [P, GT, GROUPS_R * GROUPS_R]), ALU.mult))
                done(dve.tensor_tensor(cmp_a[:], cmp_a[:], cmp_b[:], ALU.add))
                done(dve.tensor_reduce(g_rank[:], cmp_a[:], mybir.AxisListType.X, ALU.add))
                done(dve.tensor_scalar(g_rank[:], g_rank[:], float(TOP_G), None, ALU.is_lt))
                done(dve.tensor_tensor(biased[:].rearrange("p t (i j) -> p (t i) j", j=PER_G),
                                       biased[:].rearrange("p t (i j) -> p (t i) j", j=PER_G),
                                       g_rank[:].rearrange("p t i -> p (t i)").unsqueeze(2).broadcast_to(
                                           [P, GT * GROUPS_R, PER_G]), ALU.mult))
                settled()
                for t in range(GT):
                    st = dve.max(top8[:, t], biased[:, t])
                done(st)
                settled()
                for t in range(GT):
                    st = dve.match_replace(out=gate[:, t], in_to_replace=top8[:, t], in_values=biased[:, t],
                                           imm_value=TAKEN)
                done(st)
                done(dve.tensor_scalar(gate[:], gate[:], TAKEN, None, ALU.is_equal))
                done(dve.tensor_tensor(gate[:], gate[:], prob[:], ALU.mult))
                done(dve.tensor_reduce(total[:], gate[:], mybir.AxisListType.X, ALU.add))
                done(dve.tensor_scalar(total[:], total[:], 1e-20, None, ALU.add))
                done(dve.reciprocal(total[:], total[:]))
                done(dve.tensor_scalar(total[:], total[:], ROUTE_SCALE, None, ALU.mult))
                dve.tensor_tensor(gate[:], gate[:], total[:].unsqueeze(2).broadcast_to([P, GT, E_R]), ALU.mult
                                  ).then_inc(gates_done, 1)
                assert k == LINKS, k
                experts(dve, visit)(g)
                low(g * NE + (NE - 1), 1)
                for t in range(0, GT, 2):
                    dve.wait_ge(y_turned, g * GT + t + 2)
                    if t == 0:
                        dve.wait_ge(out_stored, 1 + g * 16)
                    dve.tensor_tensor(y_out[:, t:t + 2], ps_acc[:, (t % 4) // 2, t // 4].rearrange(
                        "p (t n) -> p t n", t=2), x1g[:, t:t + 2], ALU.add).then_inc(y_added, 1)



INS = {"x": "x", "ctx_1024": "ctx", "g_xattn": "g_xattn", "g_ffn": "g_ffn", "L0_xattn_cos": "cos", "L0_xattn_sin": "sin",
       "L0_xattn_ln_lat_g": "ln_lat_g", "L0_xattn_ln_lat_b": "ln_lat_b", "L0_xattn_ln_ctx_g": "ln_ctx_g",
       "L0_xattn_ln_ctx_b": "ln_ctx_b", "L0_xattn_Wq": "Wq", "L0_xattn_Wkv": "Wkv", "L0_xattn_Wo": "Wo",
       "L0_xattn_bo": "bo", "L0_ffn_router_w": "router_w", "L0_ffn_correction_bias": "correction_bias",
       "L0_ffn_up_w": "up_w", "L0_ffn_down_w": "down_w", "L0_ffn_shared_up_w": "shared_up_w",
       "L0_ffn_shared_down_w": "shared_down_w"}


def program(nc, ins, out):
    w_dram = nc.dram_tensor("w_pairs", [PAIRS, P, 2 * C2 * 3 * P], F32, kind="Internal").ap()
    wo_dram = nc.dram_tensor("wo_heads", [PAIRS, DH, 2, 2, D], F32, kind="Internal").ap()
    gates_dram = nc.dram_tensor("gates_by_expert", [E_R, TG], F32, kind="Internal").ap()
    with ExitStack() as ctx:
        pers = Persistent(nc, ctx)
        setup(nc, pers, ins, w_dram, wo_dram)
        attention(nc, pers, ins, w_dram, wo_dram)
        ffn(nc, pers, ins, out, gates_dram)


def kernel(**inputs):
    import numpy as _np
    import concourse.bacc as _bacc
    from concourse.bass_utils import run_bass_kernel_spmd as _run

    nc = _bacc.Bacc("TRN2", target_bir_lowering=False, num_devices=1)
    arrays, ins = {}, {}
    for name, short in INS.items():
        a = _np.ascontiguousarray(inputs[name])
        arrays[f"in_{name}"] = a
        ins[short] = nc.dram_tensor(f"in_{name}", a.shape, mybir.dt.from_np(a.dtype), kind="ExternalInput").ap()
    out = nc.dram_tensor("out_0", (B, N, D), F32, kind="ExternalOutput").ap()
    program(nc, ins, out)
    r = _run(nc, [arrays], core_ids=[0])
    return r.results[0]["out_0"]
```
